# Optimizing a Trainium2 kernel written in Bass

```python
import numpy as np
import jax
import jax.numpy as jnp

def _softmax(x, axis=-1):
    return jax.nn.softmax(x, axis=axis)

def _gelu(x):
    return jax.nn.gelu(x, approximate=True)

def _silu(x):
    return jax.nn.silu(x)

def _sigmoid(x):
    return jax.nn.sigmoid(x)

def _layernorm(x, axis=-1, eps=1e-05):
    m = jnp.mean(x, axis=axis, keepdims=True)
    v = jnp.var(x, axis=axis, keepdims=True)
    return (x - m) / jnp.sqrt(v + eps)

def _scatter_add(tgt, idx, src, axis=0):
    return tgt.at[idx].add(src)

def _segment_sum(src, seg, n):
    return jax.ops.segment_sum(src, seg, n)
kernel_name = 'mk_audio_tower_d2_tok_audfeat512_r4_6f59ac'

def setup_inputs(seed: int=0):
    np.random.seed(seed)
    _w = jnp.asarray

    def _rec_inputs():
        import jax
        import jax.numpy as jnp
        _rk = jax.random.key(seed)
        x = -0.000718957 + 1.00057 * jax.random.normal(jax.random.fold_in(_rk, 1), (16, 80, 256), jnp.float32)
        return x
    x = _rec_inputs()

    def _L0_tok_setup():
        import jax, jax.numpy as jnp
        import numpy as np
        from jax import lax
        B, C_IN, T = (16, 80, 512)
        DIM, INTER, L = (128, 384, 8)
        EPS = 1e-06

        def _ln(x, g, b):
            mu = jnp.mean(x, axis=-1, keepdims=True)
            var = jnp.var(x, axis=-1, keepdims=True)
            return (x - mu) * lax.rsqrt(var + EPS) * g + b

        def _forward(x, embed_w, embed_b, norm0_g, norm0_b, dw_w, dw_b, ln_g, ln_b, w1, b1, w2, b2, gamma, final_g, final_b):
            h = lax.conv_general_dilated(x, embed_w, window_strides=(1,), padding=[(3, 3)], dimension_numbers=('NCH', 'OIH', 'NCH'))
            h = h + embed_b[None, :, None]
            h = _ln(h.transpose(0, 2, 1), norm0_g, norm0_b)

            def block(h, p):
                kw, kb, lg, lb, W1, B1, W2, B2, gm = p
                residual = h
                y = lax.conv_general_dilated(h, kw, window_strides=(1,), padding=[(3, 3)], dimension_numbers=('NHC', 'HIO', 'NHC'), feature_group_count=DIM)
                y = _ln(y + kb, lg, lb)
                y = jnp.einsum('btd,fd->btf', y, W1) + B1
                y = jax.nn.gelu(y, approximate=False)
                y = jnp.einsum('btf,df->btd', y, W2) + B2
                y = gm * y
                return (residual + y, None)
            h, _ = lax.scan(block, h, (dw_w, dw_b, ln_g, ln_b, w1, b1, w2, b2, gamma))
            return _ln(h, final_g, final_b)
        key = jax.random.key(seed)
        ks = jax.random.split(key, 17)
        std = 0.02
        return {'x': jax.random.normal(ks[0], (B, C_IN, T), jnp.float32), 'embed_w': jax.random.normal(ks[1], (DIM, C_IN, 7), jnp.float32) * std, 'embed_b': jnp.zeros((DIM,), jnp.float32), 'norm0_g': jnp.ones((DIM,), jnp.float32), 'norm0_b': jnp.zeros((DIM,), jnp.float32), 'dw_w': jax.random.normal(ks[2], (L, 7, 1, DIM), jnp.float32) * std, 'dw_b': jnp.zeros((L, DIM), jnp.float32), 'ln_g': jnp.ones((L, DIM), jnp.float32), 'ln_b': jnp.zeros((L, DIM), jnp.float32), 'w1': jax.random.normal(ks[3], (L, INTER, DIM), jnp.float32) * std, 'b1': jnp.zeros((L, INTER), jnp.float32), 'w2': jax.random.normal(ks[4], (L, DIM, INTER), jnp.float32) * std, 'b2': jnp.zeros((L, DIM), jnp.float32), 'gamma': jnp.full((L, DIM), 1.0 / L, jnp.float32), 'final_g': jnp.ones((DIM,), jnp.float32), 'final_b': jnp.zeros((DIM,), jnp.float32)}
    _L0_tok_all = _L0_tok_setup()
    _L0_tok_in = {k: v for k, v in _L0_tok_all.items() if k in ('embed_w', 'embed_b', 'norm0_g', 'norm0_b', 'dw_w', 'dw_b', 'ln_g', 'ln_b', 'w1', 'b1', 'w2', 'b2', 'gamma', 'final_g', 'final_b')}
    del _L0_tok_all

    def _L0_attn_setup():
        import jax, jax.numpy as jnp
        import numpy as np
        from jax import lax
        D_MODEL = 128
        D_STATE = 16
        D_CONV = 4
        EXPAND = 2
        D_INNER = EXPAND * D_MODEL
        DT_RANK = (D_MODEL + 15) // 16

        def _mamba_dir(x, in_w, conv_w, conv_b, xproj_w, dt_w, dt_b, A_log, D, out_w):
            B, L, _ = x.shape
            xz = jnp.einsum('bld,ed->ble', x, in_w)
            xi, z = jnp.split(xz, 2, axis=-1)
            xc = xi.transpose(0, 2, 1)
            xc = lax.conv_general_dilated(xc, conv_w, window_strides=(1,), padding=[(D_CONV - 1, 0)], feature_group_count=D_INNER, dimension_numbers=('NCH', 'OIH', 'NCH'))
            xi = jax.nn.silu(xc + conv_b[None, :, None]).transpose(0, 2, 1)
            x_dbl = jnp.einsum('bld,ed->ble', xi, xproj_w)
            dt, Bc, Cc = jnp.split(x_dbl, [DT_RANK, DT_RANK + D_STATE], axis=-1)
            delta = jax.nn.softplus(jnp.einsum('blr,dr->bld', dt, dt_w) + dt_b)
            A = -jnp.exp(A_log)
            deltaA = jnp.exp(delta[..., None] * A)
            dBx = delta[..., None] * Bc[:, :, None, :] * xi[..., None]

            def step(h, inputs):
                dA_t, dBx_t, C_t = inputs
                h = dA_t * h + dBx_t
                y = jnp.einsum('bdn,bn->bd', h, C_t)
                return (h, y)
            h0 = jnp.zeros((B, D_INNER, D_STATE), dtype=x.dtype)
            _, ys = lax.scan(step, h0, (deltaA.transpose(1, 0, 2, 3), dBx.transpose(1, 0, 2, 3), Cc.transpose(1, 0, 2)))
            y = ys.transpose(1, 0, 2)
            y = y + xi * D
            y = y * jax.nn.silu(z)
            return jnp.einsum('ble,de->bld', y, out_w)

        def _forward(x, f_in_w, f_conv_w, f_conv_b, f_xproj_w, f_dt_w, f_dt_b, f_A_log, f_D, f_out_w, b_in_w, b_conv_w, b_conv_b, b_xproj_w, b_dt_w, b_dt_b, b_A_log, b_D, b_out_w, fusion_w, fusion_b, ln_g, ln_b):
            out_fwd = _mamba_dir(x, f_in_w, f_conv_w, f_conv_b, f_xproj_w, f_dt_w, f_dt_b, f_A_log, f_D, f_out_w)
            x_flip = jnp.flip(x, axis=1)
            out_bwd = _mamba_dir(x_flip, b_in_w, b_conv_w, b_conv_b, b_xproj_w, b_dt_w, b_dt_b, b_A_log, b_D, b_out_w)
            out_bwd = jnp.flip(out_bwd, axis=1)
            fused = jnp.concatenate([out_fwd, out_bwd], axis=-1)
            out = jnp.einsum('blf,df->bld', fused, fusion_w) + fusion_b
            r = x + out
            mu = jnp.mean(r, axis=-1, keepdims=True)
            var = jnp.var(r, axis=-1, keepdims=True)
            return (r - mu) * lax.rsqrt(var + 1e-05) * ln_g + ln_b

        def _mamba_params(key):
            ks = jax.random.split(key, 6)
            s = 0.02
            in_w = jax.random.normal(ks[0], (2 * D_INNER, D_MODEL), jnp.float32) * s
            conv_w = jax.random.normal(ks[1], (D_INNER, 1, D_CONV), jnp.float32) * 0.2
            conv_b = jnp.zeros((D_INNER,), jnp.float32)
            xproj_w = jax.random.normal(ks[2], (DT_RANK + 2 * D_STATE, D_INNER), jnp.float32) * s
            dt_w = jax.random.normal(ks[3], (D_INNER, DT_RANK), jnp.float32) * DT_RANK ** (-0.5)
            dt_b = jax.random.uniform(ks[4], (D_INNER,), jnp.float32, -4.0, -2.0)
            A_log = jnp.log(jnp.broadcast_to(jnp.arange(1, D_STATE + 1, dtype=jnp.float32), (D_INNER, D_STATE)))
            D = jnp.ones((D_INNER,), jnp.float32)
            out_w = jax.random.normal(ks[5], (D_MODEL, D_INNER), jnp.float32) * s
            return (in_w, conv_w, conv_b, xproj_w, dt_w, dt_b, A_log, D, out_w)
        key = jax.random.key(seed)
        kx, kf, kb, k1, k2 = jax.random.split(key, 5)
        B, L = (2, 256)
        x = jax.random.normal(kx, (B, L, D_MODEL), jnp.float32)
        f = _mamba_params(kf)
        b = _mamba_params(kb)
        fusion_w = jax.random.normal(k1, (D_MODEL, 2 * D_MODEL), jnp.float32) * 0.02
        fusion_b = jnp.zeros((D_MODEL,), jnp.float32)
        ln_g = jnp.ones((D_MODEL,), jnp.float32)
        ln_b = jnp.zeros((D_MODEL,), jnp.float32)
        names_f = ['f_in_w', 'f_conv_w', 'f_conv_b', 'f_xproj_w', 'f_dt_w', 'f_dt_b', 'f_A_log', 'f_D', 'f_out_w']
        names_b = ['b_in_w', 'b_conv_w', 'b_conv_b', 'b_xproj_w', 'b_dt_w', 'b_dt_b', 'b_A_log', 'b_D', 'b_out_w']
        d = {'x': x, 'fusion_w': fusion_w, 'fusion_b': fusion_b, 'ln_g': ln_g, 'ln_b': ln_b}
        d.update(dict(zip(names_f, f)))
        d.update(dict(zip(names_b, b)))
        return d
    _L0_attn_all = _L0_attn_setup()
    _L0_attn_in = {k: v for k, v in _L0_attn_all.items() if k in ('f_in_w', 'f_conv_w', 'f_conv_b', 'f_xproj_w', 'f_dt_w', 'f_dt_b', 'f_A_log', 'f_D', 'f_out_w', 'b_in_w', 'b_conv_w', 'b_conv_b', 'b_xproj_w', 'b_dt_w', 'b_dt_b', 'b_A_log', 'b_D', 'b_out_w', 'fusion_w', 'fusion_b', 'ln_g', 'ln_b')}
    del _L0_attn_all

    def _L0_ffn_setup():
        import jax, jax.numpy as jnp
        import numpy as np
        B, T, D = (4, 2048, 128)
        E, F, CAP = (8, 512, 1024)
        key = jax.random.key(seed)
        ks = jax.random.split(key, 6)
        s = 0.02
        return {'x': jax.random.normal(ks[0], (B, T, D), dtype=jnp.float32), 'Wr': jax.random.normal(ks[1], (D, E), dtype=jnp.float32) * s, 'W1': jax.random.normal(ks[2], (E, D, F), dtype=jnp.float32) * s, 'b1': jax.random.normal(ks[3], (E, F), dtype=jnp.float32) * s, 'W2': jax.random.normal(ks[4], (E, F, D), dtype=jnp.float32) * s, 'b2': jax.random.normal(ks[5], (E, D), dtype=jnp.float32) * s}
    _L0_ffn_all = _L0_ffn_setup()
    _L0_ffn_in = {k: v for k, v in _L0_ffn_all.items() if k in ('Wr', 'W1', 'b1', 'W2', 'b2')}
    del _L0_ffn_all

    def _L1_attn_setup():
        import jax, jax.numpy as jnp
        import numpy as np
        B, N, DIM = (4, 512, 128)
        H, DH = (8, 64)
        key = jax.random.key(seed)
        ks = jax.random.split(key, 7)
        s = 0.02
        return {'x': jax.random.normal(ks[0], (B, N, DIM), dtype=jnp.float32), 'w_qkv': jax.random.normal(ks[1], (DIM, 3 * H * DH), dtype=jnp.float32) * s, 'b_qkv': jnp.zeros((3 * H * DH,), dtype=jnp.float32), 'th1': jax.random.normal(ks[2], (H, H), dtype=jnp.float32) * (1.0 / H) + jnp.eye(H, dtype=jnp.float32), 'th2': jax.random.normal(ks[3], (H, H), dtype=jnp.float32) * (1.0 / H) + jnp.eye(H, dtype=jnp.float32), 'w_out': jax.random.normal(ks[4], (H * DH, DIM), dtype=jnp.float32) * s, 'b_out': jnp.zeros((DIM,), dtype=jnp.float32)}
    _L1_attn_all = _L1_attn_setup()
    _L1_attn_in = {k: v for k, v in _L1_attn_all.items() if k in ('w_qkv', 'b_qkv', 'th1', 'th2', 'w_out', 'b_out')}
    del _L1_attn_all

    def _L1_ffn_setup():
        import jax, jax.numpy as jnp
        import numpy as np
        DIM = 128
        INTER = 64
        SHARED_INTER = 256
        N_EXPERTS = 64
        TOP_K = 6
        key = jax.random.key(seed)
        ks = jax.random.split(key, 8)
        s = 0.05
        return {'x': jax.random.normal(ks[0], (2, 128, DIM), jnp.float32), 'w_gate': jax.random.normal(ks[1], (N_EXPERTS, DIM), jnp.float32) * s, 'w1': jax.random.normal(ks[2], (N_EXPERTS, INTER, DIM), jnp.float32) * s, 'w2': jax.random.normal(ks[3], (N_EXPERTS, INTER, DIM), jnp.float32) * s, 'w3': jax.random.normal(ks[4], (N_EXPERTS, INTER, DIM), jnp.float32) * s, 'w_sg': jax.random.normal(ks[5], (SHARED_INTER, DIM), jnp.float32) * s, 'w_su': jax.random.normal(ks[6], (SHARED_INTER, DIM), jnp.float32) * s, 'w_sd': jax.random.normal(ks[7], (DIM, SHARED_INTER), jnp.float32) * s}
    _L1_ffn_all = _L1_ffn_setup()
    _L1_ffn_in = {k: v for k, v in _L1_ffn_all.items() if k in ('w_gate', 'w1', 'w2', 'w3', 'w_sg', 'w_su', 'w_sd')}
    del _L1_ffn_all
    return {'x': x, 'L0_tok_embed_w': _L0_tok_in['embed_w'], 'L0_tok_embed_b': _L0_tok_in['embed_b'], 'L0_tok_norm0_g': _L0_tok_in['norm0_g'], 'L0_tok_norm0_b': _L0_tok_in['norm0_b'], 'L0_tok_dw_w': _L0_tok_in['dw_w'], 'L0_tok_dw_b': _L0_tok_in['dw_b'], 'L0_tok_ln_g': _L0_tok_in['ln_g'], 'L0_tok_ln_b': _L0_tok_in['ln_b'], 'L0_tok_w1': _L0_tok_in['w1'], 'L0_tok_b1': _L0_tok_in['b1'], 'L0_tok_w2': _L0_tok_in['w2'], 'L0_tok_b2': _L0_tok_in['b2'], 'L0_tok_gamma': _L0_tok_in['gamma'], 'L0_tok_final_g': _L0_tok_in['final_g'], 'L0_tok_final_b': _L0_tok_in['final_b'], 'L0_attn_f_in_w': _L0_attn_in['f_in_w'], 'L0_attn_f_conv_w': _L0_attn_in['f_conv_w'], 'L0_attn_f_conv_b': _L0_attn_in['f_conv_b'], 'L0_attn_f_xproj_w': _L0_attn_in['f_xproj_w'], 'L0_attn_f_dt_w': _L0_attn_in['f_dt_w'], 'L0_attn_f_dt_b': _L0_attn_in['f_dt_b'], 'L0_attn_f_A_log': _L0_attn_in['f_A_log'], 'L0_attn_f_D': _L0_attn_in['f_D'], 'L0_attn_f_out_w': _L0_attn_in['f_out_w'], 'L0_attn_b_in_w': _L0_attn_in['b_in_w'], 'L0_attn_b_conv_w': _L0_attn_in['b_conv_w'], 'L0_attn_b_conv_b': _L0_attn_in['b_conv_b'], 'L0_attn_b_xproj_w': _L0_attn_in['b_xproj_w'], 'L0_attn_b_dt_w': _L0_attn_in['b_dt_w'], 'L0_attn_b_dt_b': _L0_attn_in['b_dt_b'], 'L0_attn_b_A_log': _L0_attn_in['b_A_log'], 'L0_attn_b_D': _L0_attn_in['b_D'], 'L0_attn_b_out_w': _L0_attn_in['b_out_w'], 'L0_attn_fusion_w': _L0_attn_in['fusion_w'], 'L0_attn_fusion_b': _L0_attn_in['fusion_b'], 'L0_attn_ln_g': _L0_attn_in['ln_g'], 'L0_attn_ln_b': _L0_attn_in['ln_b'], 'L0_ffn_Wr': _L0_ffn_in['Wr'], 'L0_ffn_W1': _L0_ffn_in['W1'], 'L0_ffn_b1': _L0_ffn_in['b1'], 'L0_ffn_W2': _L0_ffn_in['W2'], 'L0_ffn_b2': _L0_ffn_in['b2'], 'L1_attn_w_qkv': _L1_attn_in['w_qkv'], 'L1_attn_b_qkv': _L1_attn_in['b_qkv'], 'L1_attn_th1': _L1_attn_in['th1'], 'L1_attn_th2': _L1_attn_in['th2'], 'L1_attn_w_out': _L1_attn_in['w_out'], 'L1_attn_b_out': _L1_attn_in['b_out'], 'L1_ffn_w_gate': _L1_ffn_in['w_gate'], 'L1_ffn_w1': _L1_ffn_in['w1'], 'L1_ffn_w2': _L1_ffn_in['w2'], 'L1_ffn_w3': _L1_ffn_in['w3'], 'L1_ffn_w_sg': _L1_ffn_in['w_sg'], 'L1_ffn_w_su': _L1_ffn_in['w_su'], 'L1_ffn_w_sd': _L1_ffn_in['w_sd']}

def reference(x, L0_tok_embed_w, L0_tok_embed_b, L0_tok_norm0_g, L0_tok_norm0_b, L0_tok_dw_w, L0_tok_dw_b, L0_tok_ln_g, L0_tok_ln_b, L0_tok_w1, L0_tok_b1, L0_tok_w2, L0_tok_b2, L0_tok_gamma, L0_tok_final_g, L0_tok_final_b, L0_attn_f_in_w, L0_attn_f_conv_w, L0_attn_f_conv_b, L0_attn_f_xproj_w, L0_attn_f_dt_w, L0_attn_f_dt_b, L0_attn_f_A_log, L0_attn_f_D, L0_attn_f_out_w, L0_attn_b_in_w, L0_attn_b_conv_w, L0_attn_b_conv_b, L0_attn_b_xproj_w, L0_attn_b_dt_w, L0_attn_b_dt_b, L0_attn_b_A_log, L0_attn_b_D, L0_attn_b_out_w, L0_attn_fusion_w, L0_attn_fusion_b, L0_attn_ln_g, L0_attn_ln_b, L0_ffn_Wr, L0_ffn_W1, L0_ffn_b1, L0_ffn_W2, L0_ffn_b2, L1_attn_w_qkv, L1_attn_b_qkv, L1_attn_th1, L1_attn_th2, L1_attn_w_out, L1_attn_b_out, L1_ffn_w_gate, L1_ffn_w1, L1_ffn_w2, L1_ffn_w3, L1_ffn_w_sg, L1_ffn_w_su, L1_ffn_w_sd):
    import jax
    import jax.numpy as jnp

    def _L0_tok_ref(x, embed_w, embed_b, norm0_g, norm0_b, dw_w, dw_b, ln_g, ln_b, w1, b1, w2, b2, gamma, final_g, final_b):
        import jax, jax.numpy as jnp
        import numpy as np
        from jax import lax
        B, C_IN, T = (16, 80, 512)
        DIM, INTER, L = (128, 384, 8)
        EPS = 1e-06

        def _ln(x, g, b):
            mu = jnp.mean(x, axis=-1, keepdims=True)
            var = jnp.var(x, axis=-1, keepdims=True)
            return (x - mu) * lax.rsqrt(var + EPS) * g + b

        def _forward(x, embed_w, embed_b, norm0_g, norm0_b, dw_w, dw_b, ln_g, ln_b, w1, b1, w2, b2, gamma, final_g, final_b):
            h = lax.conv_general_dilated(x, embed_w, window_strides=(1,), padding=[(3, 3)], dimension_numbers=('NCH', 'OIH', 'NCH'))
            h = h + embed_b[None, :, None]
            h = _ln(h.transpose(0, 2, 1), norm0_g, norm0_b)

            def block(h, p):
                kw, kb, lg, lb, W1, B1, W2, B2, gm = p
                residual = h
                y = lax.conv_general_dilated(h, kw, window_strides=(1,), padding=[(3, 3)], dimension_numbers=('NHC', 'HIO', 'NHC'), feature_group_count=DIM)
                y = _ln(y + kb, lg, lb)
                y = jnp.einsum('btd,fd->btf', y, W1) + B1
                y = jax.nn.gelu(y, approximate=False)
                y = jnp.einsum('btf,df->btd', y, W2) + B2
                y = gm * y
                return (residual + y, None)
            h, _ = lax.scan(block, h, (dw_w, dw_b, ln_g, ln_b, w1, b1, w2, b2, gamma))
            return _ln(h, final_g, final_b)
        return _forward(x, embed_w, embed_b, norm0_g, norm0_b, dw_w, dw_b, ln_g, ln_b, w1, b1, w2, b2, gamma, final_g, final_b)

    def _L0_attn_ref(x, f_in_w, f_conv_w, f_conv_b, f_xproj_w, f_dt_w, f_dt_b, f_A_log, f_D, f_out_w, b_in_w, b_conv_w, b_conv_b, b_xproj_w, b_dt_w, b_dt_b, b_A_log, b_D, b_out_w, fusion_w, fusion_b, ln_g, ln_b):
        import jax, jax.numpy as jnp
        import numpy as np
        from jax import lax
        D_MODEL = 128
        D_STATE = 16
        D_CONV = 4
        EXPAND = 2
        D_INNER = EXPAND * D_MODEL
        DT_RANK = (D_MODEL + 15) // 16

        def _mamba_dir(x, in_w, conv_w, conv_b, xproj_w, dt_w, dt_b, A_log, D, out_w):
            B, L, _ = x.shape
            xz = jnp.einsum('bld,ed->ble', x, in_w)
            xi, z = jnp.split(xz, 2, axis=-1)
            xc = xi.transpose(0, 2, 1)
            xc = lax.conv_general_dilated(xc, conv_w, window_strides=(1,), padding=[(D_CONV - 1, 0)], feature_group_count=D_INNER, dimension_numbers=('NCH', 'OIH', 'NCH'))
            xi = jax.nn.silu(xc + conv_b[None, :, None]).transpose(0, 2, 1)
            x_dbl = jnp.einsum('bld,ed->ble', xi, xproj_w)
            dt, Bc, Cc = jnp.split(x_dbl, [DT_RANK, DT_RANK + D_STATE], axis=-1)
            delta = jax.nn.softplus(jnp.einsum('blr,dr->bld', dt, dt_w) + dt_b)
            A = -jnp.exp(A_log)
            deltaA = jnp.exp(delta[..., None] * A)
            dBx = delta[..., None] * Bc[:, :, None, :] * xi[..., None]

            def step(h, inputs):
                dA_t, dBx_t, C_t = inputs
                h = dA_t * h + dBx_t
                y = jnp.einsum('bdn,bn->bd', h, C_t)
                return (h, y)
            h0 = jnp.zeros((B, D_INNER, D_STATE), dtype=x.dtype)
            _, ys = lax.scan(step, h0, (deltaA.transpose(1, 0, 2, 3), dBx.transpose(1, 0, 2, 3), Cc.transpose(1, 0, 2)))
            y = ys.transpose(1, 0, 2)
            y = y + xi * D
            y = y * jax.nn.silu(z)
            return jnp.einsum('ble,de->bld', y, out_w)

        def _forward(x, f_in_w, f_conv_w, f_conv_b, f_xproj_w, f_dt_w, f_dt_b, f_A_log, f_D, f_out_w, b_in_w, b_conv_w, b_conv_b, b_xproj_w, b_dt_w, b_dt_b, b_A_log, b_D, b_out_w, fusion_w, fusion_b, ln_g, ln_b):
            out_fwd = _mamba_dir(x, f_in_w, f_conv_w, f_conv_b, f_xproj_w, f_dt_w, f_dt_b, f_A_log, f_D, f_out_w)
            x_flip = jnp.flip(x, axis=1)
            out_bwd = _mamba_dir(x_flip, b_in_w, b_conv_w, b_conv_b, b_xproj_w, b_dt_w, b_dt_b, b_A_log, b_D, b_out_w)
            out_bwd = jnp.flip(out_bwd, axis=1)
            fused = jnp.concatenate([out_fwd, out_bwd], axis=-1)
            out = jnp.einsum('blf,df->bld', fused, fusion_w) + fusion_b
            r = x + out
            mu = jnp.mean(r, axis=-1, keepdims=True)
            var = jnp.var(r, axis=-1, keepdims=True)
            return (r - mu) * lax.rsqrt(var + 1e-05) * ln_g + ln_b

        def _mamba_params(key):
            ks = jax.random.split(key, 6)
            s = 0.02
            in_w = jax.random.normal(ks[0], (2 * D_INNER, D_MODEL), jnp.float32) * s
            conv_w = jax.random.normal(ks[1], (D_INNER, 1, D_CONV), jnp.float32) * 0.2
            conv_b = jnp.zeros((D_INNER,), jnp.float32)
            xproj_w = jax.random.normal(ks[2], (DT_RANK + 2 * D_STATE, D_INNER), jnp.float32) * s
            dt_w = jax.random.normal(ks[3], (D_INNER, DT_RANK), jnp.float32) * DT_RANK ** (-0.5)
            dt_b = jax.random.uniform(ks[4], (D_INNER,), jnp.float32, -4.0, -2.0)
            A_log = jnp.log(jnp.broadcast_to(jnp.arange(1, D_STATE + 1, dtype=jnp.float32), (D_INNER, D_STATE)))
            D = jnp.ones((D_INNER,), jnp.float32)
            out_w = jax.random.normal(ks[5], (D_MODEL, D_INNER), jnp.float32) * s
            return (in_w, conv_w, conv_b, xproj_w, dt_w, dt_b, A_log, D, out_w)
        return _forward(x, f_in_w, f_conv_w, f_conv_b, f_xproj_w, f_dt_w, f_dt_b, f_A_log, f_D, f_out_w, b_in_w, b_conv_w, b_conv_b, b_xproj_w, b_dt_w, b_dt_b, b_A_log, b_D, b_out_w, fusion_w, fusion_b, ln_g, ln_b)

    def _L0_ffn_ref(x, Wr, W1, b1, W2, b2):
        import jax, jax.numpy as jnp
        import numpy as np
        B, T, D = (4, 2048, 128)
        E, F, CAP = (8, 512, 1024)
        Bb, Tt, Dd = x.shape
        N = Bb * Tt
        C = min(CAP, N)
        x_flat = x.reshape(N, Dd)
        logits = x_flat @ Wr
        probs = jax.nn.softmax(logits, axis=0)
        vals, idx = jax.lax.top_k(probs.T, C)
        selected = x_flat[idx]
        h = jax.nn.gelu(jnp.einsum('ecd,edf->ecf', selected, W1) + b1[:, None, :], approximate=False)
        out_e = jnp.einsum('ecf,efd->ecd', h, W2) + b2[:, None, :]
        weighted = vals[..., None] * out_e
        output = jnp.zeros_like(x_flat).at[idx.reshape(-1)].add(weighted.reshape(-1, Dd))
        return output.reshape(Bb, Tt, Dd)

    def _L1_attn_ref(x, w_qkv, b_qkv, th1, th2, w_out, b_out):
        import jax, jax.numpy as jnp
        import numpy as np
        B, N, DIM = (4, 512, 128)
        H, DH = (8, 64)
        b, n, _ = x.shape
        scale = DH ** (-0.5)
        qkv = x @ w_qkv + b_qkv
        q, k, v = jnp.split(qkv, 3, axis=-1)
        to_heads = lambda t: t.reshape(b, n, H, DH).transpose(0, 2, 1, 3)
        q, k, v = (to_heads(q), to_heads(k), to_heads(v))
        dots = jnp.einsum('bhnd,bhmd->bhnm', q, k) * scale
        dots = jnp.einsum('gh,bhnm->bgnm', th1, dots)
        attn = jax.nn.softmax(dots, axis=-1)
        attn = jnp.einsum('gh,bhnm->bgnm', th2, attn)
        out = jnp.einsum('bhnm,bhmd->bhnd', attn, v)
        out = out.transpose(0, 2, 1, 3).reshape(b, n, H * DH)
        return out @ w_out + b_out

    def _L1_ffn_ref(x, w_gate, w1, w2, w3, w_sg, w_su, w_sd):
        import jax, jax.numpy as jnp
        import numpy as np
        DIM = 128
        INTER = 64
        SHARED_INTER = 256
        N_EXPERTS = 64
        TOP_K = 6
        orig_shape = x.shape
        xf = x.reshape(-1, x.shape[-1])
        T = xf.shape[0]
        scores = xf @ w_gate.T
        top_vals, top_idx = jax.lax.top_k(scores, TOP_K)
        expert_weights = jax.nn.softmax(top_vals, axis=-1)
        comb = jnp.zeros(scores.shape, xf.dtype).at[jnp.arange(T)[:, None], top_idx].set(expert_weights)
        x1 = jax.nn.silu(jnp.einsum('td,eid->tei', xf, w1))
        x3 = jnp.einsum('td,eid->tei', xf, w3)
        y = jnp.einsum('tei,eid->ted', x1 * x3, w2)
        routed = jnp.einsum('ted,te->td', y, comb)
        shared = jax.nn.silu(xf @ w_sg.T) * (xf @ w_su.T) @ w_sd.T
        return (routed + shared).reshape(orig_shape)
    h = _L0_tok_ref(x, L0_tok_embed_w, L0_tok_embed_b, L0_tok_norm0_g, L0_tok_norm0_b, L0_tok_dw_w, L0_tok_dw_b, L0_tok_ln_g, L0_tok_ln_b, L0_tok_w1, L0_tok_b1, L0_tok_w2, L0_tok_b2, L0_tok_gamma, L0_tok_final_g, L0_tok_final_b)
    h = h + _L0_attn_ref(_layernorm(h, axis=-1), L0_attn_f_in_w, L0_attn_f_conv_w, L0_attn_f_conv_b, L0_attn_f_xproj_w, L0_attn_f_dt_w, L0_attn_f_dt_b, L0_attn_f_A_log, L0_attn_f_D, L0_attn_f_out_w, L0_attn_b_in_w, L0_attn_b_conv_w, L0_attn_b_conv_b, L0_attn_b_xproj_w, L0_attn_b_dt_w, L0_attn_b_dt_b, L0_attn_b_A_log, L0_attn_b_D, L0_attn_b_out_w, L0_attn_fusion_w, L0_attn_fusion_b, L0_attn_ln_g, L0_attn_ln_b)
    h = h + _L0_ffn_ref(_layernorm(h, axis=-1), L0_ffn_Wr, L0_ffn_W1, L0_ffn_b1, L0_ffn_W2, L0_ffn_b2)
    h = h + _L1_attn_ref(_layernorm(h, axis=-1), L1_attn_w_qkv, L1_attn_b_qkv, L1_attn_th1, L1_attn_th2, L1_attn_w_out, L1_attn_b_out)
    h = h + _L1_ffn_ref(_layernorm(h, axis=-1), L1_ffn_w_gate, L1_ffn_w1, L1_ffn_w2, L1_ffn_w3, L1_ffn_w_sg, L1_ffn_w_su, L1_ffn_w_sd)
    return h

_drawn_inputs = setup_inputs


def setup_inputs(seed=0):
    import zlib

    import numpy as np

    out = dict(_drawn_inputs(seed))
    spreads = {'L0_tok_embed_b': (0.0, 0.1),
     'L0_tok_norm0_g': (1.0, 0.2),
     'L0_tok_norm0_b': (0.0, 0.1),
     'L0_tok_dw_b': (0.0, 0.511),
     'L0_tok_ln_g': (1.0, 0.6),
     'L0_tok_ln_b': (0.0, 0.8),
     'L0_tok_b1': (0.0, 0.8),
     'L0_tok_b2': (0.0, 0.1),
     'L0_tok_gamma': (0.125, 0.6),
     'L0_tok_final_g': (1.0, 0.2),
     'L0_tok_final_b': (0.0, 0.1),
     'L0_attn_f_conv_b': (0.0, 0.8),
     'L0_attn_f_D': (1.0, 0.6),
     'L0_attn_b_conv_b': (0.0, 0.8),
     'L0_attn_b_D': (1.0, 0.6),
     'L0_attn_fusion_b': (0.0, 2.0),
     'L0_attn_ln_g': (1.0, 0.2),
     'L0_attn_ln_b': (0.0, 0.1),
     'L1_attn_b_qkv': (0.0, 0.338),
     'L1_attn_b_out': (0.0, 0.1)}
    factors = {'L0_tok_dw_w': 6.692,
     'L0_tok_w1': 3.582,
     'L0_tok_w2': 2.853,
     'L0_attn_f_in_w': 8.0,
     'L0_attn_f_conv_w': 8.0,
     'L0_attn_f_xproj_w': 8.0,
     'L0_attn_f_dt_w': 8.0,
     'L0_attn_f_dt_b': 8.0,
     'L0_attn_f_A_log': 8.0,
     'L0_attn_f_out_w': 8.0,
     'L0_attn_b_in_w': 8.0,
     'L0_attn_b_conv_w': 8.0,
     'L0_attn_b_xproj_w': 8.0,
     'L0_attn_b_dt_w': 8.0,
     'L0_attn_b_dt_b': 8.0,
     'L0_attn_b_A_log': 8.0,
     'L0_attn_b_out_w': 8.0,
     'L0_attn_fusion_w': 8.0,
     'L0_ffn_Wr': 8.0,
     'L0_ffn_W1': 8.0,
     'L0_ffn_b1': 47.274,
     'L0_ffn_W2': 8.0,
     'L0_ffn_b2': 200.0,
     'L1_attn_w_qkv': 3.361,
     'L1_attn_th1': 8.0,
     'L1_attn_th2': 4.029,
     'L1_ffn_w_gate': 4.158,
     'L1_ffn_w1': 4.094,
     'L1_ffn_w2': 3.981,
     'L1_ffn_w3': 3.973}
    for name, (base, spread) in spreads.items():
        noise = np.random.default_rng([zlib.crc32(name.encode()), seed]).standard_normal(out[name].shape)
        drawn = base * np.exp(spread * noise) if base else spread * noise
        out[name] = jnp.asarray(drawn.astype(out[name].dtype))
    for name, factor in factors.items():
        out[name] = (out[name] * factor).astype(out[name].dtype)
    return out
```

```python
from contextlib import ExitStack

import concourse.bass as bass
from concourse import mybir

F32 = mybir.dt.float32
BF16 = mybir.dt.bfloat16
F32R = mybir.dt.float32r
I32 = mybir.dt.int32
U8 = mybir.dt.uint8
ALU = mybir.AluOpType
ACT = mybir.ActivationFunctionType
AX_X = mybir.AxisListType.X

P = 128
B = 16
L = 256
N = B * L
TOK = 512
TILES = N // TOK
SUB = TOK // P


class Mem:

    def __init__(self, nc, ctx):
        self.nc, self.ctx, self.sems = nc, ctx, []
        ctx.callback(self.clear)

    def sb(self, name, shape, dt=F32):
        return self.ctx.enter_context(self.nc.sbuf_tensor(name, shape, dt))

    def ps(self, name, shape, dt=F32):
        return self.ctx.enter_context(self.nc.psum_tensor(name, shape, dt))

    def sem(self, name):
        self.sems.append(self.nc.alloc_semaphore(name=name))
        return self.sems[-1]

    def clear(self):
        if self.sems:
            self.nc.clear_and_free_semaphores(self.sems)
            self.nc.all_engine_barrier()


def apart(eng):
    eng.nop(nofuse=True)


def tok_stage(nc, a, R, XT, ident):
    TAPS, HALO, LAYERS, CIN = 7, 3, 8, 80
    INTER = 384
    FC = INTER // P
    LP = L + 2 * HALO
    with ExitStack() as ctx:
        m = Mem(nc, ctx)
        xin = m.sb("xin", [CIN, B, LP])
        HP = m.sb("HP", [P, B, LP])
        ew = m.sb("ew", [CIN, TAPS, P])
        cols = m.sb("cols", [P, 3])
        dww = m.sb("dww", [P, LAYERS, TAPS])
        lcol = m.sb("lcol", [P, 5, LAYERS])
        b1 = m.sb("b1", [P, LAYERS, FC])
        gb2 = m.sb("gb2", [P, LAYERS])
        w1 = [m.sb(f"w1_{i}", [P, INTER]) for i in range(2)]
        w2 = [m.sb(f"w2_{i}", [P, FC, P]) for i in range(2)]
        fing = m.sb("fing", [P, 2, P])
        cv = [m.sb(f"cv{i}", [P, TOK]) for i in range(2)]
        st = [m.sb(f"st{i}", [P, SUB, 6]) for i in range(2)]
        mv = [m.sb(f"mv{i}", [P, SUB, 2]) for i in range(2)]
        ve = [m.sb(f"ve{i}", [P, SUB]) for i in range(2)]
        rs = [m.sb(f"rs{i}", [P, SUB]) for i in range(2)]
        ln = [m.sb(f"ln{i}", [P, SUB, P]) for i in range(2)]
        y = [m.sb(f"y{i}", [P, TOK]) for i in range(2)]
        g = [m.sb(f"g{i}", [P, FC, TOK]) for i in range(2)]
        yo = [m.sb(f"yo{i}", [P, TOK]) for i in range(2)]
        mhalf = m.sb("mhalf", [P, SUB])
        eps6 = m.sb("eps6", [P, SUB])
        eps5 = m.sb("eps5", [P, SUB])
        PT = [m.ps(f"PT{i}", [P, SUB, P]) for i in range(2)]
        PB = m.ps("PB", [P, TOK])
        PH = m.ps("PH", [P, FC, TOK])
        PO = m.ps("PO", [P, TOK])
        PC = m.ps("PC", [P, TOK])

        s_x = m.sem("x_loaded")
        s_wl = m.sem("weights_loaded")
        s_lw = [m.sem(f"layer_weights_loaded{i}") for i in range(2)]
        s_ms = m.sem("halo_zeroed")
        s_gb = m.sem("gamma_b2_ready")
        s_pc = m.sem("embed_conv_done")
        s_ce = m.sem("embed_evacuated")
        s_ch = m.sem("conv_chain")
        s_cv = m.sem("conv_done")
        s_t1 = m.sem("to_tokens_done")
        s_bn = m.sem("bn_stats_done")
        s_mv = m.sem("moments_ready")
        s_ve = m.sem("var_eps_ready")
        s_rs = m.sem("rstd_ready")
        s_ap = m.sem("norm_applied")
        s_t2 = m.sem("to_channels_done")
        s_y = m.sem("y_ready")
        s_h = m.sem("hidden_done")
        s_g = m.sem("gelu_done")
        s_o = m.sem("mlp_out_done")
        s_yo = m.sem("scaled_out_ready")
        s_rd = m.sem("residual_done")
        s_f = m.sem("final_chain")
        s_bn2 = m.sem("bn_stats2_done")

        block = ctx.enter_context(nc.Block())

        @block.sync
        def _(sp):
            sp.wait_ge(s_ms, 1)
            sp.dma_start(xin[:, :, HALO:HALO + L], a["x"].rearrange("b c t -> c b t")).then_inc(s_x, 16)
            sp.dma_start(ew[:, :, :], a["ew"]).then_inc(s_x, 16)
            sp.dma_start(cols[:, :], a["tok_cols"]).then_inc(s_x, 16)
            sp.dma_start(ident[:, :], a["ident"]).then_inc(s_x, 16)
            sp.dma_start(dww[:, :, :], a["dww"]).then_inc(s_wl, 16)
            sp.dma_start(lcol[:, :, :], a["lcol"]).then_inc(s_wl, 16)
            sp.dma_start(b1[:, :, :], a["tok_b1"]).then_inc(s_wl, 16)
            sp.dma_start(fing[:, :, :], a["fing"].partition_broadcast(P)).then_inc(s_wl, 16)

            def load(layer, i):
                sp.dma_start(w1[i][:, :], a["tok_w1"][bass.ds(layer, 1), :, :].rearrange("o p f -> (o p) f")
                             ).then_inc(s_lw[i], 16)
                sp.dma_start(w2[i][:, :, :], a["tok_w2"][bass.ds(layer, 1), :, :, :].rearrange("o p c d -> (o p) c d")
                             ).then_inc(s_lw[i], 16)

            load(0, 0)
            load(1, 1)
            with sp.Fori(1, LAYERS // 2) as lp:
                for i in range(2):
                    sp.wait_ge(s_o, (2 * lp + i - 1) * TILES)
                    load(2 * lp + i, i)

        @block.gpsimd
        def _(pool):
            nc.gpsimd.memset(xin[:, :, 0:HALO], 0.0)
            nc.gpsimd.memset(xin[:, :, HALO + L:], 0.0).then_inc(s_ms, 1)
            nc.gpsimd.memset(mhalf[:, :], -0.5)
            nc.gpsimd.memset(eps6[:, :], 1e-6)
            nc.gpsimd.memset(eps5[:, :], 1e-5)
            nc.gpsimd.memset(HP[:, :, 0:HALO], 0.0)
            nc.gpsimd.memset(HP[:, :, HALO + L:], 0.0).then_inc(s_ms, 1)
            pool.wait_ge(s_ms, 2)

            def rstd(i, eps, k):
                pool.wait_ge(s_mv, k + 1)
                if not isinstance(k, int) or k >= 2:
                    pool.wait_ge(s_ap, k - 1)
                nc.gpsimd.tensor_tensor(ve[i][:, :], mv[i][:, :, 1], eps[:, :], ALU.add).then_inc(s_ve, 1)
                pool.wait_ge(s_ve, k + 1)
                nc.gpsimd.tensor_tensor(rs[i][:, :], ve[i][:, :], mhalf[:, :], ALU.pow).then_inc(s_rs, 1)

            for i in range(2):
                rstd(i, eps6, i)
            with pool.Fori(1, (LAYERS + 1) * TILES // 2) as q:
                for i in range(2):
                    rstd(i, eps6, 2 * q + i)
            base = (LAYERS + 1) * TILES
            for t in range(TILES):
                rstd(0, eps6, base + 2 * t)
                rstd(1, eps5, base + 2 * t + 1)

        @block.tensor
        def _(pe):
            pe.wait_ge(s_x, 64)
            pe.wait_ge(s_ms, 2)

            def embed(t):
                if t >= 1:
                    pe.wait_ge(s_ce, t)
                for k in range(TAPS):
                    mm = nc.tensor.matmul(PC[:, :].rearrange("p (b t) -> p b t", b=2), ew[:, k, :],
                                          xin[:, 2 * t:2 * t + 2, k:k + L], start=(k == 0), stop=(k == TAPS - 1))
                mm.then_inc(s_pc, 1)

            def t1(U, t, kind):
                if kind == "embed":
                    pe.wait_ge(s_ce, t + 1)
                else:
                    pe.wait_ge(s_cv, U - TILES + 1)
                if not isinstance(U, int) or U >= 2:
                    pe.wait_ge(s_ap, U - 1)
                for j in range(SUB):
                    mm = nc.tensor.transpose(PT[t % 2][:, j, :], cv[t % 2][:, j * P:(j + 1) * P], ident[:, :])
                mm.then_inc(s_t1, 1)

            def t2(U, t):
                pe.wait_ge(s_ap, U + 1)
                if not isinstance(U, int) or U >= 1:
                    pe.wait_ge(s_y, U)
                for j in range(SUB):
                    mm = nc.tensor.transpose(PB[:, j * P:(j + 1) * P], ln[t % 2][:, j, :], ident[:, :])
                mm.then_inc(s_t2, 1)

            def hid(V, t, wi):
                pe.wait_ge(s_y, V + TILES + 1)
                if not isinstance(V, int) or V >= 1:
                    pe.wait_ge(s_g, V)
                for f in range(FC):
                    mm = nc.tensor.matmul(PH[:, f, :], w1[wi][:, f * P:(f + 1) * P], y[t % 2][:, :],
                                          start=True, stop=True)
                mm.then_inc(s_h, 1)

            def out(V, t, wi):
                pe.wait_ge(s_g, V + 1)
                if not isinstance(V, int) or V >= 1:
                    pe.wait_ge(s_yo, V)
                for f in range(FC):
                    mm = nc.tensor.matmul(PO[:, :], w2[wi][:, f, :], g[t % 2][:, f, :],
                                          start=(f == 0), stop=(f == FC - 1))
                mm.then_inc(s_o, 1)

            embed(0)
            for t in range(TILES):
                t1(t, t, "embed")
                if t + 1 < TILES:
                    embed(t + 1)
                if t >= 1:
                    t2(t - 1, t - 1)

            def layer(l, par, first):
                V0 = l * TILES
                if isinstance(l, int):
                    pe.wait_ge(s_lw[par], 32 * (l // 2 + 1))
                for t in range(TILES):
                    t1(V0 + TILES + t, t, "layer")
                    t2(V0 + TILES + t - 1, (t - 1) % TILES)
                    if t >= 2:
                        out(V0 + t - 2, t, par)
                    elif not first:
                        out(V0 + t - 2, t, 1 - par)
                    if t >= 1:
                        hid(V0 + t - 1, t - 1, par)
                    elif not first:
                        hid(V0 - 1, TILES - 1, 1 - par)

            layer(0, 0, True)
            layer(1, 1, False)
            with pe.Fori(1, LAYERS // 2) as lp:
                for par in range(2):
                    pe.wait_ge(s_lw[par], 32 * (lp + 1))
                    layer(2 * lp + par, par, False)
            V1 = LAYERS * TILES
            t2(V1 + TILES - 1, TILES - 1)
            out(V1 - 2, TILES - 2, 1)
            hid(V1 - 1, TILES - 1, 1)
            out(V1 - 1, TILES - 1, 1)
            base = V1 + TILES
            for t in range(TILES):
                pe.wait_ge(s_rd, V1 - TILES + t + 1)
                if t >= 1:
                    pe.wait_ge(s_ap, base + 2 * (t - 1) + 1)
                for j in range(SUB):
                    b, h = 2 * t + j // 2, j % 2
                    mm = nc.tensor.transpose(PT[0][:, j, :], HP[:, b, HALO + h * P:HALO + (h + 1) * P], ident[:, :])
                mm.then_inc(s_t1, 1)
                pe.wait_ge(s_ap, base + 2 * t + 2)
                pe.wait_ge(s_y, base + t)
                for j in range(SUB):
                    mm = nc.tensor.transpose(PB[:, j * P:(j + 1) * P], ln[1][:, j, :], ident[:, :])
                mm.then_inc(s_t2, 1)

        @block.scalar
        def _(act):
            act.wait_ge(s_x, 64)

            def evac_embed(t):
                act.wait_ge(s_pc, t + 1)
                if t >= 2:
                    act.wait_ge(s_t1, t - 1)
                nc.scalar.activation(cv[t % 2][:, :], PC[:, :], ACT.Identity, bias=cols[:, 0:1]).then_inc(s_ce, 1)

            def evac_y(U, t, l, embed):
                act.wait_ge(s_t2, U + 1)
                if embed:
                    nc.scalar.activation(HP[:, 2 * t:2 * t + 2, HALO:HALO + L],
                                         PB[:, :].rearrange("p (b t) -> p b t", b=2), ACT.Identity,
                                         bias=cols[:, 2:3], scale=cols[:, 1:2]).then_inc(s_y, 1)
                else:
                    if not isinstance(U, int) or U >= TILES + 2:
                        act.wait_ge(s_h, U - TILES - 1)
                    apart(act)
                    nc.scalar.activation(y[t % 2][:, :], PB[:, :], ACT.Identity,
                                         bias=lcol[:, 2, bass.ds(l, 1)],
                                         scale=lcol[:, 1, bass.ds(l, 1)]).then_inc(s_y, 1)

            def scale_out(V, t, l):
                act.wait_ge(s_o, V + 1)
                if not isinstance(V, int) or V >= 2:
                    act.wait_ge(s_rd, V - 1)
                apart(act)
                nc.scalar.activation(yo[t % 2][:, :], PO[:, :], ACT.Identity, bias=gb2[:, bass.ds(l, 1)],
                                     scale=lcol[:, 4, bass.ds(l, 1)]).then_inc(s_yo, 1)

            def gelu(V, t, l):
                act.wait_ge(s_h, V + 1)
                if not isinstance(V, int) or V >= 2:
                    act.wait_ge(s_o, V - 1)
                apart(act)
                for f in range(FC):
                    ins = nc.scalar.activation(g[t % 2][:, f, :], PH[:, f, :], ACT.Gelu,
                                               bias=b1[:, bass.ds(l, 1), f])
                ins.then_inc(s_g, 1)

            evac_embed(0)
            for t in range(TILES):
                if t + 1 < TILES:
                    evac_embed(t + 1)
                if t >= 1:
                    evac_y(t - 1, t - 1, 0, True)
            act.wait_ge(s_wl, 64)
            act.wait_ge(s_gb, 1)

            def layer(l, first):
                V0 = l * TILES
                for t in range(TILES):
                    if t == 0:
                        evac_y(V0 + TILES - 1, TILES - 1, 0 if first else l - 1, first)
                        if not first:
                            scale_out(V0 - 2, TILES - 2, l - 1)
                            gelu(V0 - 1, TILES - 1, l - 1)
                    else:
                        evac_y(V0 + TILES + t - 1, t - 1, l, False)
                        if t >= 2:
                            scale_out(V0 + t - 2, t - 2, l)
                        elif not first:
                            scale_out(V0 - 1, TILES - 1, l - 1)
                        gelu(V0 + t - 1, t - 1, l)

            layer(0, True)
            with act.Fori(1, LAYERS) as l:
                layer(l, False)
            V1 = LAYERS * TILES
            evac_y(V1 + TILES - 1, TILES - 1, LAYERS - 1, False)
            scale_out(V1 - 2, TILES - 2, LAYERS - 1)
            gelu(V1 - 1, TILES - 1, LAYERS - 1)
            scale_out(V1 - 1, TILES - 1, LAYERS - 1)
            for t in range(TILES):
                act.wait_ge(s_t2, V1 + TILES + t + 1)
                nc.scalar.activation(XT[:, t * TOK:(t + 1) * TOK], PB[:, :], ACT.Copy).then_inc(s_y, 1)

        @block.vector
        def _(dve):
            def stats(U, i, src, k):
                for j in range(SUB):
                    ins = nc.vector.bn_stats(st[i][:, j, :], src[:, j, :])
                ins.then_inc(s_bn, 1)
                dve.wait_ge(s_bn, k + 1)
                if not isinstance(k, int) or k >= 2:
                    dve.wait_ge(s_rs, k - 1)
                apart(dve)
                for j in range(SUB):
                    ins = nc.vector.bn_aggr(mv[i][:, j, :], st[i][:, j, :])
                ins.then_inc(s_mv, 1)

            def apply(i, src, k):
                dve.wait_ge(s_rs, k + 1)
                for j in range(SUB):
                    ins = nc.vector.tensor_scalar(ln[i][:, j, :], src[:, j, :], mv[i][:, j, 0:1],
                                                  rs[i][:, j:j + 1], ALU.subtract, ALU.mult)
                ins.then_inc(s_ap, 1)

            def stats_of(U, t):
                dve.wait_ge(s_t1, U + 1)
                stats(U, t % 2, PT[t % 2], U)

            def apply_of(U, t):
                if not isinstance(U, int) or U >= 2:
                    dve.wait_ge(s_t2, U - 1)
                apply(t % 2, PT[t % 2], U)

            def conv(V, t, l, first):
                if first:
                    dve.wait_ge(s_y, t + 1)
                else:
                    dve.wait_ge(s_rd, V - TILES + 1)
                dve.wait_ge(s_t1, V + TILES - 1)
                acc = cv[t % 2][:, :].rearrange("p (b t) -> p b t", b=2)
                for k in range(TAPS):
                    src = HP[:, 2 * t:2 * t + 2, k:k + L]
                    if k == 0:
                        ins = nc.vector.tensor_scalar(acc, src, dww[:, bass.ds(l, 1), k], lcol[:, 0, bass.ds(l, 1)],
                                                      ALU.mult, ALU.add)
                    else:
                        dve.wait_ge(s_ch, (TAPS - 1) * V + k)
                        ins = nc.vector.scalar_tensor_tensor(out=acc, in0=src, scalar=dww[:, bass.ds(l, 1), k],
                                                             in1=acc, op0=ALU.mult, op1=ALU.add)
                    ins.then_inc(s_ch if k < TAPS - 1 else s_cv, 1)

            def resid(V, t):
                dve.wait_ge(s_yo, V + 1)
                h = HP[:, 2 * t:2 * t + 2, HALO:HALO + L]
                nc.vector.tensor_tensor(h, h, yo[t % 2][:, :].rearrange("p (b t) -> p b t", b=2),
                                        ALU.add).then_inc(s_rd, 1)

            dve.wait_ge(s_wl, 64)
            nc.vector.tensor_tensor(gb2[:, :], lcol[:, 3, :], lcol[:, 4, :], ALU.mult).then_inc(s_gb, 1)
            for t in range(TILES):
                stats_of(t, t)
                if t >= 1:
                    apply_of(t - 1, t - 1)
            dve.wait_ge(s_ms, 2)

            def layer(l, first):
                V0 = l * TILES
                for t in range(TILES):
                    if t >= 1:
                        stats_of(V0 + TILES + t - 1, t - 1)
                    elif not first:
                        stats_of(V0 + TILES - 1, TILES - 1)
                    if t == 0 and first:
                        apply_of(TILES - 1, TILES - 1)
                        conv(V0, 0, l, True)
                    else:
                        conv(V0 + t, t, l, first)
                        apply_of(V0 + TILES + t - 1, (t - 1) % TILES)
                    if t >= 3 or not first:
                        resid(V0 + t - 3, (t - 3) % TILES)

            layer(0, True)
            with dve.Fori(1, LAYERS) as l:
                layer(l, False)
            V1 = LAYERS * TILES
            stats_of(V1 + TILES - 1, TILES - 1)
            apply_of(V1 + TILES - 1, TILES - 1)
            for t in range(TILES - 3, TILES):
                resid(V1 - TILES + t, t)
            base = V1 + TILES
            G = fing[:, 0:1, :].to_broadcast([P, SUB, P])
            Bf = fing[:, 1:2, :].to_broadcast([P, SUB, P])
            for t in range(TILES):
                dve.wait_ge(s_t1, base + t + 1)
                stats(0, 0, PT[0], base + 2 * t)
                if t == 0:
                    dve.wait_ge(s_t2, base)
                apply(0, PT[0], base + 2 * t)
                dve.wait_ge(s_ap, base + 2 * t + 1)
                r = R[:, SUB * t:SUB * (t + 1), :]
                nc.vector.tensor_tensor(r, ln[0][:, :, :], G, ALU.mult).then_inc(s_f, 1)
                dve.wait_ge(s_f, 2 * t + 1)
                nc.vector.tensor_tensor(r, r, Bf, ALU.add).then_inc(s_f, 1)
                dve.wait_ge(s_f, 2 * t + 2)
                stats(0, 1, r, base + 2 * t + 1)
                dve.wait_ge(s_t2, base + t)
                apply(1, r, base + 2 * t + 1)


def bn_norm(dve, nc, src, st, mv, bn_done, moments_ready, rstd_used, k):
    apart(dve)
    for j in range(src.shape[1]):
        ins = nc.vector.bn_stats(st[:, j, :], src[:, j, :])
    ins.then_inc(bn_done, 1)
    dve.wait_ge(bn_done, k + 1)
    if not isinstance(k, int) or k >= 2:
        dve.wait_ge(rstd_used, k - 1)
    apart(dve)
    for j in range(src.shape[1]):
        ins = nc.vector.bn_aggr(mv[:, j, :], st[:, j, :])
    ins.then_inc(moments_ready, 1)


def pool_rstd(pool, nc, mv, ve, rs, eps, mhalf, moments_ready, var_eps_ready, rstd_ready, applied, k):
    pool.wait_ge(moments_ready, k + 1)
    if not isinstance(k, int) or k >= 2:
        pool.wait_ge(applied, k - 1)
    nc.gpsimd.tensor_tensor(ve[:, :], mv[:, :, 1], eps[:, :], ALU.add).then_inc(var_eps_ready, 1)
    pool.wait_ge(var_eps_ready, k + 1)
    nc.gpsimd.tensor_tensor(rs[:, :], ve[:, :], mhalf[:, :], ALU.pow).then_inc(rstd_ready, 1)


def bn_apply(dve, nc, out, src, mv, rs, rstd_ready, applied, k):
    dve.wait_ge(rstd_ready, k + 1)
    for j in range(src.shape[1]):
        ins = nc.vector.tensor_scalar(out[:, j, :], src[:, j, :], mv[:, j, 0:1], rs[:, j:j + 1],
                                      ALU.subtract, ALU.mult)
    ins.then_inc(applied, 1)


def mixer_stage(nc, a, R, XT, ident):
    S, CH, K, RANK = 16, 2, 4, 8
    BC = 2 * S
    XR = BC + RANK
    STEPS = S * CH
    NDA, NHC = 4, 4
    SMALL = 1.0 / 64
    with ExitStack() as ctx:
        m = Mem(nc, ctx)
        inw = m.sb("inw", [P, 2, 4 * P])
        mcol = m.sb("mcol", [P, 2, CH, 3])
        cw = m.sb("m_cw", [P, 2, CH, K, P])
        alog = m.sb("alog", [P, 2, CH, S])
        negA = m.sb("negA", [P, 2, CH, S])
        xpw = m.sb("xpw", [P, 2, CH, XR])
        dtw = m.sb("dtw", [XR, 2, CH * P])
        outw = m.sb("outw", [P, 2, CH * P])
        fusw = m.sb("fusw", [P, 2, P])
        fusb = m.sb("fusb", [P, 1])
        gb = m.sb("mix_gb", [P, 2, P])
        eye3 = m.sb("eye3", [3 * BC, BC])
        pick = m.sb("pick", [3 * BC, BC, P], BF16)
        Wc = m.sb("Wc", [P, 2, CH, P])
        xs = [m.sb(f"xs{d}", [P, CH, TOK]) for d in range(2)]
        zs = [m.sb(f"zs{d}", [P, CH, TOK]) for d in range(2)]
        x40 = m.sb("x40", [XR, TOK])
        rem = m.sb("rem", [BC, TOK])
        mid = m.sb("mid", [BC, TOK], BF16)
        rows = [m.sb(f"rows{d}", [3 * BC, TOK], BF16) for d in range(2)]
        rv = m.sb("rv", [P, CH, TOK])
        eu = m.sb("eu", [P, CH, TOK])
        lw = m.sb("lw", [P, CH, TOK])
        pp = m.sb("pp", [P, CH, TOK])
        small = m.sb("small", [P, CH, TOK], U8)
        dl = [m.sb(f"dl{d}", [P, CH, TOK]) for d in range(2)]
        du = [m.sb(f"du{d}", [P, CH, TOK]) for d in range(2)]
        dA = [[m.sb(f"dA{d}_{i}", [P, TOK]) for i in range(NDA)] for d in range(2)]
        dbx = [m.sb(f"dbx{i}", [P, TOK]) for i in range(2)]
        hs = [m.sb(f"hs{i}", [P, TOK]) for i in range(2)]
        hc = [m.sb(f"hc{i}", [P, TOK]) for i in range(NHC)]
        yv = m.sb("yv", [P, CH, TOK])
        yb = [m.sb(f"yb{d}", [P, CH, TOK]) for d in range(2)]
        oT = m.sb("oT", [P, TOK])
        rT = m.sb("rT", [P, TOK])
        st = [m.sb(f"mst{i}", [P, SUB, 6]) for i in range(2)]
        mv = [m.sb(f"mmv{i}", [P, SUB, 2]) for i in range(2)]
        ve = [m.sb(f"mve{i}", [P, SUB]) for i in range(2)]
        rs = [m.sb(f"mrs{i}", [P, SUB]) for i in range(2)]
        ln = [m.sb(f"mln{i}", [P, SUB, P]) for i in range(2)]
        eps = m.sb("meps", [P, SUB])
        mhalf = m.sb("mmhalf", [P, SUB])
        Bb = [m.ps(f"Bb{i}", [P, TOK]) for i in range(2)]
        Cb = [m.ps(f"Cb{i}", [P, TOK]) for i in range(2)]
        PY = [m.ps(f"PY{i}", [P, TOK]) for i in range(CH)]
        PI = [m.ps(f"PI{i}", [P, TOK]) for i in range(2)]

        names = ("weights_loaded zeroed exp_alog negA_ready pick_ready wc_done wc_ready taps_ready z_done "
                 "conv_done silu_done zs_ready xproj_done x40_ready hi_ready split_chain rows_ready dt_done "
                 "exp_u softplus_in poly_chain poly_done mask_done log1p_done delta_ready du_ready "
                 "bcast_done dA_ready dbx_ready state_ready hc_ready y_step post_done yb_ready "
                 "out_done out_copied sum_ready sum_turned bn_done moments_ready var_eps_ready rstd_ready applied "
                 "gain_chain x_turned x_stored ln_a").split()
        s = {n: m.sem("m_" + n) for n in names}

        block = ctx.enter_context(nc.Block())

        TAIL = {"out": 2, "copy": 8, "sum": 6, "turn": 6, "stats1": 7, "apply1": 9, "stats2": 11, "apply2": 13,
                "back": 2, "store": 6}
        PREP = {"conv0": 6, "conv1": 10, "silu": 16, "xproj": 14, "x40": 19, "split": 16, "dt": 16,
                "softplus": 21, "log": 23, "z": 20, "zs": 28, "blend": 26}

        def prep(name, d):
            return PREP[name] + (2 if d == 0 and name != "conv0" else 0)

        def drive(eng, prologue, unit, epilogue):
            prologue()
            for T in range(2):
                unit(T, 0, True, T > 0)
                unit(T, 1, True, T > 0)
            with eng.Fori(2, TILES - 1) as T:
                unit(T, 0, True, True)
                unit(T, 1, True, True)
            unit(TILES - 1, 0, True, True)
            unit(TILES - 1, 1, False, True)
            epilogue()

        def tile_cols(T):
            return bass.ds(T * TOK, TOK)

        def tile_subs(T):
            return bass.ds(T * SUB, SUB)

        @block.sync
        def _(sp):
            for dst, src in ((inw[:, :, :], a["inw"]), (mcol[:, :, :, :], a["mcol"]), (alog[:, :, :, :], a["alog"]),
                             (xpw[:, :, :, :], a["xpw"]), (outw[:, :, :], a["outw"]), (fusw[:, :, :], a["fusw"]),
                             (fusb[:, :], a["fusb"]), (gb[:, :, :], a["mix_gb"].partition_broadcast(P)),
                             (eye3[:, :], a["eye3"]),
                             (cw[:, :, :, :, :], a["m_cw"].partition_broadcast(P))):
                sp.dma_start(dst, src).then_inc(s["weights_loaded"], 16)
            sp.wait_ge(s["zeroed"], 1)
            sp.dma_start(dtw[BC:XR, :, :], a["dtw"]).then_inc(s["weights_loaded"], 16)

        WL = 176

        @block.gpsimd
        def _(pool):
            nc.gpsimd.memset(dtw[:, :, :], 0.0).then_inc(s["zeroed"], 1)
            for i in range(NDA):
                nc.gpsimd.memset(dA[0][i][:, 0:TOK:L], 0.0)
                nc.gpsimd.memset(dA[1][i][:, L - 1:TOK:L], 0.0)
            nc.gpsimd.memset(eps[:, :], 1e-5)
            nc.gpsimd.memset(mhalf[:, :], -0.5).then_inc(s["zeroed"], 1)
            pool.wait_ge(s["zeroed"], 2)
            pool.wait_ge(s["weights_loaded"], WL)

            for d in range(2):
                x_half = inw[:, d, 0:CH * P].rearrange("p (c e) -> p c e", c=CH)
                for k in range(K):
                    ins = nc.gpsimd.tensor_tensor(cw[:, d, :, k, :], cw[:, d, :, k, :], x_half, ALU.mult)
            ins.then_inc(s["taps_ready"], 1)

            def poly(v):
                pool.wait_ge(s["exp_u"], v + 1)
                if not isinstance(v, int) or v >= 1:
                    pool.wait_ge(s["log1p_done"], v)
                apart(pool)
                n = 0
                for i, (x, f, add) in enumerate(((eu, -0.25, 1.0 / 3), (pp, 1.0, -0.5), (pp, 1.0, 1.0))):
                    nc.gpsimd.tensor_scalar(pp[:, :, :], x[:, :, :], f, add, ALU.mult, ALU.add
                                            ).then_inc(s["poly_chain"], 1)
                    n += 1
                    pool.wait_ge(s["poly_chain"], 6 * v + n)
                    apart(pool)
                    nc.gpsimd.tensor_tensor(pp[:, :, :], pp[:, :, :], eu[:, :, :], ALU.mult
                                            ).then_inc(s["poly_chain"], 1)
                    n += 1
                    if i < 2:
                        pool.wait_ge(s["poly_chain"], 6 * v + n)
                        apart(pool)

            def delta(v, d):
                pool.wait_ge(s["log1p_done"], v + 1)
                if not isinstance(v, int) or v >= 2:
                    pool.wait_ge(s["dA_ready"], STEPS * (v - 1))
                    pool.wait_ge(s["dbx_ready"], STEPS * (v - 1))
                nc.gpsimd.tensor_tensor(dl[d][:, :, :], rv[:, :, :], lw[:, :, :], ALU.add
                                        ).then_inc(s["delta_ready"], 1)
                pool.wait_ge(s["delta_ready"], v + 1)
                nc.gpsimd.tensor_tensor(du[d][:, :, :], dl[d][:, :, :], xs[d][:, :, :], ALU.mult
                                        ).then_inc(s["du_ready"], 1)

            def root(T, i):
                pool_rstd(pool, nc, mv[i], ve[i], rs[i], eps, mhalf, s["moments_ready"], s["var_eps_ready"],
                          s["rstd_ready"], s["applied"], 2 * T + i)

            def gate(u, d):
                pool.wait_ge(s["post_done"], u + 1)
                if not isinstance(u, int) or u >= 2:
                    pool.wait_ge(s["out_done"], (u - d) // 2 if isinstance(u, int) else T_of[0])
                nc.gpsimd.tensor_tensor(yb[d][:, :, :], yv[:, :, :], zs[d][:, :, :], ALU.mult
                                        ).then_inc(s["yb_ready"], 1)

            T_of = [0]

            def delta_of(v, d):
                poly(v)
                delta(v, d)

            def unit(T, d, has_next, has_prev):
                u = 2 * T + d
                T_of[0] = T
                if has_prev and d == 0:
                    root(T - 1, 0)
                    root(T - 1, 1)
                if has_next:
                    delta_of(u + 1, 1 - d)
                gate(u, d)

            def epilogue():
                root(TILES - 1, 0)
                root(TILES - 1, 1)

            drive(pool, lambda: delta_of(0, 0), unit, epilogue)

        @block.tensor
        def _(pe):
            pe.wait_ge(s["weights_loaded"], WL)
            for d in range(2):
                for c in range(CH):
                    mm = nc.tensor.matmul(PI[0][:, (d * CH + c) * P:(d * CH + c + 1) * P],
                                          outw[:, d, c * P:(c + 1) * P], fusw[:, d, :], start=True, stop=True)
            mm.then_inc(s["wc_done"], 1)

            def conv(v, d, c, T, free):
                if free is None:
                    pe.wait_ge(s["taps_ready"], 1)
                    pe.wait_ge(s["wc_ready"], 1)
                for name, value in free or ():
                    pe.wait_ge(s[name], value)
                out = PI[c][:, :].rearrange("p (b t) -> p b t", b=2)
                x = XT[:, tile_cols(T)].rearrange("p (b t) -> p b t", b=2)
                for k in reversed(range(K)):
                    n = K - 1 - k
                    near, far = slice(n, L), slice(0, L - n)
                    mm = nc.tensor.matmul(out[:, :, near if d == 0 else far], cw[:, d, c, k, :],
                                          x[:, :, far if d == 0 else near], start=(n == 0), stop=(k == 0),
                                          skip_group_check=True)
                mm.then_inc(s["conv_done"], 1)

            def z(v, d, T):
                pe.wait_ge(s["softplus_in"], v + 1)
                for c in range(CH):
                    mm = nc.tensor.matmul(PI[c][:, :], inw[:, d, (CH + c) * P:(CH + c + 1) * P],
                                          XT[:, tile_cols(T)], start=True, stop=True)
                mm.then_inc(s["z_done"], 1)

            def xproj(v, d):
                pe.wait_ge(s["silu_done"], v + 1)
                for c in range(CH):
                    mm = nc.tensor.matmul(PI[0][0:XR, :], xpw[:, d, c, :], xs[d][:, c, :],
                                          start=(c == 0), stop=(c == CH - 1))
                mm.then_inc(s["xproj_done"], 1)

            def dt(v, d):
                pe.wait_ge(s["hi_ready"], v + 1)
                for c in range(CH):
                    mm = nc.tensor.matmul(PI[c][:, :], dtw[:, d, c * P:(c + 1) * P], x40[:, :],
                                          start=True, stop=True)
                mm.then_inc(s["dt_done"], 1)

            def bcast(u, d, n):
                if n == 0:
                    pe.wait_ge(s["rows_ready"], u + 1)
                if not isinstance(u, int) or STEPS * u + 2 * n - 2 > 0:
                    pe.wait_ge(s["dbx_ready"], STEPS * u + 2 * n - 2)
                    pe.wait_ge(s["hc_ready"], STEPS * u + 2 * n - 2)
                nc.tensor.matmul(Bb[n % 2][:, :], pick[:, n, :], rows[d][:, :], start=True, stop=True)
                nc.tensor.matmul(Cb[n % 2][:, :], pick[:, S + n, :], rows[d][:, :], start=True, stop=True
                                 ).then_inc(s["bcast_done"], 1)

            def ysum(u, n, c):
                pe.wait_ge(s["hc_ready"], STEPS * u + 2 * n + c + 1)
                if n == 0 and (not isinstance(u, int) or u >= 1):
                    pe.wait_ge(s["post_done"], u)
                nc.tensor.matmul(PY[c][:, :], ident[:, :], hc[(2 * n + c) % NHC][:, :], start=(n == 0), stop=(n == S - 1)
                                 ).then_inc(s["y_step"], 1)

            def tail_out(T, last):
                pe.wait_ge(s["yb_ready"], 2 * T + 2)
                pe.wait_ge(s["zs_ready"], 2 * T + 2 if last else 2 * T + 3)
                k = 0
                for d in range(2):
                    for c in range(CH):
                        mm = nc.tensor.matmul(PI[0][:, :], Wc[:, d, c, :], yb[d][:, c, :],
                                              start=(k == 0), stop=(k == 3))
                        k += 1
                mm.then_inc(s["out_done"], 1)

            def tail_turn(T):
                pe.wait_ge(s["sum_ready"], T + 1)
                for j in range(SUB):
                    mm = nc.tensor.transpose(PI[1][:, j * P:(j + 1) * P], rT[:, j * P:(j + 1) * P], ident[:, :])
                mm.then_inc(s["sum_turned"], 1)

            def tail_back(T, last):
                pe.wait_ge(s["applied"], 2 * T + 2)
                if last:
                    pe.wait_ge(s["out_copied"], T + 1)
                else:
                    pe.wait_ge(s["zs_ready"], 2 * T + 4)
                for j in range(SUB):
                    mm = nc.tensor.transpose(PI[0][:, j * P:(j + 1) * P], ln[1][:, j, :], ident[:, :])
                mm.then_inc(s["x_turned"], 1)

            def prologue():
                pe.wait_ge(s["pick_ready"], 1)
                for c in range(CH):
                    conv(0, 0, c, 0, None)
                xproj(0, 0)
                dt(0, 0)
                z(0, 0, 0)

            def unit(T, d, has_next, has_prev):
                u = 2 * T + d
                T_next = T + d
                if not has_prev:
                    free = [[("zs_ready", u + 1)]] * 2
                elif d == 0:
                    free = [[("out_copied", T)], [("applied", 2 * T - 1)]]
                else:
                    free = [[("x_stored", T)], [("zs_ready", u + 1)]]
                bcast(u, d, 0)
                for n in range(S):
                    if n + 1 < S:
                        bcast(u, d, n + 1)
                    for c in range(CH):
                        step = 2 * n + c
                        ysum(u, n, c)
                        if has_prev and d == 0 and step == TAIL["out"]:
                            tail_out(T - 1, False)
                        if has_prev and d == 0 and step == TAIL["turn"]:
                            tail_turn(T - 1)
                        if has_prev and d == 1 and step == TAIL["back"]:
                            tail_back(T - 1, False)
                        for k in range(CH):
                            if has_next and step == prep(f"conv{k}", d):
                                conv(u + 1, 1 - d, k, T_next, free[k])
                        if has_next and step == prep("xproj", d):
                            xproj(u + 1, 1 - d)
                        if has_next and step == prep("dt", d):
                            dt(u + 1, 1 - d)
                        if has_next and step == prep("z", d):
                            z(u + 1, 1 - d, T_next)

            def epilogue():
                tail_out(TILES - 1, True)
                tail_turn(TILES - 1)
                tail_back(TILES - 1, True)

            drive(pe, prologue, unit, epilogue)

        @block.scalar
        def _(act):
            act.wait_ge(s["weights_loaded"], WL)
            act.wait_ge(s["zeroed"], 2)
            nc.scalar.activation(alog[:, :, :, :], alog[:, :, :, :], ACT.Exp).then_inc(s["exp_alog"], 1)
            act.wait_ge(s["exp_alog"], 1)
            nc.scalar.activation(negA[:, :, :, :], alog[:, :, :, :], ACT.Copy, scale=-1.0).then_inc(s["negA_ready"], 1)
            nc.scalar.activation(pick[:, :, :], eye3[:, :].unsqueeze(2).to_broadcast([3 * BC, BC, P]), ACT.Copy
                                 ).then_inc(s["pick_ready"], 1)
            act.wait_ge(s["wc_done"], 1)
            nc.scalar.activation(Wc[:, :, :, :].rearrange("p d c e -> p (d c e)"), PI[0][:, :], ACT.Copy
                                 ).then_inc(s["wc_ready"], 1)
            act.wait_ge(s["negA_ready"], 1)

            def silu(v, d):
                if not isinstance(v, int) or v >= 2:
                    act.wait_ge(s["yb_ready"], v - 1)
                for c in range(CH):
                    act.wait_ge(s["conv_done"], CH * v + c + 1)
                    ins = nc.scalar.activation(xs[d][:, c, :], PI[c][:, :], ACT.Silu, bias=mcol[:, d, c, 0:1])
                ins.then_inc(s["silu_done"], 1)

            def silu_z(v, d):
                act.wait_ge(s["z_done"], v + 1)
                if not isinstance(v, int) or v >= 2:
                    act.wait_ge(s["yb_ready"], v - 1)
                for c in range(CH):
                    ins = nc.scalar.activation(zs[d][:, c, :], PI[c][:, :], ACT.Silu)
                ins.then_inc(s["zs_ready"], 1)

            def x40_copy(v, d):
                act.wait_ge(s["xproj_done"], v + 1)
                if not isinstance(v, int) or v >= 1:
                    act.wait_ge(s["dt_done"], v)
                    act.wait_ge(s["rows_ready"], v)
                if not isinstance(v, int) or v >= 2:
                    act.wait_ge(s["bcast_done"], S * (v - 1))
                nc.scalar.activation(x40[:, :], PI[0][0:XR, :], ACT.Copy).then_inc(s["x40_ready"], 1)
                nc.scalar.activation(rows[d][0:BC, :], PI[0][0:BC, :], ACT.Copy).then_inc(s["hi_ready"], 1)

            def softplus(v, d):
                act.wait_ge(s["dt_done"], v + 1)
                if not isinstance(v, int) or v >= 1:
                    act.wait_ge(s["delta_ready"], v)
                for c in range(CH):
                    bias = mcol[:, d, c, 1:2]
                    nc.scalar.activation(rv[:, c, :], PI[c][:, :], ACT.Relu, bias=bias)
                    ins = nc.scalar.activation(lw[:, c, :], PI[c][:, :], ACT.Abs, bias=bias)
                ins.then_inc(s["softplus_in"], 1)
                act.wait_ge(s["softplus_in"], v + 1)
                nc.scalar.activation(eu[:, :, :], lw[:, :, :], ACT.Exp, scale=-1.0).then_inc(s["exp_u"], 1)

            def log(v):
                act.wait_ge(s["exp_u"], v + 1)
                nc.scalar.activation(lw[:, :, :], eu[:, :, :], ACT.Ln, bias=1.0).then_inc(s["ln_a"], 1)

            def decay(u, d, n, c):
                step = 2 * n + c
                if step == 0:
                    act.wait_ge(s["delta_ready"], u + 1)
                if not isinstance(u, int) or STEPS * u + step - NDA + 1 > 0:
                    act.wait_ge(s["state_ready"], STEPS * u + step - NDA + 1)
                src = dl[d][:, c, :].rearrange("p (b t) -> p b t", b=2)
                dst = dA[d][step % NDA][:, :].rearrange("p (b t) -> p b t", b=2)
                lo = 1 if d == 0 else 0
                nc.scalar.activation(dst[:, :, lo:lo + L - 1], src[:, :, lo:lo + L - 1], ACT.Exp,
                                     scale=negA[:, d, c, n:n + 1]).then_inc(s["dA_ready"], 1)

            def tail_out(T):
                act.wait_ge(s["out_done"], T + 1)
                if not isinstance(T, int) or T >= 1:
                    act.wait_ge(s["sum_ready"], T)
                nc.scalar.activation(oT[:, :], PI[0][:, :], ACT.Identity, bias=fusb[:, 0:1]
                                     ).then_inc(s["out_copied"], 1)

            def tail_store(T):
                act.wait_ge(s["x_turned"], T + 1)
                apart(act)
                nc.scalar.activation(XT[:, tile_cols(T)], PI[0][:, :], ACT.Copy).then_inc(s["x_stored"], 1)

            def prologue():
                silu(0, 0)
                x40_copy(0, 0)
                softplus(0, 0)
                log(0)
                silu_z(0, 0)

            def unit(T, d, has_next, has_prev):
                u = 2 * T + d
                for n in range(S):
                    for c in range(CH):
                        step = 2 * n + c
                        decay(u, d, n, c)
                        if has_prev and d == 0 and step == TAIL["copy"]:
                            tail_out(T - 1)
                        if has_prev and d == 1 and step == TAIL["store"]:
                            tail_store(T - 1)
                        if has_next and step == prep("silu", d):
                            silu(u + 1, 1 - d)
                        if has_next and step == prep("x40", d):
                            x40_copy(u + 1, 1 - d)
                        if has_next and step == prep("softplus", d):
                            softplus(u + 1, 1 - d)
                        if has_next and step == prep("log", d):
                            log(u + 1)
                        if has_next and step == prep("zs", d):
                            silu_z(u + 1, 1 - d)

            def epilogue():
                tail_out(TILES - 1)
                tail_store(TILES - 1)

            drive(act, prologue, unit, epilogue)

        @block.vector
        def _(dve):
            dve.wait_ge(s["zeroed"], 2)
            dve.wait_ge(s["weights_loaded"], WL)

            def split(v, d):
                dve.wait_ge(s["hi_ready"], v + 1)
                nc.vector.tensor_tensor(rem[:, :], x40[0:BC, :], rows[d][0:BC, :], ALU.subtract
                                        ).then_inc(s["split_chain"], 1)
                dve.wait_ge(s["split_chain"], 2 * v + 1)
                nc.vector.tensor_copy(mid[:, :], rem[:, :]).then_inc(s["split_chain"], 1)
                nc.vector.tensor_copy(rows[d][BC:2 * BC, :], rem[:, :])
                dve.wait_ge(s["split_chain"], 2 * v + 2)
                nc.vector.tensor_tensor(rows[d][2 * BC:3 * BC, :], rem[:, :], mid[:, :], ALU.subtract
                                        ).then_inc(s["rows_ready"], 1)

            def blend(v):
                dve.wait_ge(s["ln_a"], v + 1)
                nc.vector.tensor_scalar(small[:, :, :], eu[:, :, :], SMALL, None, ALU.is_lt
                                        ).then_inc(s["mask_done"], 1)
                dve.wait_ge(s["mask_done"], v + 1)
                dve.wait_ge(s["poly_chain"], 6 * v + 6)
                apart(dve)
                nc.vector.copy_predicated(lw[:, :, :], small[:, :, :], pp[:, :, :]).then_inc(s["log1p_done"], 1)

            def order(d, ap):
                return ap if d == 0 else ap[:, ::-1]

            def to_state(u, d, n, c):
                step = 2 * n + c
                if step == 0:
                    dve.wait_ge(s["du_ready"], u + 1)
                if c == 0:
                    dve.wait_ge(s["bcast_done"], S * u + n + 1)
                nc.vector.tensor_tensor(dbx[step % 2][:, :], du[d][:, c, :], Bb[n % 2][:, :], ALU.mult
                                        ).then_inc(s["dbx_ready"], 1)

            def scan(u, d, n, c):
                step = 2 * n + c
                dve.wait_ge(s["dA_ready"], STEPS * u + step + 1)
                dve.wait_ge(s["dbx_ready"], STEPS * u + step + 1)
                nc.vector.tensor_tensor_scan(order(d, hs[step % 2][:, :]), order(d, dA[d][step % NDA][:, :]),
                                             order(d, dbx[step % 2][:, :]), 0.0, ALU.mult, ALU.add
                                             ).then_inc(s["state_ready"], 1)

            def from_state(u, n, c):
                step = 2 * n + c
                dve.wait_ge(s["state_ready"], STEPS * u + step + 1)
                if not isinstance(u, int) or STEPS * u + step - NHC + 1 > 0:
                    dve.wait_ge(s["y_step"], STEPS * u + step - NHC + 1)
                nc.vector.tensor_tensor(hc[step % NHC][:, :], hs[step % 2][:, :], Cb[n % 2][:, :], ALU.mult
                                        ).then_inc(s["hc_ready"], 1)

            def post(u, d):
                dve.wait_ge(s["y_step"], STEPS * (u + 1))
                if not isinstance(u, int) or u >= 1:
                    dve.wait_ge(s["yb_ready"], u)
                for c in range(CH):
                    ins = nc.vector.scalar_tensor_tensor(out=yv[:, c, :], in0=xs[d][:, c, :],
                                                         scalar=mcol[:, d, c, 2:3], in1=PY[c][:, :],
                                                         op0=ALU.mult, op1=ALU.add)
                ins.then_inc(s["post_done"], 1)

            def tail_sum(T):
                dve.wait_ge(s["out_copied"], T + 1)
                if not isinstance(T, int) or T >= 1:
                    dve.wait_ge(s["sum_turned"], T)
                nc.vector.tensor_tensor(rT[:, :], oT[:, :], XT[:, tile_cols(T)], ALU.add).then_inc(s["sum_ready"], 1)

            def tail_stats(T, i):
                if i == 0:
                    dve.wait_ge(s["sum_turned"], T + 1)
                    src = PI[1][:, :].rearrange("p (j c) -> p j c", j=SUB)
                else:
                    dve.wait_ge(s["gain_chain"], 3 * T + 3)
                    src = R[:, tile_subs(T), :]
                bn_norm(dve, nc, src, st[i], mv[i], s["bn_done"], s["moments_ready"], s["rstd_ready"], 2 * T + i)

            def tail_apply(T, i):
                src = PI[1][:, :].rearrange("p (j c) -> p j c", j=SUB) if i == 0 else R[:, tile_subs(T), :]
                if i == 1 and (not isinstance(T, int) or T >= 1):
                    dve.wait_ge(s["x_turned"], T)
                bn_apply(dve, nc, ln[i], src, mv[i], rs[i], s["rstd_ready"], s["applied"], 2 * T + i)
                if i == 0:
                    x = ln[0][:, :, :]
                    dve.wait_ge(s["applied"], 2 * T + 1)
                    nc.vector.tensor_tensor(x, x, gb[:, 0:1, :].to_broadcast([P, SUB, P]), ALU.mult
                                            ).then_inc(s["gain_chain"], 1)
                    dve.wait_ge(s["gain_chain"], 3 * T + 1)
                    nc.vector.tensor_tensor(x, x, gb[:, 1:2, :].to_broadcast([P, SUB, P]), ALU.add
                                            ).then_inc(s["gain_chain"], 1)
                    dve.wait_ge(s["gain_chain"], 3 * T + 2)
                    r = R[:, tile_subs(T), :]
                    nc.vector.tensor_tensor(r, r, x, ALU.add).then_inc(s["gain_chain"], 1)

            def prologue():
                split(0, 0)
                blend(0)

            def unit(T, d, has_next, has_prev):
                u = 2 * T + d
                to_state(u, d, 0, 0)
                for n in range(S):
                    for c in range(CH):
                        step = 2 * n + c
                        scan(u, d, n, c)
                        if step + 1 < STEPS:
                            to_state(u, d, (step + 1) // 2, (step + 1) % 2)
                        from_state(u, n, c)
                        if has_prev and d == 0:
                            if step == TAIL["sum"]:
                                tail_sum(T - 1)
                            if step == TAIL["stats1"]:
                                tail_stats(T - 1, 0)
                            if step == TAIL["apply1"]:
                                tail_apply(T - 1, 0)
                            if step == TAIL["stats2"]:
                                tail_stats(T - 1, 1)
                            if step == TAIL["apply2"]:
                                tail_apply(T - 1, 1)
                        if has_next:
                            if step == prep("split", d):
                                split(u + 1, 1 - d)
                            if step == prep("blend", d):
                                blend(u + 1)
                post(u, d)

            def epilogue():
                T = TILES - 1
                tail_sum(T)
                tail_stats(T, 0)
                tail_apply(T, 0)
                tail_stats(T, 1)
                tail_apply(T, 1)

            drive(dve, prologue, unit, epilogue)


def expert_choice_stage(nc, a, R, XT, ident, w_dram):
    E, F, CAP = 8, 512, 1024
    FC = F // P
    BITS = 30
    with ExitStack() as ctx:
        m = Mem(nc, ctx)
        wr = m.sb("wr", [P, E])
        w1 = m.sb("e_w1", [P, E, F])
        b1 = m.sb("e_b1", [P, E, FC])
        w2 = m.sb("e_w2", [P, E, FC, P])
        b2 = m.sb("e_b2", [P, E])
        same = m.sb("same", [P, P])
        before = m.sb("before", [P, P])
        bit = m.sb("bit", [P, BITS], I32)
        ones = m.sb("e_ones", [P, L])
        LT = m.sb("LT", [P, 2, E, B])
        V = m.sb("V", [P, L])
        pr = m.sb("pr", [P, L])
        junk = m.sb("junk", [P, L])
        gt = m.sb("gt", [P, L])
        eq = m.sb("eq", [P, L])
        cum = m.sb("cum", [P, L])
        wt = m.sb("wt", [P, L])
        mx = m.sb("mx", [P, 1])
        mrow = m.sb("mrow", [1, E, B])
        m8 = m.sb("m8", [1, E])
        nmx = m.sb("nmx", [P, 1])
        ssum = m.sb("ssum", [P, 1])
        rtot = m.sb("rtot", [P, 1])
        cur = m.sb("cur", [P, 1], I32)
        cand = m.sb("cand", [P, 1], I32)
        keep = m.sb("keep", [P, 1], I32)
        cnt = m.sb("cnt", [P, 1])
        room = m.sb("room", [P, 1])
        off = m.sb("off", [P, 1])
        wb = [m.sb(f"wb{i}", [P, E, TOK]) for i in range(2)]
        hb = [m.sb(f"hb{i}", [P, FC, TOK]) for i in range(2)]
        part = [m.sb(f"part{i}", [P, TOK]) for i in range(2)]
        acc = m.sb("acc", [P, TOK])
        st = m.sb("est", [P, SUB, 6])
        mv = m.sb("emv", [P, SUB, 2])
        ve = m.sb("eve", [P, SUB])
        rs = m.sb("ers", [P, SUB])
        ln = m.sb("eln", [P, SUB, P])
        eps = m.sb("eeps", [P, SUB])
        mhalf = m.sb("emhalf", [P, SUB])
        PH = m.ps("ePH", [P, FC, TOK])
        PO = [m.ps(f"ePO{i}", [P, TOK]) for i in range(2)]
        PT = m.ps("ePT", [P, TOK])
        PB = m.ps("ePB", [P, TOK])

        names = ("routing_loaded experts_loaded logits_done logits_copied rows_turned rows_copied max_done max_turned "
                 "max8_done max_row_ready max_sent negmax_ready exp_done total_sent chain counted bit_sent "
                 "weight_ready weight_stored wb_loaded0 wb_loaded1 hid_done gelu_done out_done part_ready acc_step "
                 "acc_turned resid_done bn_done moments_ready var_eps_ready rstd_ready applied x_turned x_stored "
                 "consts zero_cur off_ready").split()
        s = {n: m.sem("e_" + n) for n in names}
        block = ctx.enter_context(nc.Block())

        def drive(eng, unit, tail):
            for T in range(2):
                unit(T, T > 0)
            with eng.Fori(2, TILES) as T:
                unit(T, True)
            tail(TILES - 1)

        @block.sync
        def _(sp):
            for dst, src in ((wr[:, :], a["wr"]), (same[:, :], a["same"]), (before[:, :], a["before"]),
                             (bit[:, :], a["bit"].partition_broadcast(P))):
                sp.dma_start(dst, src).then_inc(s["routing_loaded"], 16)
            for dst, src in ((w1[:, :, :], a["e_w1"]), (b1[:, :, :], a["e_b1"]), (w2[:, :, :, :], a["e_w2"]),
                             (b2[:, :], a["e_b2"])):
                sp.dma_start(dst, src).then_inc(s["experts_loaded"], 16)
            sp.wait_ge(s["weight_ready"], 1)
            sp.dma_start(w_dram.rearrange("e (b t) -> (e b) t", b=B), wt[:, :]).then_inc(s["weight_stored"], 16)
            sp.wait_ge(s["weight_stored"], 16)

            def load(T, i):
                sp.dma_start(wb[i][:, :, :], w_dram[:, bass.ds(T * TOK, TOK)].partition_broadcast(P)
                             ).then_inc(s[f"wb_loaded{i}"], 16)

            load(0, 0)
            load(1, 1)
            with sp.Fori(1, TILES // 2) as q:
                for i in range(2):
                    sp.wait_ge(s["part_ready"], E * (2 * q + i - 1))
                    load(2 * q + i, i)

        @block.gpsimd
        def _(pool):
            nc.gpsimd.memset(eps[:, :], 1e-5)
            nc.gpsimd.memset(ones[:, :], 1.0).then_inc(s["consts"], 1)
            nc.gpsimd.memset(mhalf[:, :], -0.5).then_inc(s["consts"], 1)
            pool.wait_ge(s["consts"], 2)

            def root(T):
                pool_rstd(pool, nc, mv, ve, rs, eps, mhalf, s["moments_ready"], s["var_eps_ready"],
                          s["rstd_ready"], s["applied"], T)

            root(0)
            root(1)
            with pool.Fori(2, TILES) as T:
                root(T)

        @block.tensor
        def _(pe):
            pe.wait_ge(s["routing_loaded"], 64)
            for j in range(N // P):
                mm = nc.tensor.matmul(PT[:, j * E:(j + 1) * E], XT[:, j * P:(j + 1) * P], wr[:, :],
                                      start=True, stop=True)
            mm.then_inc(s["logits_done"], 1)
            pe.wait_ge(s["logits_copied"], 1)
            for h in range(2):
                mm = nc.tensor.transpose(PB[:, h * P:(h + 1) * P], LT[:, h, :, :].rearrange("p e b -> p (e b)"),
                                         ident[:, :])
            mm.then_inc(s["rows_turned"], 1)
            pe.wait_ge(s["max_done"], 1)
            nc.tensor.transpose(PT[0:1, 0:P], mx[:, :], ident[:, :]).then_inc(s["max_turned"], 1)
            pe.wait_ge(s["max_row_ready"], 1)
            pe.wait_ge(s["consts"], 2)
            nc.tensor.matmul(PT[:, 0:1], mrow[:, :, :].rearrange("o e b -> o (e b)"), ones[0:1, 0:1],
                             start=True, stop=True).then_inc(s["max_sent"], 1)
            pe.wait_ge(s["exp_done"], 1)
            nc.tensor.matmul(PT[:, 0:1], same[:, :], ssum[:, :], start=True, stop=True).then_inc(s["total_sent"], 1)
            pe.wait_ge(s["counted"], 1)
            nc.tensor.matmul(PT[:, 0:1], same[:, :], cnt[:, :], start=True, stop=True).then_inc(s["bit_sent"], 1)
            with pe.Fori(1, BITS) as i:
                pe.wait_ge(s["counted"], i + 1)
                nc.tensor.matmul(PT[:, 0:1], same[:, :], cnt[:, :], start=True, stop=True).then_inc(s["bit_sent"], 1)
            pe.wait_ge(s["counted"], BITS + 1)
            nc.tensor.matmul(PT[:, 0:1], same[:, :], cnt[:, :], start=True, stop=True).then_inc(s["bit_sent"], 1)
            pe.wait_ge(s["counted"], BITS + 2)
            nc.tensor.matmul(PB[:, 0:1], before[:, :], cum[:, L - 1:L], start=True, stop=True
                             ).then_inc(s["bit_sent"], 1)

            pe.wait_ge(s["experts_loaded"], 64)

            def hid(T, g, e):
                for f in range(FC):
                    if not isinstance(g, int) or g >= 1:
                        pe.wait_ge(s["gelu_done"], FC * (g - 1) + f + 1)
                    nc.tensor.matmul(PH[:, f, :], w1[:, e, f * P:(f + 1) * P], XT[:, bass.ds(T * TOK, TOK)],
                                     start=True, stop=True).then_inc(s["hid_done"], 1)

            def out(g, e, i):
                pe.wait_ge(s["gelu_done"], FC * (g + 1))
                if not isinstance(g, int) or g >= 2:
                    pe.wait_ge(s["part_ready"], g - 1)
                for f in range(FC):
                    mm = nc.tensor.matmul(PO[i][:, :], w2[:, e, f, :], hb[i][:, f, :],
                                          start=(f == 0), stop=(f == FC - 1))
                mm.then_inc(s["out_done"], 1)

            def turn(T):
                pe.wait_ge(s["acc_step"], E * (T + 1))
                for j in range(SUB):
                    mm = nc.tensor.transpose(PT[:, j * P:(j + 1) * P], acc[:, j * P:(j + 1) * P], ident[:, :])
                mm.then_inc(s["acc_turned"], 1)

            def back(T):
                pe.wait_ge(s["applied"], T + 1)
                if not isinstance(T, int) or T >= 1:
                    pe.wait_ge(s["x_stored"], T)
                for j in range(SUB):
                    mm = nc.tensor.transpose(PB[:, j * P:(j + 1) * P], ln[:, j, :], ident[:, :])
                mm.then_inc(s["x_turned"], 1)

            def unit(T, has_prev):
                for e in range(E):
                    g = T * E + e
                    hid(T, g, e)
                    if not isinstance(g, int) or g >= 1:
                        out(g - 1, (e - 1) % E, (e + 1) % 2)
                    if has_prev and e == 1:
                        turn(T - 1)
                    if has_prev and e == 4:
                        back(T - 1)

            def tail(T):
                out(E * TILES - 1, E - 1, 1)
                turn(T)
                back(T)

            drive(pe, unit, tail)

        @block.scalar
        def _(act):
            act.wait_ge(s["logits_done"], 1)
            nc.scalar.activation(LT[:, :, :, :], PT[:, 0:N // P * E].rearrange("p (b h e) -> p h e b", h=2, e=E),
                                 ACT.Copy).then_inc(s["logits_copied"], 1)
            act.wait_ge(s["rows_turned"], 1)
            nc.scalar.activation(V[:, :], PB[:, 0:L], ACT.Copy).then_inc(s["rows_copied"], 1)
            act.wait_ge(s["max_sent"], 1)
            nc.scalar.activation(nmx[:, :], PT[:, 0:1], ACT.Copy, scale=-1.0).then_inc(s["negmax_ready"], 1)
            act.wait_ge(s["negmax_ready"], 1)
            act.wait_ge(s["rows_copied"], 1)
            nc.scalar.activation(pr[:, :], V[:, :], ACT.Exp, bias=nmx[:, :], accum_out=ssum[:, :]
                                 ).then_inc(s["exp_done"], 1)
            act.wait_ge(s["bit_sent"], BITS + 2)
            nc.scalar.activation(off[:, :], PB[:, 0:1], ACT.Copy).then_inc(s["off_ready"], 1)
            act.wait_ge(s["experts_loaded"], 64)

            def gelu(g, e, i):
                for f in range(FC):
                    act.wait_ge(s["hid_done"], FC * g + f + 1)
                    if f == 0 and (not isinstance(g, int) or g >= 2):
                        act.wait_ge(s["out_done"], g - 1)
                    nc.scalar.activation(hb[i][:, f, :], PH[:, f, :], ACT.Gelu, bias=b1[:, e, f:f + 1]
                                         ).then_inc(s["gelu_done"], 1)

            def store(T):
                act.wait_ge(s["x_turned"], T + 1)
                apart(act)
                nc.scalar.activation(XT[:, bass.ds(T * TOK, TOK)], PB[:, :], ACT.Copy).then_inc(s["x_stored"], 1)

            def unit(T, has_prev):
                for e in range(E):
                    gelu(T * E + e, e, e % 2)
                    if has_prev and e == 4:
                        store(T - 1)

            drive(act, unit, store)

        @block.vector
        def _(dve):
            n = [0]

            def link(ins):
                n[0] += 1
                ins.then_inc(s["chain"], 1)
                dve.wait_ge(s["chain"], n[0])

            nc.vector.memset(cur[:, :], 0).then_inc(s["zero_cur"], 1)
            dve.wait_ge(s["rows_copied"], 1)
            nc.vector.reduce_max(mx[:, :], V[:, :], AX_X).then_inc(s["max_done"], 1)
            dve.wait_ge(s["max_turned"], 1)
            link(nc.vector.reduce_max(m8[:, :], PT[0:1, 0:P].rearrange("o (e b) -> o e b", b=B), AX_X))
            nc.vector.tensor_copy(mrow[:, :, :], m8[:, :].unsqueeze(2).to_broadcast([1, E, B])
                                  ).then_inc(s["max_row_ready"], 1)
            dve.wait_ge(s["total_sent"], 1)
            link(nc.vector.reciprocal(rtot[:, :], PT[:, 0:1]))
            link(nc.vector.tensor_scalar(pr[:, :], pr[:, :], rtot[:, :], None, ALU.mult))
            dve.wait_ge(s["routing_loaded"], 64)
            dve.wait_ge(s["zero_cur"], 1)
            PER = 3
            n0 = n[0]

            def search(i):
                nc.vector.tensor_tensor(cand[:, :], cur[:, :], bit[:, bass.ds(i, 1)], ALU.bitwise_or
                                        ).then_inc(s["chain"], 1)
                dve.wait_ge(s["chain"], n0 + PER * i + 1)
                nc.vector.tensor_scalar(junk[:, :], pr[:, :], cand[:, :].bitcast(F32), None, ALU.is_ge, ALU.add,
                                        accum_out=cnt[:, :]).then_inc(s["counted"], 1)
                dve.wait_ge(s["bit_sent"], i + 1)
                nc.vector.tensor_scalar(keep[:, :], PT[:, 0:1], float(CAP), None, ALU.is_ge).then_inc(s["chain"], 1)
                dve.wait_ge(s["chain"], n0 + PER * i + 2)
                apart(dve)
                nc.vector.copy_predicated(cur[:, :], keep[:, :], cand[:, :]).then_inc(s["chain"], 1)
                dve.wait_ge(s["chain"], n0 + PER * i + 3)

            with dve.Fori(0, BITS) as i:
                search(i)
            n[0] = n0 + PER * BITS
            thr = cur[:, :].bitcast(F32)
            nc.vector.tensor_scalar(gt[:, :], pr[:, :], thr, None, ALU.is_gt, ALU.add, accum_out=cnt[:, :]
                                    ).then_inc(s["counted"], 1)
            link(nc.vector.tensor_scalar(eq[:, :], pr[:, :], thr, None, ALU.is_equal))
            nc.vector.tensor_tensor_scan(cum[:, :], ones[:, :], eq[:, :], 0.0, ALU.mult, ALU.add
                                         ).then_inc(s["counted"], 1)
            dve.wait_ge(s["bit_sent"], BITS + 1)
            link(nc.vector.tensor_scalar(room[:, :], PT[:, 0:1], -1.0, float(CAP), ALU.mult, ALU.add))
            dve.wait_ge(s["off_ready"], 1)
            link(nc.vector.tensor_scalar(cum[:, :], cum[:, :], off[:, :], room[:, :], ALU.add, ALU.is_le))
            link(nc.vector.tensor_tensor(eq[:, :], eq[:, :], cum[:, :], ALU.mult))
            link(nc.vector.tensor_tensor(gt[:, :], gt[:, :], eq[:, :], ALU.add))
            nc.vector.tensor_tensor(wt[:, :], gt[:, :], pr[:, :], ALU.mult).then_inc(s["weight_ready"], 1)
            dve.wait_ge(s["experts_loaded"], 64)

            def weigh(T, g, e, i, ti):
                dve.wait_ge(s["out_done"], g + 1)
                if e == 0:
                    dve.wait_ge(s[f"wb_loaded{ti}"], 16 * T_half[0])
                dst = acc if e == 0 else part[i]
                if e == 0 and (not isinstance(T, int) or T >= 1):
                    dve.wait_ge(s["acc_turned"], T)
                ins = nc.vector.scalar_tensor_tensor(out=dst[:, :], in0=PO[i][:, :], scalar=b2[:, e:e + 1],
                                                     in1=wb[ti][:, e, :], op0=ALU.add, op1=ALU.mult)
                ins.then_inc(s["part_ready"], 1)

            def add(T, g, e, i):
                dve.wait_ge(s["part_ready"], g + 1)
                if e == 0:
                    apart(dve)
                    nc.vector.engine_nop().then_inc(s["acc_step"], 1)
                else:
                    dve.wait_ge(s["acc_step"], g)
                    nc.vector.tensor_tensor(acc[:, :], acc[:, :], part[i][:, :], ALU.add).then_inc(s["acc_step"], 1)

            def resid(T):
                dve.wait_ge(s["acc_turned"], T + 1)
                r = R[:, bass.ds(T * SUB, SUB), :]
                nc.vector.tensor_tensor(r, r, PT[:, :].rearrange("p (j c) -> p j c", j=SUB), ALU.add
                                        ).then_inc(s["resid_done"], 1)

            def stats(T):
                dve.wait_ge(s["resid_done"], T + 1)
                bn_norm(dve, nc, R[:, bass.ds(T * SUB, SUB), :], st, mv, s["bn_done"], s["moments_ready"],
                        s["rstd_ready"], T)

            def apply(T):
                if not isinstance(T, int) or T >= 1:
                    dve.wait_ge(s["x_turned"], T)
                bn_apply(dve, nc, ln, R[:, bass.ds(T * SUB, SUB), :], mv, rs, s["rstd_ready"], s["applied"], T)

            T_half = [0]

            def unit(T, ti, has_prev):
                T_half[0] = T // 2 + 1 if isinstance(T, int) else T_half[0]
                for e in range(E):
                    g = T * E + e
                    weigh(T, g, e, e % 2, ti)
                    add(T, g, e, e % 2)
                    if has_prev and e == 1:
                        resid(T - 1)
                    if has_prev and e == 2:
                        stats(T - 1)
                    if has_prev and e == 3:
                        apply(T - 1)

            unit(0, 0, False)
            unit(1, 1, True)
            with dve.Fori(1, TILES // 2) as q:
                for i in range(2):
                    T_half[0] = q + 1
                    unit(2 * q + i, i, True)
            resid(TILES - 1)
            stats(TILES - 1)
            apply(TILES - 1)


def attention_stage(nc, a, R, XT, ident):
    H, DH = 8, 64
    INNER = H * DH
    IC = INNER // P
    SCALE = DH ** -0.5
    NT = L // P
    with ExitStack() as ctx:
        m = Mem(nc, ctx)
        wqkv = m.sb("wqkv", [P, 3 * INNER])
        bqk = m.sb("bqk", [P, 2, IC])
        bv = m.sb("bv", [P, INNER])
        th1 = m.sb("th1", [P, IC, H])
        th2 = m.sb("th2", [P, H, INNER])
        wo = m.sb("wo", [P, IC, P])
        bo = m.sb("bo", [P, 1])
        xb = [m.sb(f"xb{i}", [P, L]) for i in range(2)]
        qT = [m.sb(f"qT{i}", [P, IC, L]) for i in range(2)]
        kT = [m.sb(f"kT{i}", [P, IC, L]) for i in range(2)]
        v = [m.sb(f"v{i}", [P, NT, INNER]) for i in range(2)]
        vh = [m.sb(f"vh{i}", [P, NT, INNER]) for i in range(2)]
        qg = [m.sb(f"qg{i}", [P, IC, L]) for i in range(2)]
        nm = [m.sb(f"nm{i}", [P, NT]) for i in range(2)]
        sm = [m.sb(f"sm{i}", [P, NT]) for i in range(2)]
        ri = [m.sb(f"ri{i}", [P, NT]) for i in range(2)]
        ex = [m.sb(f"ex{i}", [P, NT, L]) for i in range(2)]
        at = [m.sb(f"at{i}", [P, NT, L]) for i in range(2)]
        oT = m.sb("a_oT", [P, IC, L])
        fo = m.sb("fo", [P, L])
        st = m.sb("ast", [P, NT, 6])
        mv = m.sb("amv", [P, NT, 2])
        ve = m.sb("ave", [P, NT])
        rs = m.sb("ars", [P, NT])
        ln = m.sb("aln", [P, NT, P])
        eps = m.sb("aeps", [P, NT])
        mhalf = m.sb("amhalf", [P, NT])
        PS = [m.ps(f"aPS{i}", [P, NT, L]) for i in range(2)]
        PA = m.ps("aPA", [P, NT, L])
        PO = [m.ps(f"aPO{i}", [P, 2, L]) for i in range(2)]
        PQ = m.ps("aPQ", [P, 2, TOK])
        PX = m.ps("aPX", [P, TOK])

        names = ("loaded consts x_copied q_done q_ready k_done k_ready v_done v_ready vh_ready qg_ready scores_done "
                 "max_ready exp_done recip_ready norm_done turned at_ready out_done out_copied proj_done proj_copied "
                 "proj_turned resid_done bn_done moments_ready var_eps_ready rstd_ready applied x_turned "
                 "x_stored").split()
        s = {n: m.sem("a_" + n) for n in names}
        block = ctx.enter_context(nc.Block())
        LOADED = 16 * 7

        def after(eng, name, n):
            if not isinstance(n, int) or n > 0:
                eng.wait_ge(s[name], n)

        def drive(eng, prologue, unit, epilogue):
            prologue()
            unit(0, 0, True, False)
            unit(1, 1, True, True)
            with eng.Fori(1, B // 2 - 1) as q:
                for i in range(2):
                    unit(2 * q + i, i, True, True)
            unit(B - 2, 0, True, True)
            unit(B - 1, 1, False, True)
            epilogue()

        @block.sync
        def _(sp):
            for dst, src in ((wqkv[:, :], a["wqkv"]), (bqk[:, :, :], a["bqk"]), (bv[:, :], a["bv"].partition_broadcast(P)),
                             (th1[:, :, :], a["th1"]), (th2[:, :, :], a["th2"].partition_broadcast(P)),
                             (wo[:, :, :], a["wo"]), (bo[:, :], a["bo"])):
                sp.dma_start(dst, src).then_inc(s["loaded"], 16)

        @block.gpsimd
        def _(pool):
            nc.gpsimd.memset(eps[:, :], 1e-5)
            nc.gpsimd.memset(mhalf[:, :], -0.5).then_inc(s["consts"], 1)
            pool.wait_ge(s["consts"], 1)
            pool.wait_ge(s["loaded"], LOADED)

            def x_copy(b, i):
                after(pool, "v_done", b - 1)
                apart(pool)
                nc.gpsimd.tensor_copy(xb[i][:, :], XT[:, bass.ds(b * L, L)]).then_inc(s["x_copied"], 1)

            def heads(b, i, g):
                c = H * b + g
                if g == 0:
                    pool.wait_ge(s["v_ready"], b + 1)
                after(pool, "out_done", c - 1)
                nc.gpsimd.tensor_tensor(vh[g % 2][:, :, :], v[i][:, :, :],
                                        th2[:, g:g + 1, :].to_broadcast([P, NT, INNER]), ALU.mult
                                        ).then_inc(s["vh_ready"], 1)

            def root(b):
                pool_rstd(pool, nc, mv, ve, rs, eps, mhalf, s["moments_ready"], s["var_eps_ready"],
                          s["rstd_ready"], s["applied"], b)

            def unit(b, i, has_next, has_prev):
                for g in range(H):
                    heads(b, i, g)
                    if has_next and g == 0:
                        x_copy(b + 1, 1 - i)
                    if has_prev and g == 3:
                        root(b - 1)

            drive(pool, lambda: x_copy(0, 0), unit, lambda: root(B - 1))

        @block.tensor
        def _(pe):
            pe.wait_ge(s["loaded"], LOADED)

            def q_or_k(b, i, which):
                after(pe, "v_ready", b) if which == 0 else pe.wait_ge(s["q_ready"], b + 1)
                for c in range(IC):
                    mm = nc.tensor.matmul(PQ[:, c // 2, c % 2 * L:(c % 2 + 1) * L],
                                          wqkv[:, which * INNER + c * P:which * INNER + (c + 1) * P],
                                          XT[:, bass.ds(b * L, L)], start=True, stop=True)
                mm.then_inc(s["q_done" if which == 0 else "k_done"], 1)

            def v_proj(b, i):
                pe.wait_ge(s["k_ready"], b + 1)
                pe.wait_ge(s["x_copied"], b + 1)
                for t in range(NT):
                    mm = nc.tensor.matmul(PQ[:, t, :], xb[i][:, t * P:(t + 1) * P], wqkv[:, 2 * INNER:3 * INNER],
                                          start=True, stop=True)
                mm.then_inc(s["v_done"], 1)

            def scores(b, i, g):
                c = H * b + g
                pe.wait_ge(s["qg_ready"], c + 1)
                if g == 0:
                    pe.wait_ge(s["k_ready"], b + 1)
                after(pe, "exp_done", c - 1)
                for t in range(NT):
                    for j in range(IC):
                        mm = nc.tensor.matmul(PS[g % 2][:, t, :], qg[g % 2][:, j, t * P:(t + 1) * P],
                                              kT[i][:, j, :], start=(j == 0), stop=(j == IC - 1))
                mm.then_inc(s["scores_done"], 1)

            def turn_probs(c, g):
                pe.wait_ge(s["norm_done"], c + 1)
                after(pe, "at_ready", c)
                for t in range(NT):
                    for k in range(NT):
                        mm = nc.tensor.transpose(PA[:, k, t * P:(t + 1) * P], ex[g % 2][:, t, k * P:(k + 1) * P],
                                                 ident[:, :])
                mm.then_inc(s["turned"], 1)

            def out(b, g):
                c = H * b + g
                pe.wait_ge(s["at_ready"], c + 1)
                pe.wait_ge(s["vh_ready"], c + 1)
                if g == 0:
                    after(pe, "out_copied", b)
                for k in range(NT):
                    for j in range(IC):
                        mm = nc.tensor.matmul(PO[j // 2][:, j % 2, :], vh[g % 2][:, k, j * P:(j + 1) * P],
                                              at[g % 2][:, k, :], start=(g == 0 and k == 0 and j % 2 == 0),
                                              stop=(g == H - 1 and k == NT - 1), skip_group_check=True)
                mm.then_inc(s["out_done"], 1)

            def project(b):
                pe.wait_ge(s["out_copied"], b + 1)
                after(pe, "x_stored", b)
                for j in range(IC):
                    mm = nc.tensor.matmul(PX[:, 0:L], wo[:, j, :], oT[:, j, :], start=(j == 0), stop=(j == IC - 1))
                mm.then_inc(s["proj_done"], 1)

            def turn(b):
                pe.wait_ge(s["proj_copied"], b + 1)
                for t in range(NT):
                    mm = nc.tensor.transpose(PX[:, t * P:(t + 1) * P], fo[:, t * P:(t + 1) * P], ident[:, :])
                mm.then_inc(s["proj_turned"], 1)

            def back(b):
                pe.wait_ge(s["applied"], b + 1)
                for t in range(NT):
                    mm = nc.tensor.transpose(PX[:, t * P:(t + 1) * P], ln[:, t, :], ident[:, :])
                mm.then_inc(s["x_turned"], 1)

            def prologue():
                q_or_k(0, 0, 0)
                q_or_k(0, 0, 1)
                v_proj(0, 0)
                scores(0, 0, 0)

            def unit(b, i, has_next, has_prev):
                for g in range(H):
                    c = H * b + g
                    if g + 1 < H:
                        scores(b, i, g + 1)
                    elif has_next:
                        scores(b + 1, 1 - i, 0)
                    turn_probs(c, g)
                    if g > 0:
                        out(b, g - 1)
                    elif has_prev:
                        out(b - 1, H - 1)
                    if has_prev and g == 1:
                        project(b - 1)
                    if has_prev and g == 2:
                        turn(b - 1)
                    if has_prev and g == 4:
                        back(b - 1)
                    if has_next and g == 2:
                        q_or_k(b + 1, 1 - i, 0)
                    if has_next and g == 3:
                        q_or_k(b + 1, 1 - i, 1)
                    if has_next and g == 4:
                        v_proj(b + 1, 1 - i)

            def epilogue():
                out(B - 1, H - 1)
                project(B - 1)
                turn(B - 1)
                back(B - 1)

            drive(pe, prologue, unit, epilogue)

        @block.scalar
        def _(act):
            act.wait_ge(s["loaded"], LOADED)

            def q_or_k(b, i, which):
                if which == 0:
                    act.wait_ge(s["q_done"], b + 1)
                    after(act, "qg_ready", H * (b - 1))
                else:
                    act.wait_ge(s["k_done"], b + 1)
                    after(act, "scores_done", H * (b - 1))
                dst = (qT, kT)[which][i]
                for c in range(IC):
                    ins = nc.scalar.activation(dst[:, c, :], PQ[:, c // 2, c % 2 * L:(c % 2 + 1) * L], ACT.Identity,
                                               bias=bqk[:, which, c:c + 1])
                ins.then_inc(s["q_ready" if which == 0 else "k_ready"], 1)

            def exps(c, g):
                act.wait_ge(s["max_ready"], c + 1)
                after(act, "turned", c - 1)
                after(act, "norm_done", c - 1)
                for t in range(NT):
                    ins = nc.scalar.activation(ex[g % 2][:, t, :], PS[g % 2][:, t, :], ACT.Exp,
                                               bias=nm[g % 2][:, t:t + 1], accum_out=sm[g % 2][:, t:t + 1])
                ins.then_inc(s["exp_done"], 1)

            def copy_probs(c, g):
                act.wait_ge(s["turned"], c + 1)
                after(act, "out_done", c - 1)
                nc.scalar.activation(at[g % 2][:, :, :], PA[:, :, :], ACT.Copy).then_inc(s["at_ready"], 1)

            def copy_out(b):
                act.wait_ge(s["out_done"], H * (b + 1))
                after(act, "proj_done", b)
                for j in range(2):
                    ins = nc.scalar.activation(oT[:, 2 * j:2 * j + 2, :], PO[j][:, :, :], ACT.Copy)
                ins.then_inc(s["out_copied"], 1)

            def copy_proj(b):
                act.wait_ge(s["proj_done"], b + 1)
                after(act, "proj_turned", b)
                nc.scalar.activation(fo[:, :], PX[:, 0:L], ACT.Identity, bias=bo[:, 0:1]
                                     ).then_inc(s["proj_copied"], 1)

            def store(b):
                act.wait_ge(s["x_turned"], b + 1)
                apart(act)
                nc.scalar.activation(XT[:, bass.ds(b * L, L)], PX[:, 0:L], ACT.Copy).then_inc(s["x_stored"], 1)

            def prologue():
                q_or_k(0, 0, 0)
                q_or_k(0, 0, 1)
                exps(0, 0)

            def unit(b, i, has_next, has_prev):
                for g in range(H):
                    c = H * b + g
                    if g + 1 < H or has_next:
                        exps(c + 1, (g + 1) % H)
                    copy_probs(c, g)
                    if has_prev and g == 0:
                        copy_out(b - 1)
                    if has_prev and g == 1:
                        copy_proj(b - 1)
                    if has_prev and g == 4:
                        store(b - 1)
                    if has_next and g == 2:
                        q_or_k(b + 1, 1 - i, 0)
                    if has_next and g == 3:
                        q_or_k(b + 1, 1 - i, 1)

            def epilogue():
                copy_out(B - 1)
                copy_proj(B - 1)
                store(B - 1)

            drive(act, prologue, unit, epilogue)

        @block.vector
        def _(dve):
            dve.wait_ge(s["loaded"], LOADED)

            def v_copy(b, i):
                dve.wait_ge(s["v_done"], b + 1)
                after(dve, "vh_ready", H * (b - 1))
                nc.vector.tensor_tensor(v[i][:, :, :], PQ[:, :, :], bv[:, :].unsqueeze(1).to_broadcast([P, NT, INNER]),
                                        ALU.add).then_inc(s["v_ready"], 1)

            def mix_q(b, i, g):
                c = H * b + g
                if g == 0:
                    dve.wait_ge(s["q_ready"], b + 1)
                after(dve, "scores_done", c - 1)
                for j in range(IC):
                    ins = nc.vector.tensor_scalar(qg[g % 2][:, j, :], qT[i][:, j, :], th1[:, j, g:g + 1], SCALE,
                                                  ALU.mult, ALU.mult)
                ins.then_inc(s["qg_ready"], 1)

            def maxima(c, g):
                dve.wait_ge(s["scores_done"], c + 1)
                after(dve, "exp_done", c - 1)
                nc.vector.tensor_reduce(nm[g % 2][:, :], PS[g % 2][:, :, :], AX_X, ALU.max, negate=True
                                        ).then_inc(s["max_ready"], 1)

            def norms(c, g):
                dve.wait_ge(s["exp_done"], c + 1)
                nc.vector.reciprocal(ri[g % 2][:, :], sm[g % 2][:, :]).then_inc(s["recip_ready"], 1)
                dve.wait_ge(s["recip_ready"], c + 1)
                for t in range(NT):
                    e = ex[g % 2][:, t, :]
                    ins = nc.vector.tensor_scalar(e, e, ri[g % 2][:, t:t + 1], None, ALU.mult)
                ins.then_inc(s["norm_done"], 1)

            def subs(b):
                return R[:, bass.ds(b * NT, NT), :]

            def resid(b):
                dve.wait_ge(s["proj_turned"], b + 1)
                nc.vector.tensor_tensor(subs(b), subs(b), PX[:, 0:L].rearrange("p (j c) -> p j c", j=NT), ALU.add
                                        ).then_inc(s["resid_done"], 1)

            def stats(b):
                dve.wait_ge(s["resid_done"], b + 1)
                bn_norm(dve, nc, subs(b), st, mv, s["bn_done"], s["moments_ready"], s["rstd_ready"], b)

            def apply(b):
                after(dve, "x_turned", b)
                bn_apply(dve, nc, ln, subs(b), mv, rs, s["rstd_ready"], s["applied"], b)

            def prologue():
                mix_q(0, 0, 0)
                mix_q(0, 0, 1)
                v_copy(0, 0)
                maxima(0, 0)
                norms(0, 0)

            def unit(b, i, has_next, has_prev):
                for g in range(H):
                    c = H * b + g
                    if g + 2 < H:
                        mix_q(b, i, g + 2)
                    elif has_next:
                        mix_q(b + 1, 1 - i, g + 2 - H)
                    if g + 1 < H or has_next:
                        maxima(c + 1, (g + 1) % H)
                        norms(c + 1, (g + 1) % H)
                    if has_prev and g == 2:
                        resid(b - 1)
                        stats(b - 1)
                    if has_prev and g == 3:
                        apply(b - 1)
                    if has_next and g == 4:
                        v_copy(b + 1, 1 - i)

            def epilogue():
                resid(B - 1)
                stats(B - 1)
                apply(B - 1)

            drive(dve, prologue, unit, epilogue)


def experts_stage(nc, a, R, XT, ident, out):
    E, INTER, TOP, SHARED = 64, 64, 6, 256
    PAIRS = E * INTER // P
    SC = SHARED // P
    CH = PAIRS + SC
    PIECES = 4
    PIECE = CH * P // PIECES
    FULL, GONE = 3.0e38, -3.0e38
    with ExitStack() as ctx:
        m = Mem(nc, ctx)
        wg = m.sb("x_wg", [P, E])
        w1h = m.sb("x_w1h", [P, CH * P], F32R)
        w3h = m.sb("x_w3h", [P, CH * P], F32R)
        w1l = m.sb("x_w1l", [P, CH * P], F32R)
        w3l = m.sb("x_w3l", [P, CH * P], F32R)
        w2 = m.sb("x_w2", [P, CH, P])
        eye2 = m.sb("eye2", [P, E])
        raw = [m.sb(f"x_raw{i}", [P, PIECE]) for i in range(2)]
        pick = m.sb("x_pick", [P, E, INTER], F32R)
        xb = [m.sb(f"x_xb{i}", [P, TOK]) for i in range(2)]
        xh = [m.sb(f"x_xh{i}", [P, TOK], F32R) for i in range(2)]
        xl = [m.sb(f"x_xl{i}", [P, TOK], F32R) for i in range(2)]
        sc = m.sb("x_sc", [P, SUB, E + 2])
        mr = m.sb("x_mr", [P, SUB, E + 2])
        top = m.sb("x_top", [P, SUB, 8])
        nmx = m.sb("x_nmx", [P, SUB])
        mask = m.sb("x_mask", [P, SUB, E])
        ex = m.sb("x_ex", [P, SUB, E])
        sm = m.sb("x_sm", [P, SUB])
        ri = m.sb("x_ri", [P, SUB])
        cf = m.sb("x_cf", [E, TOK])
        parts = [m.sb(f"x_parts{i}", [P, TOK], F32R) for i in range(2)]
        s1 = [m.sb(f"x_s1{i}", [P, TOK]) for i in range(2)]
        hx = [m.sb(f"x_hx{i}", [P, TOK]) for i in range(2)]
        hh = [m.sb(f"x_hh{i}", [P, TOK]) for i in range(2)]
        ro = m.sb("x_ro", [P, TOK])
        ft = [m.sb(f"x_ft{i}", [P, SUB, P]) for i in range(2)]
        P1 = [m.ps(f"xP1{i}", [P, TOK]) for i in range(2)]
        P3 = [m.ps(f"xP3{i}", [P, TOK]) for i in range(2)]
        PW = [m.ps(f"xPW{i}", [P, TOK]) for i in range(2)]
        PO = m.ps("xPO", [P, TOK])
        PX = m.ps("xPX", [P, TOK])

        names = ("gate_loaded up1_loaded up3_loaded down_loaded consts pick_ready x_copied x_high x_split w_high w_split scores_done gate_chain top_ready "
                 "mask_ready exp_done comb_ready comb_turned comb_copied parts_ready gate_half_done up_half_done up_done silu_done product_done "
                 "hidden_ready down_done sum_copied sum_turned final_ready stored0 stored1").split()
        s = {n: m.sem("x_" + n) for n in names}
        block = ctx.enter_context(nc.Block())

        def after(eng, name, n):
            if not isinstance(n, int) or n > 0:
                eng.wait_ge(s[name], n)

        def drive(eng, prologue, unit, epilogue):
            prologue()
            unit(0, 0, True, False)
            unit(1, 1, True, True)
            with eng.Fori(1, TILES // 2 - 1) as q:
                for i in range(2):
                    unit(2 * q + i, i, True, True)
            unit(TILES - 2, 0, True, True)
            unit(TILES - 1, 1, False, True)
            epilogue()

        @block.sync
        def _(sp):
            sp.dma_start(wg[:, :], a["x_wg"]).then_inc(s["gate_loaded"], 16)
            sp.dma_start(eye2[:, :], a["eye2"]).then_inc(s["gate_loaded"], 16)
            for k in range(PIECES):
                for n in range(2):
                    if k > 0:
                        sp.wait_ge(s["w_split"], 2 * k - 1 + n)
                    sp.dma_start(raw[n][:, :], a[("x_w1", "x_w3")[n]][:, k * PIECE:(k + 1) * PIECE]
                                 ).then_inc(s[("up1_loaded", "up3_loaded")[n]], 16)
            sp.dma_start(w2[:, :, :], a["x_w2"]).then_inc(s["down_loaded"], 16)

            def store(T, i):
                sp.wait_ge(s["final_ready"], T + 1)
                sp.dma_start(out[:, bass.ds(T * SUB, SUB), :], ft[i][:, :, :]).then_inc(s[f"stored{i}"], 16)

            with sp.Fori(0, TILES // 2) as q:
                for i in range(2):
                    store(2 * q + i, i)
            for i in range(2):
                sp.wait_ge(s[f"stored{i}"], 16 * (TILES // 2))

        @block.gpsimd
        def _(pool):
            nc.gpsimd.memset(sc[:, :, E:E + 2], FULL).then_inc(s["consts"], 1)

            def x_copy(T, i):
                after(pool, "up_done", CH * (T - 1))
                apart(pool)
                nc.gpsimd.tensor_copy(xb[i][:, :], XT[:, bass.ds(T * TOK, TOK)]).then_inc(s["x_copied"], 1)

            def x_low(T, i):
                pool.wait_ge(s["x_high"], T + 1)
                nc.gpsimd.tensor_tensor(xl[i][:, :], xb[i][:, :], xh[i][:, :], ALU.subtract).then_inc(s["x_split"], 1)

            for i in range(2):
                x_copy(i, i)
                x_low(i, i)
            with pool.Fori(1, TILES // 2) as q:
                for i in range(2):
                    x_copy(2 * q + i, i)
                    x_low(2 * q + i, i)

        @block.tensor
        def _(pe):
            pe.wait_ge(s["gate_loaded"], 32)

            def gate_scores(T, i):
                pe.wait_ge(s["x_copied"], T + 1)
                after(pe, "final_ready", T - 1)
                for j in range(SUB):
                    mm = nc.tensor.matmul(PX[:, j * E:(j + 1) * E], xb[i][:, j * P:(j + 1) * P], wg[:, :],
                                          start=True, stop=True)
                mm.then_inc(s["scores_done"], 1)

            def gate_turn(T):
                pe.wait_ge(s["comb_ready"], T + 1)
                apart(pe)
                for j in range(SUB):
                    mm = nc.tensor.transpose(PX[0:E, j * P:(j + 1) * P], ex[:, j, :], ident[:, :])
                mm.then_inc(s["comb_turned"], 1)

            def up(T, i, c):
                g = CH * T + c
                last = c - 2 if c >= 2 else CH - 2 + c
                cols = slice(c * P, (c + 1) * P)
                if c == 0:
                    pe.wait_ge(s["x_split"], T + 1)
                    pe.wait_ge(s["parts_ready"], T + 1)
                after(pe, "silu_done", g - 1)
                apart(pe)
                nc.tensor.matmul(P1[c % 2][:, :], w1h[:, cols], xh[i][:, :], start=True, stop=False)
                nc.tensor.matmul(P1[c % 2][:, :], w1l[:, cols], xh[i][:, :], start=False, stop=False)
                nc.tensor.matmul(P1[c % 2][:, :], w1h[:, cols], xl[i][:, :], start=False, stop=True
                                 ).then_inc(s["gate_half_done"], 1)
                if last >= PAIRS:
                    after(pe, "hidden_ready", g - 1)
                else:
                    after(pe, "product_done", (T if c >= 2 else T - 1) * PAIRS + last + 1)
                apart(pe)
                nc.tensor.matmul(P3[c % 2][:, :], w3h[:, cols], xh[i][:, :], start=True, stop=False)
                nc.tensor.matmul(P3[c % 2][:, :], w3l[:, cols], xh[i][:, :], start=False, stop=False)
                mm = nc.tensor.matmul(P3[c % 2][:, :], w3h[:, cols], xl[i][:, :], start=False, stop=True)
                if c < PAIRS:
                    mm.then_inc(s["up_half_done"], 1)
                    pk = pick[:, 2 * c:2 * c + 2, :].rearrange("p e i -> p (e i)")
                    after(pe, "hidden_ready", g - 1)
                    apart(pe)
                    mm = nc.tensor.matmul(PW[c % 2][:, :], pk, parts[i][:, :], start=True, stop=True)
                mm.then_inc(s["up_done"], 1)

            def down(T, c):
                g = CH * T + c
                pe.wait_ge(s["hidden_ready"], g + 1)
                if c == 0:
                    after(pe, "sum_copied", T)
                nc.tensor.matmul(PO[:, :], w2[:, c, :], hh[c % 2][:, :], start=(c == 0), stop=(c == CH - 1)
                                 ).then_inc(s["down_done"], 1)

            def turn(T):
                pe.wait_ge(s["sum_copied"], T + 1)
                for j in range(SUB):
                    mm = nc.tensor.transpose(PX[:, j * P:(j + 1) * P], ro[:, j * P:(j + 1) * P], ident[:, :])
                mm.then_inc(s["sum_turned"], 1)

            def prologue():
                gate_scores(0, 0)
                gate_turn(0)
                pe.wait_ge(s["pick_ready"], 1)
                pe.wait_ge(s["w_split"], 2 * PIECES)
                pe.wait_ge(s["down_loaded"], 16)
                up(0, 0, 0)
                up(0, 0, 1)

            def unit(T, i, has_next, has_prev):
                for c in range(CH):
                    if c + 2 < CH:
                        up(T, i, c + 2)
                    elif has_next:
                        up(T + 1, 1 - i, c + 2 - CH)
                    down(T, c)
                    if has_prev and c == 1:
                        turn(T - 1)
                    if has_next and c == 8:
                        gate_scores(T + 1, 1 - i)
                    if has_next and c == 18:
                        gate_turn(T + 1)

            drive(pe, prologue, unit, lambda: turn(TILES - 1))

        @block.scalar
        def _(act):
            act.wait_ge(s["gate_loaded"], 32)
            nc.scalar.activation(pick[:, :, :], eye2[:, :].unsqueeze(2).to_broadcast([P, E, INTER]), ACT.Copy
                                 ).then_inc(s["pick_ready"], 1)

            def gate_exp(T):
                act.wait_ge(s["top_ready"], T + 1)
                after(act, "comb_turned", T)
                for j in range(SUB):
                    ins = nc.scalar.activation(ex[:, j, :], sc[:, j, 0:E], ACT.Exp, bias=nmx[:, j:j + 1])
                ins.then_inc(s["exp_done"], 1)

            def gate_copy(T, i):
                act.wait_ge(s["comb_turned"], T + 1)
                after(act, "parts_ready", T)
                nc.scalar.activation(cf[:, :], PX[0:E, :], ACT.Copy).then_inc(s["comb_copied"], 1)

            def silu(T, c):
                g = CH * T + c
                act.wait_ge(s["gate_half_done"], g + 1)
                after(act, "hidden_ready", g - 1)
                nc.scalar.activation(s1[c % 2][:, :], P1[c % 2][:, :], ACT.Silu).then_inc(s["silu_done"], 1)

            def copy_sum(T):
                act.wait_ge(s["down_done"], CH * (T + 1))
                after(act, "sum_turned", T)
                nc.scalar.activation(ro[:, :], PO[:, :], ACT.Copy).then_inc(s["sum_copied"], 1)

            def prologue():
                gate_exp(0)
                gate_copy(0, 0)
                silu(0, 0)

            def unit(T, i, has_next, has_prev):
                if has_prev:
                    copy_sum(T - 1)
                for c in range(CH):
                    if c + 1 < CH:
                        silu(T, c + 1)
                    elif has_next:
                        silu(T + 1, 0)
                    if has_next and c == 14:
                        gate_exp(T + 1)
                    if has_next and c == 19:
                        gate_copy(T + 1, 1 - i)

            drive(act, prologue, unit, lambda: copy_sum(TILES - 1))

        @block.vector
        def _(dve):
            dve.wait_ge(s["consts"], 1)
            LINKS = 7

            def gate_top(T):
                dve.wait_ge(s["scores_done"], T + 1)
                after(dve, "exp_done", T)
                nc.vector.tensor_copy(sc[:, :, 0:E], PX[:, 0:SUB * E].rearrange("p (j e) -> p j e", j=SUB)
                                      ).then_inc(s["gate_chain"], 1)
                dve.wait_ge(s["gate_chain"], LINKS * T + 1)
                apart(dve)
                for j in range(SUB):
                    ins = nc.vector.max(top[:, j, :], sc[:, j, 0:E])
                ins.then_inc(s["gate_chain"], 1)
                dve.wait_ge(s["gate_chain"], LINKS * T + 2)
                apart(dve)
                nc.vector.tensor_scalar(nmx[:, :], top[:, :, 0], -1.0, None, ALU.mult).then_inc(s["top_ready"], 1)
                nc.vector.memset(top[:, :, TOP:8], FULL).then_inc(s["gate_chain"], 1)
                dve.wait_ge(s["gate_chain"], LINKS * T + 3)
                apart(dve)
                for j in range(SUB):
                    ins = nc.vector.match_replace(mr[:, j, :], top[:, j, :], sc[:, j, :], GONE)
                ins.then_inc(s["gate_chain"], 1)
                dve.wait_ge(s["gate_chain"], LINKS * T + 4)
                nc.vector.tensor_scalar(mask[:, :, :], mr[:, :, 0:E], GONE, None, ALU.is_equal
                                        ).then_inc(s["mask_ready"], 1)

            def gate_weights(T):
                dve.wait_ge(s["mask_ready"], T + 1)
                dve.wait_ge(s["exp_done"], T + 1)
                for j in range(SUB):
                    ins = nc.vector.scalar_tensor_tensor(out=mask[:, j, :], in0=ex[:, j, :], scalar=1.0,
                                                         in1=mask[:, j, :], op0=ALU.mult, op1=ALU.mult,
                                                         accum_out=sm[:, j:j + 1])
                ins.then_inc(s["gate_chain"], 1)
                dve.wait_ge(s["gate_chain"], LINKS * T + 5)
                nc.vector.reciprocal(ri[:, :], sm[:, :]).then_inc(s["gate_chain"], 1)
                dve.wait_ge(s["gate_chain"], LINKS * T + 6)
                for j in range(SUB):
                    ins = nc.vector.tensor_scalar(ex[:, j, :], mask[:, j, :], ri[:, j:j + 1], None, ALU.mult)
                ins.then_inc(s["comb_ready"], 1)

            def gate_split(T, i):
                dve.wait_ge(s["comb_copied"], T + 1)
                after(dve, "up_done", CH * (T - 1))
                nc.vector.tensor_copy(parts[i][0:E, :], cf[:, :]).then_inc(s["gate_chain"], 1)
                dve.wait_ge(s["gate_chain"], LINKS * T + 7)
                nc.vector.tensor_tensor(parts[i][E:2 * E, :], cf[:, :], parts[i][0:E, :], ALU.subtract
                                        ).then_inc(s["parts_ready"], 1)

            def x_high(T, i):
                dve.wait_ge(s["x_copied"], T + 1)
                nc.vector.tensor_copy(xh[i][:, :], xb[i][:, :]).then_inc(s["x_high"], 1)

            def split_weights():
                for k in range(PIECES):
                    piece = slice(k * PIECE, (k + 1) * PIECE)
                    for n, (name, wh, wl) in enumerate((("up1_loaded", w1h, w1l), ("up3_loaded", w3h, w3l))):
                        dve.wait_ge(s[name], 16 * (k + 1))
                        nc.vector.tensor_copy(wh[:, piece], raw[n][:, :]).then_inc(s["w_high"], 1)
                        dve.wait_ge(s["w_high"], 2 * k + n + 1)
                        nc.vector.tensor_tensor(wl[:, piece], raw[n][:, :], wh[:, piece], ALU.subtract
                                                ).then_inc(s["w_split"], 1)

            def product(T, c):
                g = CH * T + c
                if c < PAIRS:
                    dve.wait_ge(s["up_half_done"], PAIRS * T + c + 1)
                else:
                    dve.wait_ge(s["up_done"], g + 1)
                dve.wait_ge(s["silu_done"], g + 1)
                after(dve, "down_done", g - 1)
                dst = hx if c < PAIRS else hh
                nc.vector.tensor_tensor(dst[c % 2][:, :], s1[c % 2][:, :], P3[c % 2][:, :], ALU.mult
                                        ).then_inc(s["product_done" if c < PAIRS else "hidden_ready"], 1)

            def weigh(T, c):
                g = CH * T + c
                dve.wait_ge(s["product_done"], PAIRS * T + c + 1)
                dve.wait_ge(s["up_done"], g + 1)
                after(dve, "down_done", g - 1)
                nc.vector.tensor_tensor(hh[c % 2][:, :], hx[c % 2][:, :], PW[c % 2][:, :], ALU.mult
                                        ).then_inc(s["hidden_ready"], 1)

            def final(T, i):
                dve.wait_ge(s["sum_turned"], T + 1)
                if T_stored[0] is not None:
                    dve.wait_ge(s[f"stored{i}"], T_stored[0])
                nc.vector.tensor_tensor(ft[i][:, :, :], R[:, bass.ds(T * SUB, SUB), :],
                                        PX[:, :].rearrange("p (j c) -> p j c", j=SUB), ALU.add
                                        ).then_inc(s["final_ready"], 1)

            T_stored = [None]

            def prologue():
                x_high(0, 0)
                gate_top(0)
                gate_weights(0)
                gate_split(0, 0)
                split_weights()

            def unit(T, i, has_next, has_prev):
                for c in range(CH):
                    product(T, c)
                    if c < PAIRS:
                        weigh(T, c)
                    if has_prev and c == 3:
                        final(T - 1, 1 - i)
                    if has_next and c == 5:
                        x_high(T + 1, 1 - i)
                    if has_next and c == 10:
                        gate_top(T + 1)
                    if has_next and c == 16:
                        gate_weights(T + 1)
                    if has_next and c == 21:
                        gate_split(T + 1, 1 - i)

            prologue()
            unit(0, 0, True, False)
            unit(1, 1, True, True)
            unit(2, 0, True, True)
            T_stored[0] = 16
            unit(3, 1, True, True)
            with dve.Fori(2, TILES // 2 - 1) as q:
                T_stored[0] = 16 * (q - 1)
                unit(2 * q, 0, True, True)
                T_stored[0] = 16 * q
                unit(2 * q + 1, 1, True, True)
            T_stored[0] = 16 * (TILES // 2 - 2)
            unit(TILES - 2, 0, True, True)
            T_stored[0] = 16 * (TILES // 2 - 1)
            unit(TILES - 1, 1, False, True)
            final(TILES - 1, 1)


def audio_tower(nc, a, out):
    with ExitStack() as ctx:
        m = Mem(nc, ctx)
        R = m.sb("R", [P, N // P, P])
        XT = m.sb("XT", [P, N])
        ident = m.sb("ident", [P, P])
        tok_stage(nc, a, R, XT, ident)
        mixer_stage(nc, a, R, XT, ident)
        w_dram = nc.dram_tensor("token_weights", (8, N), F32, kind="Internal").ap()
        expert_choice_stage(nc, a, R, XT, ident, w_dram)
        attention_stage(nc, a, R, XT, ident)
        experts_stage(nc, a, R, XT, ident, out)


def lay_out(i):
    import numpy as np
    t = "L0_tok_"
    d = {}
    d["x"] = i["x"]
    d["ident"] = np.eye(P, dtype=np.float32)
    d["ew"] = i[t + "embed_w"].transpose(1, 2, 0)
    d["tok_cols"] = np.stack([i[t + "embed_b"], i[t + "norm0_g"], i[t + "norm0_b"]], 1)
    d["dww"] = i[t + "dw_w"][:, :, 0, :].transpose(2, 0, 1)
    d["lcol"] = np.stack([i[t + k].T for k in ("dw_b", "ln_g", "ln_b", "b2", "gamma")], 1)
    d["tok_b1"] = i[t + "b1"].reshape(8, 3, P).transpose(2, 0, 1)
    d["tok_w1"] = i[t + "w1"].transpose(0, 2, 1)
    d["tok_w2"] = i[t + "w2"].transpose(0, 2, 1).reshape(8, 3, P, P).transpose(0, 2, 1, 3)
    d["fing"] = np.stack([i[t + "final_g"], i[t + "final_b"]])
    def both(name, f):
        return np.stack([f(i["L0_attn_f_" + name]), f(i["L0_attn_b_" + name])], 1)
    halves = lambda v: v.reshape(2, P, -1).transpose(1, 0, 2)
    d["inw"] = both("in_w", lambda w: w.T)
    d["mcol"] = np.concatenate([both(k, halves) for k in ("conv_b", "dt_b", "D")], 3)
    d["m_cw"] = np.stack([i[f"L0_attn_{k}_conv_w"][:, 0, :].reshape(2, P, 4).transpose(0, 2, 1) for k in "fb"])
    d["alog"] = both("A_log", halves)
    d["xpw"] = both("xproj_w", lambda w: halves(np.concatenate([w[8:40], w[0:8]]).T))
    d["dtw"] = both("dt_w", lambda w: w.T)
    d["outw"] = both("out_w", lambda w: w)
    d["fusw"] = i["L0_attn_fusion_w"].reshape(P, 2, P).transpose(2, 1, 0)
    d["fusb"] = i["L0_attn_fusion_b"].reshape(P, 1)
    d["mix_gb"] = np.stack([i["L0_attn_ln_g"], i["L0_attn_ln_b"]])
    d["eye3"] = np.tile(np.eye(32, dtype=np.float32), (3, 1))
    d["wr"] = i["L0_ffn_Wr"]
    d["e_w1"] = i["L0_ffn_W1"].transpose(1, 0, 2)
    d["e_b1"] = i["L0_ffn_b1"].reshape(8, 4, P).transpose(2, 0, 1)
    d["e_w2"] = i["L0_ffn_W2"].reshape(8, 4, P, P).transpose(2, 0, 1, 3)
    d["e_b2"] = i["L0_ffn_b2"].T
    expert, sample = np.arange(P) // B, np.arange(P) % B
    same = expert[:, None] == expert[None, :]
    d["same"] = same.astype(np.float32)
    d["before"] = (same & (sample[:, None] < sample[None, :])).astype(np.float32)
    d["bit"] = (1 << np.arange(29, -1, -1)).astype(np.int32)
    d["wqkv"] = i["L1_attn_w_qkv"]
    bq = i["L1_attn_b_qkv"].reshape(3, 4, P)
    d["bqk"] = bq[0:2].transpose(2, 0, 1)
    d["bv"] = bq[2].reshape(512)
    d["th1"] = np.repeat(i["L1_attn_th1"], 64, 1).reshape(8, 4, P).transpose(2, 1, 0)
    d["th2"] = np.repeat(i["L1_attn_th2"].T, 64, 1)
    d["wo"] = i["L1_attn_w_out"].reshape(4, P, P).transpose(1, 0, 2)
    d["bo"] = i["L1_attn_b_out"].reshape(P, 1)
    d["x_wg"] = i["L1_ffn_w_gate"].T
    up = lambda w, shared: np.concatenate([i[w].reshape(64 * 64, P), i[shared]]).T
    d["x_w1"] = up("L1_ffn_w1", "L1_ffn_w_sg")
    d["x_w3"] = up("L1_ffn_w3", "L1_ffn_w_su")
    d["x_w2"] = np.concatenate([i["L1_ffn_w2"].reshape(32, P, P), i["L1_ffn_w_sd"].T.reshape(2, P, P)]
                               ).transpose(1, 0, 2)
    d["eye2"] = np.tile(np.eye(64, dtype=np.float32), (2, 1))
    return {k: np.ascontiguousarray(v) for k, v in d.items()}


def kernel(**inputs):
    import numpy as np
    import concourse.bacc as bacc
    from concourse.bass_utils import run_bass_kernel_spmd

    nc = bacc.Bacc("TRN2", target_bir_lowering=False, num_devices=1)
    laid = lay_out({k: np.asarray(v) for k, v in inputs.items()})
    arrays, aps = {}, {}
    for name, v in laid.items():
        arrays[f"in_{name}"] = v
        aps[name] = nc.dram_tensor(f"in_{name}", v.shape, mybir.dt.from_np(v.dtype), kind="ExternalInput").ap()
    out = nc.dram_tensor("out_0", (P, N // P, P), F32, kind="ExternalOutput").ap()
    audio_tower(nc, aps, out)
    r = run_bass_kernel_spmd(nc, [arrays], core_ids=[0])
    got = r.results[0]["out_0"]
    return np.ascontiguousarray(got.transpose(1, 0, 2)).reshape(B, L, P)
```

```python
from contextlib import ExitStack

import concourse.bass as bass
from concourse import mybir

F32 = mybir.dt.float32
BF16 = mybir.dt.bfloat16
F32R = mybir.dt.float32r
I32 = mybir.dt.int32
U8 = mybir.dt.uint8
ALU = mybir.AluOpType
ACT = mybir.ActivationFunctionType
AX_X = mybir.AxisListType.X

P = 128
B = 16
L = 256
N = B * L
TOK = 512
TILES = N // TOK
SUB = TOK // P


class Mem:

    def __init__(self, nc, ctx):
        self.nc, self.ctx, self.sems = nc, ctx, []
        ctx.callback(self.clear)

    def sb(self, name, shape, dt=F32):
        return self.ctx.enter_context(self.nc.sbuf_tensor(name, shape, dt))

    def ps(self, name, shape, dt=F32):
        return self.ctx.enter_context(self.nc.psum_tensor(name, shape, dt))

    def sem(self, name):
        self.sems.append(self.nc.alloc_semaphore(name=name))
        return self.sems[-1]

    def clear(self):
        if self.sems:
            self.nc.clear_and_free_semaphores(self.sems)
            self.nc.all_engine_barrier()


def apart(eng):
    eng.nop(nofuse=True)


def tok_stage(nc, a, R, XT, ident):
    TAPS, HALO, LAYERS, CIN = 7, 3, 8, 80
    INTER = 384
    FC = INTER // P
    LP = L + 2 * HALO
    VT = TAPS - 3
    with ExitStack() as ctx:
        m = Mem(nc, ctx)
        xin = m.sb("xin", [CIN, B, LP])
        HP = m.sb("HP", [P, B, LP])
        ew = m.sb("ew", [CIN, TAPS, P])
        cols = m.sb("cols", [P, 3])
        dww = m.sb("dww", [P, LAYERS, TAPS])
        lcol = m.sb("lcol", [P, 5, LAYERS])
        b1 = m.sb("b1", [P, LAYERS, FC])
        gb2 = m.sb("gb2", [P, LAYERS])
        w1 = [m.sb(f"w1_{i}", [P, INTER]) for i in range(2)]
        w2 = [m.sb(f"w2_{i}", [P, FC, P]) for i in range(2)]
        fing = m.sb("fing", [P, 2, P])
        cv = [m.sb(f"cv{i}", [P, TOK]) for i in range(2)]
        wg = m.sb("wg", [P, TAPS])
        last = [m.sb(f"last{i}", [P, TOK]) for i in range(2)]
        prod = [m.sb(f"prod{i}", [P, TOK]) for i in range(2)]
        side = [m.sb(f"side{i}", [P, TOK]) for i in range(2)]
        st = [m.sb(f"st{i}", [P, SUB, 6]) for i in range(2)]
        mv = [m.sb(f"mv{i}", [P, SUB, 2]) for i in range(2)]
        ve = [m.sb(f"ve{i}", [P, SUB]) for i in range(2)]
        rs = [m.sb(f"rs{i}", [P, SUB]) for i in range(2)]
        ln = [m.sb(f"ln{i}", [P, SUB, P]) for i in range(2)]
        y = [m.sb(f"y{i}", [P, TOK]) for i in range(2)]
        g = [m.sb(f"g{i}", [P, FC, TOK]) for i in range(2)]
        yo = [m.sb(f"yo{i}", [P, TOK]) for i in range(2)]
        mhalf = m.sb("mhalf", [P, SUB])
        eps6 = m.sb("eps6", [P, SUB])
        eps5 = m.sb("eps5", [P, SUB])
        PT = [m.ps(f"PT{i}", [P, SUB, P]) for i in range(2)]
        PB = m.ps("PB", [P, TOK])
        PH = m.ps("PH", [P, FC, TOK])
        PO = m.ps("PO", [P, TOK])
        PC = m.ps("PC", [P, TOK])

        s_x = m.sem("x_loaded")
        s_wl = m.sem("weights_loaded")
        s_lw = [m.sem(f"layer_weights_loaded{i}") for i in range(2)]
        s_ms = m.sem("halo_zeroed")
        s_gb = m.sem("gamma_b2_ready")
        s_pc = m.sem("embed_conv_done")
        s_ce = m.sem("embed_evacuated")
        s_ch = m.sem("conv_chain")
        s_cv = m.sem("conv_done")
        s_wg = m.sem("layer_taps_ready")
        s_lt = m.sem("last_tap_ready")
        s_sc = m.sem("side_chain")
        s_sd = m.sem("side_taps_ready")
        s_t1 = m.sem("to_tokens_done")
        s_bn = m.sem("bn_stats_done")
        s_mv = m.sem("moments_ready")
        s_ve = m.sem("var_eps_ready")
        s_rs = m.sem("rstd_ready")
        s_ap = m.sem("norm_applied")
        s_t2 = m.sem("to_channels_done")
        s_y = m.sem("y_ready")
        s_h = m.sem("hidden_done")
        s_g = m.sem("gelu_done")
        s_o = m.sem("mlp_out_done")
        s_yo = m.sem("scaled_out_ready")
        s_rd = m.sem("residual_done")
        s_f = m.sem("final_chain")

        block = ctx.enter_context(nc.Block())

        @block.sync
        def _(sp):
            sp.wait_ge(s_ms, 1)
            sp.dma_start(xin[:, :, HALO:HALO + L], a["x"].rearrange("b c t -> c b t")).then_inc(s_x, 16)
            sp.dma_start(ew[:, :, :], a["ew"]).then_inc(s_x, 16)
            sp.dma_start(cols[:, :], a["tok_cols"]).then_inc(s_x, 16)
            sp.dma_start(ident[:, :], a["ident"]).then_inc(s_x, 16)
            sp.dma_start(dww[:, :, :], a["dww"]).then_inc(s_wl, 16)
            sp.dma_start(lcol[:, :, :], a["lcol"]).then_inc(s_wl, 16)
            sp.dma_start(b1[:, :, :], a["tok_b1"]).then_inc(s_wl, 16)
            sp.dma_start(fing[:, :, :], a["fing"].partition_broadcast(P)).then_inc(s_wl, 16)

            def load(layer, i):
                sp.dma_start(w1[i][:, :], a["tok_w1"][bass.ds(layer, 1), :, :].rearrange("o p f -> (o p) f")
                             ).then_inc(s_lw[i], 16)
                sp.dma_start(w2[i][:, :, :], a["tok_w2"][bass.ds(layer, 1), :, :, :].rearrange("o p c d -> (o p) c d")
                             ).then_inc(s_lw[i], 16)

            load(0, 0)
            load(1, 1)
            with sp.Fori(1, LAYERS // 2) as lp:
                for i in range(2):
                    sp.wait_ge(s_o, (2 * lp + i - 1) * TILES)
                    load(2 * lp + i, i)

        @block.gpsimd
        def _(pool):
            nc.gpsimd.memset(xin[:, :, 0:HALO], 0.0)
            nc.gpsimd.memset(xin[:, :, HALO + L:], 0.0).then_inc(s_ms, 1)
            nc.gpsimd.memset(mhalf[:, :], -0.5)
            nc.gpsimd.memset(eps6[:, :], 1e-6)
            nc.gpsimd.memset(eps5[:, :], 1e-5)
            nc.gpsimd.memset(HP[:, :, 0:HALO], 0.0)
            nc.gpsimd.memset(HP[:, :, HALO + L:], 0.0).then_inc(s_ms, 1)
            pool.wait_ge(s_ms, 2)

            def rstd(i, eps, k):
                pool.wait_ge(s_mv, k + 1)
                if not isinstance(k, int) or k >= 2:
                    pool.wait_ge(s_ap, k - 1)
                nc.gpsimd.tensor_tensor(ve[i][:, :], mv[i][:, :, 1], eps[:, :], ALU.add).then_inc(s_ve, 1)
                pool.wait_ge(s_ve, k + 1)
                nc.gpsimd.tensor_tensor(rs[i][:, :], ve[i][:, :], mhalf[:, :], ALU.pow).then_inc(s_rs, 1)

            def side_taps(V, t):
                if t == 0:
                    pool.wait_ge(s_wg, V // TILES + 1 if isinstance(V, int) else layer_count[0])
                pool.wait_ge(s_lt, V + 1)
                if not isinstance(V, int) or V >= 2:
                    pool.wait_ge(s_cv, V - 1)
                apart(pool)
                tmp = lambda x: x[:, :].rearrange("p (b t) -> p b t", b=2)
                for n in range(2):
                    k = VT + n
                    ins = nc.gpsimd.tensor_scalar(tmp(prod[n]), HP[:, 2 * t:2 * t + 2, k:k + L], wg[:, k:k + 1], 0.0,
                                                  ALU.mult, ALU.add)
                ins.then_inc(s_sc, 1)
                pool.wait_ge(s_sc, 2 * V + 1)
                apart(pool)
                nc.gpsimd.tensor_tensor(prod[0][:, :], prod[0][:, :], prod[1][:, :], ALU.add).then_inc(s_sc, 1)
                pool.wait_ge(s_sc, 2 * V + 2)
                apart(pool)
                nc.gpsimd.tensor_tensor(side[t % 2][:, :], prod[0][:, :], last[t % 2][:, :], ALU.add
                                        ).then_inc(s_sd, 1)

            for U in range(TILES - 1):
                rstd(U % 2, eps6, U)
            side_taps(0, 0)
            layer_count = [0]

            def layer(l, final):
                for t in range(TILES):
                    layer_count[0] = l + 2
                    V = l * TILES + t
                    rstd((t + 1) % 2, eps6, V + TILES - 1)
                    if t + 1 < TILES or not final:
                        side_taps(V + 1, (t + 1) % TILES)

            layer(0, False)
            with pool.Fori(1, LAYERS - 1) as l:
                layer(l, False)
            layer(LAYERS - 1, True)
            rstd(1, eps6, (LAYERS + 1) * TILES - 1)
            base = (LAYERS + 1) * TILES
            for t in range(TILES):
                rstd(0, eps6, base + 2 * t)
                rstd(1, eps5, base + 2 * t + 1)

        @block.tensor
        def _(pe):
            pe.wait_ge(s_x, 64)
            pe.wait_ge(s_ms, 2)

            def embed(t):
                if t >= 1:
                    pe.wait_ge(s_ce, t)
                for k in range(TAPS):
                    mm = nc.tensor.matmul(PC[:, :].rearrange("p (b t) -> p b t", b=2), ew[:, k, :],
                                          xin[:, 2 * t:2 * t + 2, k:k + L], start=(k == 0), stop=(k == TAPS - 1))
                mm.then_inc(s_pc, 1)

            def t1(U, t, kind):
                if kind == "embed":
                    pe.wait_ge(s_ce, t + 1)
                else:
                    pe.wait_ge(s_cv, U - TILES + 1)
                if not isinstance(U, int) or U >= 2:
                    pe.wait_ge(s_ap, U - 1)
                for j in range(SUB):
                    mm = nc.tensor.transpose(PT[t % 2][:, j, :], cv[t % 2][:, j * P:(j + 1) * P], ident[:, :])
                mm.then_inc(s_t1, 1)

            def t2(U, t):
                pe.wait_ge(s_ap, U + 1)
                if not isinstance(U, int) or U >= 1:
                    pe.wait_ge(s_y, U)
                for j in range(SUB):
                    mm = nc.tensor.transpose(PB[:, j * P:(j + 1) * P], ln[t % 2][:, j, :], ident[:, :])
                mm.then_inc(s_t2, 1)

            def hid(V, t, wi):
                pe.wait_ge(s_y, V + TILES + 1)
                if not isinstance(V, int) or V >= 1:
                    pe.wait_ge(s_g, FC * V)
                for f in range(FC):
                    mm = nc.tensor.matmul(PH[:, f, :], w1[wi][:, f * P:(f + 1) * P], y[t % 2][:, :],
                                          start=True, stop=True)
                mm.then_inc(s_h, 1)

            def out(V, t, wi):
                if not isinstance(V, int) or V >= 1:
                    pe.wait_ge(s_yo, V)
                for f in range(FC):
                    pe.wait_ge(s_g, FC * V + f + 1)
                    mm = nc.tensor.matmul(PO[:, :], w2[wi][:, f, :], g[t % 2][:, f, :],
                                          start=(f == 0), stop=(f == FC - 1))
                mm.then_inc(s_o, 1)

            embed(0)
            for t in range(TILES):
                t1(t, t, "embed")
                if t + 1 < TILES:
                    embed(t + 1)
                if t >= 1:
                    t2(t - 1, t - 1)

            def layer(l, par, first):
                V0 = l * TILES
                if isinstance(l, int):
                    pe.wait_ge(s_lw[par], 32 * (l // 2 + 1))
                for t in range(TILES):
                    t1(V0 + TILES + t, t, "layer")
                    t2(V0 + TILES + t - 1, (t - 1) % TILES)
                    if t >= 2:
                        out(V0 + t - 2, t, par)
                    elif not first:
                        out(V0 + t - 2, t, 1 - par)
                    if t >= 1:
                        hid(V0 + t - 1, t - 1, par)
                    elif not first:
                        hid(V0 - 1, TILES - 1, 1 - par)

            layer(0, 0, True)
            layer(1, 1, False)
            with pe.Fori(1, LAYERS // 2) as lp:
                for par in range(2):
                    pe.wait_ge(s_lw[par], 32 * (lp + 1))
                    layer(2 * lp + par, par, False)
            V1 = LAYERS * TILES
            t2(V1 + TILES - 1, TILES - 1)
            out(V1 - 2, TILES - 2, 1)
            hid(V1 - 1, TILES - 1, 1)
            out(V1 - 1, TILES - 1, 1)
            base = V1 + TILES
            def final_turn(t):
                pe.wait_ge(s_rd, V1 - TILES + t + 1)
                if t >= 2:
                    pe.wait_ge(s_ap, base + 2 * (t - 2) + 1)
                for j in range(SUB):
                    b, h = 2 * t + j // 2, j % 2
                    mm = nc.tensor.transpose(PT[t % 2][:, j, :], HP[:, b, HALO + h * P:HALO + (h + 1) * P],
                                             ident[:, :])
                mm.then_inc(s_t1, 1)

            final_turn(0)
            for t in range(TILES):
                if t + 1 < TILES:
                    final_turn(t + 1)
                pe.wait_ge(s_ap, base + 2 * t + 2)
                pe.wait_ge(s_y, base + t)
                for j in range(SUB):
                    mm = nc.tensor.transpose(PB[:, j * P:(j + 1) * P], ln[1][:, j, :], ident[:, :])
                mm.then_inc(s_t2, 1)

        @block.scalar
        def _(act):
            act.wait_ge(s_x, 64)

            def evac_embed(t):
                act.wait_ge(s_pc, t + 1)
                if t >= 2:
                    act.wait_ge(s_t1, t - 1)
                nc.scalar.activation(cv[t % 2][:, :], PC[:, :], ACT.Identity, bias=cols[:, 0:1]).then_inc(s_ce, 1)

            def evac_y(U, t, l, embed):
                act.wait_ge(s_t2, U + 1)
                if embed:
                    nc.scalar.activation(HP[:, 2 * t:2 * t + 2, HALO:HALO + L],
                                         PB[:, :].rearrange("p (b t) -> p b t", b=2), ACT.Identity,
                                         bias=cols[:, 2:3], scale=cols[:, 1:2]).then_inc(s_y, 1)
                else:
                    if not isinstance(U, int) or U >= TILES + 2:
                        act.wait_ge(s_h, U - TILES - 1)
                    apart(act)
                    nc.scalar.activation(y[t % 2][:, :], PB[:, :], ACT.Identity,
                                         bias=lcol[:, 2, bass.ds(l, 1)],
                                         scale=lcol[:, 1, bass.ds(l, 1)]).then_inc(s_y, 1)

            def scale_out(V, t, l):
                act.wait_ge(s_o, V + 1)
                if not isinstance(V, int) or V >= 2:
                    act.wait_ge(s_rd, V - 1)
                apart(act)
                nc.scalar.activation(yo[t % 2][:, :], PO[:, :], ACT.Identity, bias=gb2[:, bass.ds(l, 1)],
                                     scale=lcol[:, 4, bass.ds(l, 1)]).then_inc(s_yo, 1)

            def gelu(V, t, l):
                act.wait_ge(s_h, V + 1)
                if not isinstance(V, int) or V >= 2:
                    act.wait_ge(s_o, V - 1)
                apart(act)
                for f in range(FC):
                    nc.scalar.activation(g[t % 2][:, f, :], PH[:, f, :], ACT.Gelu,
                                         bias=b1[:, bass.ds(l, 1), f]).then_inc(s_g, 1)

            evac_embed(0)
            for t in range(TILES):
                if t + 1 < TILES:
                    evac_embed(t + 1)
                if t >= 1:
                    evac_y(t - 1, t - 1, 0, True)
            act.wait_ge(s_wl, 64)
            act.wait_ge(s_gb, 1)

            def layer_taps(l, V):
                if not isinstance(V, int) or V > 0:
                    act.wait_ge(s_sd, V)
                apart(act)
                nc.scalar.activation(wg[:, :], dww[:, bass.ds(l, 1), :].rearrange("p o k -> p (o k)"), ACT.Copy
                                     ).then_inc(s_wg, 1)

            def last_tap(V, t, l):
                if isinstance(V, int) and V < TILES:
                    act.wait_ge(s_y, t + 1)
                else:
                    act.wait_ge(s_rd, V - TILES + 1)
                if not isinstance(V, int) or V >= 2:
                    act.wait_ge(s_sd, V - 1)
                apart(act)
                nc.scalar.activation(last[t % 2][:, :].rearrange("p (b t) -> p b t", b=2),
                                     HP[:, 2 * t:2 * t + 2, TAPS - 1:TAPS - 1 + L], ACT.Identity,
                                     bias=lcol[:, 0, bass.ds(l, 1)], scale=dww[:, bass.ds(l, 1), TAPS - 1]
                                     ).then_inc(s_lt, 1)

            layer_taps(0, 0)
            last_tap(0, 0, 0)
            last_tap(1, 1, 0)

            def layer(l, first, final=False):
                V0 = l * TILES
                for t in range(TILES):
                    if t + 1 == TILES and not final:
                        layer_taps(l + 1, V0 + TILES)
                    if t + 2 < TILES:
                        last_tap(V0 + t + 2, t + 2, l)
                    elif not final:
                        last_tap(V0 + t + 2, t + 2 - TILES, l + 1)
                    if t == 0:
                        evac_y(V0 + TILES - 1, TILES - 1, 0 if first else l - 1, first)
                        if not first:
                            scale_out(V0 - 2, TILES - 2, l - 1)
                            gelu(V0 - 1, TILES - 1, l - 1)
                    else:
                        evac_y(V0 + TILES + t - 1, t - 1, l, False)
                        if t >= 2:
                            scale_out(V0 + t - 2, t - 2, l)
                        elif not first:
                            scale_out(V0 - 1, TILES - 1, l - 1)
                        gelu(V0 + t - 1, t - 1, l)

            layer(0, True)
            with act.Fori(1, LAYERS - 1) as l:
                layer(l, False)
            layer(LAYERS - 1, False, True)
            V1 = LAYERS * TILES
            evac_y(V1 + TILES - 1, TILES - 1, LAYERS - 1, False)
            scale_out(V1 - 2, TILES - 2, LAYERS - 1)
            gelu(V1 - 1, TILES - 1, LAYERS - 1)
            scale_out(V1 - 1, TILES - 1, LAYERS - 1)
            for t in range(TILES):
                act.wait_ge(s_t2, V1 + TILES + t + 1)
                nc.scalar.activation(XT[:, t * TOK:(t + 1) * TOK], PB[:, :], ACT.Copy).then_inc(s_y, 1)

        @block.vector
        def _(dve):
            def stats(U, i, src, k):
                for j in range(SUB):
                    ins = nc.vector.bn_stats(st[i][:, j, :], src[:, j, :])
                ins.then_inc(s_bn, 1)
                dve.wait_ge(s_bn, k + 1)
                if not isinstance(k, int) or k >= 2:
                    dve.wait_ge(s_rs, k - 1)
                apart(dve)
                for j in range(SUB):
                    ins = nc.vector.bn_aggr(mv[i][:, j, :], st[i][:, j, :])
                ins.then_inc(s_mv, 1)

            def apply(i, src, k):
                dve.wait_ge(s_rs, k + 1)
                for j in range(SUB):
                    ins = nc.vector.tensor_scalar(ln[i][:, j, :], src[:, j, :], mv[i][:, j, 0:1],
                                                  rs[i][:, j:j + 1], ALU.subtract, ALU.mult)
                ins.then_inc(s_ap, 1)

            def stats_of(U, t):
                dve.wait_ge(s_t1, U + 1)
                stats(U, t % 2, PT[t % 2], U)

            def apply_of(U, t):
                if not isinstance(U, int) or U >= 2:
                    dve.wait_ge(s_t2, U - 1)
                apply(t % 2, PT[t % 2], U)

            def conv(V, t, l, first):
                if first:
                    dve.wait_ge(s_y, t + 1)
                else:
                    dve.wait_ge(s_rd, V - TILES + 1)
                dve.wait_ge(s_t1, V + TILES - 1)
                acc = cv[t % 2][:, :].rearrange("p (b t) -> p b t", b=2)
                dve.wait_ge(s_sd, V + 1)
                for k in range(VT):
                    src = HP[:, 2 * t:2 * t + 2, k:k + L]
                    if k > 0:
                        dve.wait_ge(s_ch, (VT - 1) * V + k)
                    more = acc if k > 0 else side[t % 2][:, :].rearrange("p (b t) -> p b t", b=2)
                    ins = nc.vector.scalar_tensor_tensor(out=acc, in0=src, scalar=dww[:, bass.ds(l, 1), k],
                                                         in1=more, op0=ALU.mult, op1=ALU.add)
                    ins.then_inc(s_ch if k < VT - 1 else s_cv, 1)

            def resid(V, t):
                dve.wait_ge(s_yo, V + 1)
                h = HP[:, 2 * t:2 * t + 2, HALO:HALO + L]
                nc.vector.tensor_tensor(h, h, yo[t % 2][:, :].rearrange("p (b t) -> p b t", b=2),
                                        ALU.add).then_inc(s_rd, 1)

            dve.wait_ge(s_wl, 64)
            nc.vector.tensor_tensor(gb2[:, :], lcol[:, 3, :], lcol[:, 4, :], ALU.mult).then_inc(s_gb, 1)
            for t in range(TILES):
                stats_of(t, t)
                if t >= 1:
                    apply_of(t - 1, t - 1)
            dve.wait_ge(s_ms, 2)

            def layer(l, first):
                V0 = l * TILES
                for t in range(TILES):
                    if t >= 1:
                        stats_of(V0 + TILES + t - 1, t - 1)
                    elif not first:
                        stats_of(V0 + TILES - 1, TILES - 1)
                    if t == 0 and first:
                        apply_of(TILES - 1, TILES - 1)
                        conv(V0, 0, l, True)
                    else:
                        conv(V0 + t, t, l, first)
                        apply_of(V0 + TILES + t - 1, (t - 1) % TILES)
                    if t >= 3 or not first:
                        resid(V0 + t - 3, (t - 3) % TILES)

            layer(0, True)
            with dve.Fori(1, LAYERS) as l:
                layer(l, False)
            V1 = LAYERS * TILES
            stats_of(V1 + TILES - 1, TILES - 1)
            apply_of(V1 + TILES - 1, TILES - 1)
            for t in range(TILES - 3, TILES):
                resid(V1 - TILES + t, t)
            base = V1 + TILES
            G = fing[:, 0:1, :].to_broadcast([P, SUB, P])
            Bf = fing[:, 1:2, :].to_broadcast([P, SUB, P])

            def second_apply(t):
                dve.wait_ge(s_t2, base + t)
                apply(1, R[:, SUB * t:SUB * (t + 1), :], base + 2 * t + 1)

            for t in range(TILES):
                dve.wait_ge(s_t1, base + t + 1)
                stats(0, 0, PT[t % 2], base + 2 * t)
                if t == 0:
                    dve.wait_ge(s_t2, base)
                else:
                    second_apply(t - 1)
                apply(0, PT[t % 2], base + 2 * t)
                dve.wait_ge(s_ap, base + 2 * t + 1)
                r = R[:, SUB * t:SUB * (t + 1), :]
                nc.vector.tensor_tensor(r, ln[0][:, :, :], G, ALU.mult).then_inc(s_f, 1)
                dve.wait_ge(s_f, 2 * t + 1)
                nc.vector.tensor_tensor(r, r, Bf, ALU.add).then_inc(s_f, 1)
                dve.wait_ge(s_f, 2 * t + 2)
                stats(0, 1, r, base + 2 * t + 1)
            second_apply(TILES - 1)


def bn_norm(dve, nc, src, st, mv, bn_done, moments_ready, rstd_used, k):
    apart(dve)
    for j in range(src.shape[1]):
        ins = nc.vector.bn_stats(st[:, j, :], src[:, j, :])
    ins.then_inc(bn_done, 1)
    dve.wait_ge(bn_done, k + 1)
    if not isinstance(k, int) or k >= 2:
        dve.wait_ge(rstd_used, k - 1)
    apart(dve)
    for j in range(src.shape[1]):
        ins = nc.vector.bn_aggr(mv[:, j, :], st[:, j, :])
    ins.then_inc(moments_ready, 1)


def pool_rstd(pool, nc, mv, ve, rs, eps, mhalf, moments_ready, var_eps_ready, rstd_ready, applied, k):
    pool.wait_ge(moments_ready, k + 1)
    if not isinstance(k, int) or k >= 2:
        pool.wait_ge(applied, k - 1)
    nc.gpsimd.tensor_tensor(ve[:, :], mv[:, :, 1], eps[:, :], ALU.add).then_inc(var_eps_ready, 1)
    pool.wait_ge(var_eps_ready, k + 1)
    nc.gpsimd.tensor_tensor(rs[:, :], ve[:, :], mhalf[:, :], ALU.pow).then_inc(rstd_ready, 1)


def bn_apply(dve, nc, out, src, mv, rs, rstd_ready, applied, k):
    dve.wait_ge(rstd_ready, k + 1)
    for j in range(src.shape[1]):
        ins = nc.vector.tensor_scalar(out[:, j, :], src[:, j, :], mv[:, j, 0:1], rs[:, j:j + 1],
                                      ALU.subtract, ALU.mult)
    ins.then_inc(applied, 1)


def mixer_stage(nc, a, R, XT, ident):
    S, CH, K, RANK = 16, 2, 4, 8
    BC = 2 * S
    XR = BC + RANK
    STEPS = S * CH
    NDA, NHC = 4, 4
    SMALL = 1.0 / 64
    with ExitStack() as ctx:
        m = Mem(nc, ctx)
        inw = m.sb("inw", [P, 2, 4 * P])
        mcol = m.sb("mcol", [P, 2, CH, 3])
        cw = m.sb("m_cw", [P, 2, CH, K, P])
        alog = m.sb("alog", [P, 2, CH, S])
        negA = m.sb("negA", [P, 2, CH, S])
        xpw = m.sb("xpw", [P, 2, CH, XR])
        dtw = m.sb("dtw", [XR, 2, CH * P])
        outw = m.sb("outw", [P, 2, CH * P])
        fusw = m.sb("fusw", [P, 2, P])
        fusb = m.sb("fusb", [P, 1])
        gb = m.sb("mix_gb", [P, 2, P])
        eye3 = m.sb("eye3", [3 * BC, BC])
        pick = m.sb("pick", [3 * BC, BC, P], BF16)
        Wc = m.sb("Wc", [P, 2, CH, P])
        xs = [m.sb(f"xs{d}", [P, CH, TOK]) for d in range(2)]
        zs = [m.sb(f"zs{d}", [P, CH, TOK]) for d in range(2)]
        x40 = m.sb("x40", [XR, TOK])
        rem = m.sb("rem", [BC, TOK])
        mid = m.sb("mid", [BC, TOK], BF16)
        rows = [m.sb(f"rows{d}", [3 * BC, TOK], BF16) for d in range(2)]
        rv = m.sb("rv", [P, CH, TOK])
        eu = m.sb("eu", [P, CH, TOK])
        lw = m.sb("lw", [P, CH, TOK])
        pp = m.sb("pp", [P, CH, TOK])
        small = m.sb("small", [P, CH, TOK], U8)
        dl = [m.sb(f"dl{d}", [P, CH, TOK]) for d in range(2)]
        du = [m.sb(f"du{d}", [P, CH, TOK]) for d in range(2)]
        dA = [[m.sb(f"dA{d}_{i}", [P, TOK]) for i in range(NDA)] for d in range(2)]
        dbx = [m.sb(f"dbx{i}", [P, TOK]) for i in range(2)]
        hs = [m.sb(f"hs{i}", [P, TOK]) for i in range(2)]
        hc = [m.sb(f"hc{i}", [P, TOK]) for i in range(NHC)]
        yv = m.sb("yv", [P, CH, TOK])
        yb = [m.sb(f"yb{d}", [P, CH, TOK]) for d in range(2)]
        oT = m.sb("oT", [P, TOK])
        rT = m.sb("rT", [P, TOK])
        st = [m.sb(f"mst{i}", [P, SUB, 6]) for i in range(2)]
        mv = [m.sb(f"mmv{i}", [P, SUB, 2]) for i in range(2)]
        ve = [m.sb(f"mve{i}", [P, SUB]) for i in range(2)]
        rs = [m.sb(f"mrs{i}", [P, SUB]) for i in range(2)]
        ln = [m.sb(f"mln{i}", [P, SUB, P]) for i in range(2)]
        eps = m.sb("meps", [P, SUB])
        mhalf = m.sb("mmhalf", [P, SUB])
        Bb = [m.ps(f"Bb{i}", [P, TOK]) for i in range(2)]
        Cb = [m.ps(f"Cb{i}", [P, TOK]) for i in range(2)]
        PY = [m.ps(f"PY{i}", [P, TOK]) for i in range(CH)]
        PI = [m.ps(f"PI{i}", [P, TOK]) for i in range(2)]

        names = ("weights_loaded zeroed exp_alog negA_ready pick_ready wc_done wc_ready taps_ready z_done "
                 "conv_done silu_done zs_ready xproj_done x40_ready hi_ready split_chain rows_ready dt_done "
                 "exp_u softplus_in poly_chain mask_done log1p_done delta_ready du_ready "
                 "bcast_done dA_ready dbx_ready state_ready hc_ready y_step post_done yb_ready "
                 "out_done out_copied sum_ready sum_turned bn_done moments_ready var_eps_ready rstd_ready applied "
                 "gain_chain x_turned x_stored ln_a").split()
        s = {n: m.sem("m_" + n) for n in names}

        block = ctx.enter_context(nc.Block())

        TAIL = {"out": 4, "copy": 9, "sum": 8, "turn": 8, "stats1": 9, "apply1": 10, "stats2": 12, "apply2": 14,
                "back": 2, "store": 6}
        PREP = {"conv0": 6, "conv1": 10, "silu": 16, "xproj": 14, "x40": 19, "split": 16, "dt": 16,
                "softplus": 21, "log": 23, "z": 20, "zs": 28, "blend": 26}

        def prep(name, d):
            return PREP[name] + (2 if d == 0 else 0)

        def drive(eng, prologue, unit, epilogue):
            prologue()
            for T in range(2):
                unit(T, 0, True, T > 0)
                unit(T, 1, True, T > 0)
            with eng.Fori(2, TILES - 1) as T:
                unit(T, 0, True, True)
                unit(T, 1, True, True)
            unit(TILES - 1, 0, True, True)
            unit(TILES - 1, 1, False, True)
            epilogue()

        def tile_cols(T):
            return bass.ds(T * TOK, TOK)

        def tile_subs(T):
            return bass.ds(T * SUB, SUB)

        @block.sync
        def _(sp):
            for dst, src in ((inw[:, :, :], a["inw"]), (mcol[:, :, :, :], a["mcol"]), (alog[:, :, :, :], a["alog"]),
                             (xpw[:, :, :, :], a["xpw"]), (outw[:, :, :], a["outw"]), (fusw[:, :, :], a["fusw"]),
                             (fusb[:, :], a["fusb"]), (gb[:, :, :], a["mix_gb"].partition_broadcast(P)),
                             (eye3[:, :], a["eye3"]),
                             (cw[:, :, :, :, :], a["m_cw"].partition_broadcast(P))):
                sp.dma_start(dst, src).then_inc(s["weights_loaded"], 16)
            sp.wait_ge(s["zeroed"], 1)
            sp.dma_start(dtw[BC:XR, :, :], a["dtw"]).then_inc(s["weights_loaded"], 16)

        WL = 176

        @block.gpsimd
        def _(pool):
            nc.gpsimd.memset(dtw[:, :, :], 0.0).then_inc(s["zeroed"], 1)
            for i in range(NDA):
                nc.gpsimd.memset(dA[0][i][:, 0:TOK:L], 0.0)
                nc.gpsimd.memset(dA[1][i][:, L - 1:TOK:L], 0.0)
            nc.gpsimd.memset(eps[:, :], 1e-5)
            nc.gpsimd.memset(mhalf[:, :], -0.5).then_inc(s["zeroed"], 1)
            pool.wait_ge(s["zeroed"], 2)
            pool.wait_ge(s["weights_loaded"], WL)

            for d in range(2):
                x_half = inw[:, d, 0:CH * P].rearrange("p (c e) -> p c e", c=CH)
                for k in range(K):
                    ins = nc.gpsimd.tensor_tensor(cw[:, d, :, k, :], cw[:, d, :, k, :], x_half, ALU.mult)
            ins.then_inc(s["taps_ready"], 1)

            def poly(v):
                pool.wait_ge(s["exp_u"], v + 1)
                if not isinstance(v, int) or v >= 1:
                    pool.wait_ge(s["log1p_done"], v)
                apart(pool)
                n = 0
                for i, (x, f, add) in enumerate(((eu, -0.25, 1.0 / 3), (pp, 1.0, -0.5), (pp, 1.0, 1.0))):
                    nc.gpsimd.tensor_scalar(pp[:, :, :], x[:, :, :], f, add, ALU.mult, ALU.add
                                            ).then_inc(s["poly_chain"], 1)
                    n += 1
                    pool.wait_ge(s["poly_chain"], 6 * v + n)
                    apart(pool)
                    nc.gpsimd.tensor_tensor(pp[:, :, :], pp[:, :, :], eu[:, :, :], ALU.mult
                                            ).then_inc(s["poly_chain"], 1)
                    n += 1
                    if i < 2:
                        pool.wait_ge(s["poly_chain"], 6 * v + n)
                        apart(pool)

            def delta(v, d):
                pool.wait_ge(s["log1p_done"], v + 1)
                if not isinstance(v, int) or v >= 2:
                    pool.wait_ge(s["dA_ready"], STEPS * (v - 1))
                    pool.wait_ge(s["dbx_ready"], STEPS * (v - 1))
                nc.gpsimd.tensor_tensor(dl[d][:, :, :], rv[:, :, :], lw[:, :, :], ALU.add
                                        ).then_inc(s["delta_ready"], 1)
                pool.wait_ge(s["delta_ready"], v + 1)
                nc.gpsimd.tensor_tensor(du[d][:, :, :], dl[d][:, :, :], xs[d][:, :, :], ALU.mult
                                        ).then_inc(s["du_ready"], 1)

            def root(T, i):
                pool_rstd(pool, nc, mv[i], ve[i], rs[i], eps, mhalf, s["moments_ready"], s["var_eps_ready"],
                          s["rstd_ready"], s["applied"], 2 * T + i)

            def gate(T, d):
                pool.wait_ge(s["post_done"], 2 * T + d + 1)
                if not isinstance(T, int) or T >= 1:
                    pool.wait_ge(s["out_done"], T)
                nc.gpsimd.tensor_tensor(yb[d][:, :, :], yv[:, :, :], zs[d][:, :, :], ALU.mult
                                        ).then_inc(s["yb_ready"], 1)

            def delta_of(v, d):
                poly(v)
                delta(v, d)

            def unit(T, d, has_next, has_prev):
                if has_prev and d == 0:
                    root(T - 1, 0)
                    root(T - 1, 1)
                if has_next:
                    delta_of(2 * T + d + 1, 1 - d)
                gate(T, d)

            def epilogue():
                root(TILES - 1, 0)
                root(TILES - 1, 1)

            drive(pool, lambda: delta_of(0, 0), unit, epilogue)

        @block.tensor
        def _(pe):
            pe.wait_ge(s["weights_loaded"], WL)
            for d in range(2):
                for c in range(CH):
                    mm = nc.tensor.matmul(PI[0][:, (d * CH + c) * P:(d * CH + c + 1) * P],
                                          outw[:, d, c * P:(c + 1) * P], fusw[:, d, :], start=True, stop=True)
            mm.then_inc(s["wc_done"], 1)

            def conv(v, d, c, T, free, half):
                if free is None and half == 0:
                    pe.wait_ge(s["taps_ready"], 1)
                    pe.wait_ge(s["wc_ready"], 1)
                for name, value in free or ():
                    if half == 0:
                        pe.wait_ge(s[name], value)
                out = PI[c][:, :].rearrange("p (b t) -> p b t", b=2)
                x = XT[:, tile_cols(T)].rearrange("p (b t) -> p b t", b=2)
                for n in (2 * half, 2 * half + 1):
                    k = K - 1 - n
                    near, far = slice(n, L), slice(0, L - n)
                    mm = nc.tensor.matmul(out[:, :, near if d == 0 else far], cw[:, d, c, k, :],
                                          x[:, :, far if d == 0 else near], start=(n == 0), stop=(k == 0),
                                          skip_group_check=True)
                if half == 1:
                    mm.then_inc(s["conv_done"], 1)

            def z(v, d, T):
                pe.wait_ge(s["softplus_in"], v + 1)
                for c in range(CH):
                    mm = nc.tensor.matmul(PI[c][:, :], inw[:, d, (CH + c) * P:(CH + c + 1) * P],
                                          XT[:, tile_cols(T)], start=True, stop=True)
                mm.then_inc(s["z_done"], 1)

            def xproj(v, d):
                pe.wait_ge(s["silu_done"], v + 1)
                for c in range(CH):
                    mm = nc.tensor.matmul(PI[0][0:XR, :], xpw[:, d, c, :], xs[d][:, c, :],
                                          start=(c == 0), stop=(c == CH - 1))
                mm.then_inc(s["xproj_done"], 1)

            def dt(v, d):
                pe.wait_ge(s["hi_ready"], v + 1)
                for c in range(CH):
                    mm = nc.tensor.matmul(PI[c][:, :], dtw[:, d, c * P:(c + 1) * P], x40[:, :],
                                          start=True, stop=True)
                mm.then_inc(s["dt_done"], 1)

            def bcast(u, d, n):
                if n == 0:
                    pe.wait_ge(s["rows_ready"], u + 1)
                if not isinstance(u, int) or STEPS * u + 2 * n - 2 > 0:
                    pe.wait_ge(s["dbx_ready"], STEPS * u + 2 * n - 2)
                    pe.wait_ge(s["hc_ready"], STEPS * u + 2 * n - 2)
                nc.tensor.matmul(Bb[n % 2][:, :], pick[:, n, :], rows[d][:, :], start=True, stop=True)
                nc.tensor.matmul(Cb[n % 2][:, :], pick[:, S + n, :], rows[d][:, :], start=True, stop=True
                                 ).then_inc(s["bcast_done"], 1)

            def ysum(u, n, c):
                pe.wait_ge(s["hc_ready"], STEPS * u + 2 * n + c + 1)
                if n == 0 and (not isinstance(u, int) or u >= 1):
                    pe.wait_ge(s["post_done"], u)
                nc.tensor.matmul(PY[c][:, :], ident[:, :], hc[(2 * n + c) % NHC][:, :], start=(n == 0), stop=(n == S - 1)
                                 ).then_inc(s["y_step"], 1)

            def tail_out(T, last, d):
                if d == 0:
                    pe.wait_ge(s["zs_ready"], 2 * T + 2 if last else 2 * T + 3)
                pe.wait_ge(s["yb_ready"], 2 * T + d + 1)
                for c in range(CH):
                    mm = nc.tensor.matmul(PI[0][:, :], Wc[:, d, c, :], yb[d][:, c, :],
                                          start=(d == 0 and c == 0), stop=(d == 1 and c == CH - 1),
                                          skip_group_check=True)
                if d == 1:
                    mm.then_inc(s["out_done"], 1)

            def tail_turn(T):
                pe.wait_ge(s["sum_ready"], T + 1)
                for j in range(SUB):
                    mm = nc.tensor.transpose(PI[1][:, j * P:(j + 1) * P], rT[:, j * P:(j + 1) * P], ident[:, :])
                mm.then_inc(s["sum_turned"], 1)

            def tail_back(T, last):
                pe.wait_ge(s["applied"], 2 * T + 2)
                if last:
                    pe.wait_ge(s["out_copied"], T + 1)
                else:
                    pe.wait_ge(s["zs_ready"], 2 * T + 4)
                for j in range(SUB):
                    mm = nc.tensor.transpose(PI[0][:, j * P:(j + 1) * P], ln[1][:, j, :], ident[:, :])
                mm.then_inc(s["x_turned"], 1)

            def prologue():
                pe.wait_ge(s["pick_ready"], 1)
                for c in range(CH):
                    for half in range(2):
                        conv(0, 0, c, 0, None, half)
                xproj(0, 0)
                dt(0, 0)
                z(0, 0, 0)
                bcast(0, 0, 0)

            def unit(T, d, has_next, has_prev):
                u = 2 * T + d
                T_next = T + d
                if not has_prev:
                    free = [[("zs_ready", u + 1)]] * 2
                elif d == 0:
                    free = [[("out_copied", T)], [("applied", 2 * T - 1)]]
                else:
                    free = [[("x_stored", T)], [("zs_ready", u + 1)]]
                for n in range(S):
                    if n + 1 < S:
                        bcast(u, d, n + 1)
                    elif has_next:
                        bcast(u + 1, 1 - d, 0)
                    for c in range(CH):
                        step = 2 * n + c
                        ysum(u, n, c)
                        if has_prev and d == 0 and step in (TAIL["out"] - 2, TAIL["out"]):
                            tail_out(T - 1, False, int(step == TAIL["out"]))
                        if has_prev and d == 0 and step == TAIL["turn"]:
                            tail_turn(T - 1)
                        if has_prev and d == 1 and step == TAIL["back"]:
                            tail_back(T - 1, False)
                        for k in range(CH):
                            for half in range(2):
                                if has_next and step == prep(f"conv{k}", d) + 2 * half:
                                    conv(u + 1, 1 - d, k, T_next, free[k], half)
                        if has_next and step == prep("xproj", d):
                            xproj(u + 1, 1 - d)
                        if has_next and step == prep("dt", d):
                            dt(u + 1, 1 - d)
                        if has_next and step == prep("z", d):
                            z(u + 1, 1 - d, T_next)

            def epilogue():
                tail_out(TILES - 1, True, 0)
                tail_out(TILES - 1, True, 1)
                tail_turn(TILES - 1)
                tail_back(TILES - 1, True)

            drive(pe, prologue, unit, epilogue)

        @block.scalar
        def _(act):
            act.wait_ge(s["weights_loaded"], WL)
            act.wait_ge(s["zeroed"], 2)
            nc.scalar.activation(alog[:, :, :, :], alog[:, :, :, :], ACT.Exp).then_inc(s["exp_alog"], 1)
            act.wait_ge(s["exp_alog"], 1)
            nc.scalar.activation(negA[:, :, :, :], alog[:, :, :, :], ACT.Copy, scale=-1.0).then_inc(s["negA_ready"], 1)
            nc.scalar.activation(pick[:, :, :], eye3[:, :].unsqueeze(2).to_broadcast([3 * BC, BC, P]), ACT.Copy
                                 ).then_inc(s["pick_ready"], 1)
            act.wait_ge(s["wc_done"], 1)
            nc.scalar.activation(Wc[:, :, :, :].rearrange("p d c e -> p (d c e)"), PI[0][:, :], ACT.Copy
                                 ).then_inc(s["wc_ready"], 1)
            act.wait_ge(s["negA_ready"], 1)

            def silu(v, d):
                if not isinstance(v, int) or v >= 2:
                    act.wait_ge(s["yb_ready"], v - 1)
                for c in range(CH):
                    act.wait_ge(s["conv_done"], CH * v + c + 1)
                    ins = nc.scalar.activation(xs[d][:, c, :], PI[c][:, :], ACT.Silu, bias=mcol[:, d, c, 0:1])
                ins.then_inc(s["silu_done"], 1)

            def silu_z(v, d):
                act.wait_ge(s["z_done"], v + 1)
                if not isinstance(v, int) or v >= 2:
                    act.wait_ge(s["yb_ready"], v - 1)
                for c in range(CH):
                    ins = nc.scalar.activation(zs[d][:, c, :], PI[c][:, :], ACT.Silu)
                ins.then_inc(s["zs_ready"], 1)

            def x40_copy(v, d):
                act.wait_ge(s["xproj_done"], v + 1)
                if not isinstance(v, int) or v >= 1:
                    act.wait_ge(s["dt_done"], v)
                    act.wait_ge(s["rows_ready"], v)
                if not isinstance(v, int) or v >= 2:
                    act.wait_ge(s["bcast_done"], S * (v - 1))
                nc.scalar.activation(x40[:, :], PI[0][0:XR, :], ACT.Copy).then_inc(s["x40_ready"], 1)
                nc.scalar.activation(rows[d][0:BC, :], PI[0][0:BC, :], ACT.Copy).then_inc(s["hi_ready"], 1)

            def softplus(v, d):
                act.wait_ge(s["dt_done"], v + 1)
                if not isinstance(v, int) or v >= 1:
                    act.wait_ge(s["delta_ready"], v)
                for c in range(CH):
                    bias = mcol[:, d, c, 1:2]
                    nc.scalar.activation(rv[:, c, :], PI[c][:, :], ACT.Relu, bias=bias)
                    ins = nc.scalar.activation(lw[:, c, :], PI[c][:, :], ACT.Abs, bias=bias)
                ins.then_inc(s["softplus_in"], 1)
                act.wait_ge(s["softplus_in"], v + 1)
                nc.scalar.activation(eu[:, :, :], lw[:, :, :], ACT.Exp, scale=-1.0).then_inc(s["exp_u"], 1)

            def log(v):
                act.wait_ge(s["exp_u"], v + 1)
                nc.scalar.activation(lw[:, :, :], eu[:, :, :], ACT.Ln, bias=1.0).then_inc(s["ln_a"], 1)

            def decay(u, d, n, c):
                step = 2 * n + c
                if step == 0:
                    act.wait_ge(s["delta_ready"], u + 1)
                if not isinstance(u, int) or STEPS * u + step - NDA + 1 > 0:
                    act.wait_ge(s["state_ready"], STEPS * u + step - NDA + 1)
                src = dl[d][:, c, :].rearrange("p (b t) -> p b t", b=2)
                dst = dA[d][step % NDA][:, :].rearrange("p (b t) -> p b t", b=2)
                lo = 1 if d == 0 else 0
                nc.scalar.activation(dst[:, :, lo:lo + L - 1], src[:, :, lo:lo + L - 1], ACT.Exp,
                                     scale=negA[:, d, c, n:n + 1]).then_inc(s["dA_ready"], 1)

            def tail_out(T):
                act.wait_ge(s["out_done"], T + 1)
                if not isinstance(T, int) or T >= 1:
                    act.wait_ge(s["sum_ready"], T)
                nc.scalar.activation(oT[:, :], PI[0][:, :], ACT.Identity, bias=fusb[:, 0:1]
                                     ).then_inc(s["out_copied"], 1)

            def tail_store(T):
                act.wait_ge(s["x_turned"], T + 1)
                apart(act)
                nc.scalar.activation(XT[:, tile_cols(T)], PI[0][:, :], ACT.Copy).then_inc(s["x_stored"], 1)

            def prologue():
                silu(0, 0)
                x40_copy(0, 0)
                softplus(0, 0)
                log(0)
                silu_z(0, 0)

            def unit(T, d, has_next, has_prev):
                u = 2 * T + d
                for n in range(S):
                    for c in range(CH):
                        step = 2 * n + c
                        decay(u, d, n, c)
                        if has_prev and d == 0 and step == TAIL["copy"]:
                            tail_out(T - 1)
                        if has_prev and d == 1 and step == TAIL["store"]:
                            tail_store(T - 1)
                        if has_next and step == prep("silu", d):
                            silu(u + 1, 1 - d)
                        if has_next and step == prep("x40", d):
                            x40_copy(u + 1, 1 - d)
                        if has_next and step == prep("softplus", d):
                            softplus(u + 1, 1 - d)
                        if has_next and step == prep("log", d):
                            log(u + 1)
                        if has_next and step == prep("zs", d):
                            silu_z(u + 1, 1 - d)

            def epilogue():
                tail_out(TILES - 1)
                tail_store(TILES - 1)

            drive(act, prologue, unit, epilogue)

        @block.vector
        def _(dve):
            dve.wait_ge(s["zeroed"], 2)
            dve.wait_ge(s["weights_loaded"], WL)

            def split(v, d):
                dve.wait_ge(s["hi_ready"], v + 1)
                nc.vector.tensor_tensor(rem[:, :], x40[0:BC, :], rows[d][0:BC, :], ALU.subtract
                                        ).then_inc(s["split_chain"], 1)
                dve.wait_ge(s["split_chain"], 2 * v + 1)
                nc.vector.tensor_copy(mid[:, :], rem[:, :]).then_inc(s["split_chain"], 1)
                nc.vector.tensor_copy(rows[d][BC:2 * BC, :], rem[:, :])
                dve.wait_ge(s["split_chain"], 2 * v + 2)
                nc.vector.tensor_tensor(rows[d][2 * BC:3 * BC, :], rem[:, :], mid[:, :], ALU.subtract
                                        ).then_inc(s["rows_ready"], 1)

            def blend(v):
                dve.wait_ge(s["ln_a"], v + 1)
                nc.vector.tensor_scalar(small[:, :, :], eu[:, :, :], SMALL, None, ALU.is_lt
                                        ).then_inc(s["mask_done"], 1)
                dve.wait_ge(s["mask_done"], v + 1)
                dve.wait_ge(s["poly_chain"], 6 * v + 6)
                apart(dve)
                nc.vector.copy_predicated(lw[:, :, :], small[:, :, :], pp[:, :, :]).then_inc(s["log1p_done"], 1)

            def order(d, ap):
                return ap if d == 0 else ap[:, ::-1]

            def to_state(u, d, n, c):
                step = 2 * n + c
                if step == 0:
                    dve.wait_ge(s["du_ready"], u + 1)
                if c == 0:
                    dve.wait_ge(s["bcast_done"], S * u + n + 1)
                nc.vector.tensor_tensor(dbx[step % 2][:, :], du[d][:, c, :], Bb[n % 2][:, :], ALU.mult
                                        ).then_inc(s["dbx_ready"], 1)

            def scan(u, d, n, c):
                step = 2 * n + c
                dve.wait_ge(s["dA_ready"], STEPS * u + step + 1)
                dve.wait_ge(s["dbx_ready"], STEPS * u + step + 1)
                nc.vector.tensor_tensor_scan(order(d, hs[step % 2][:, :]), order(d, dA[d][step % NDA][:, :]),
                                             order(d, dbx[step % 2][:, :]), 0.0, ALU.mult, ALU.add
                                             ).then_inc(s["state_ready"], 1)

            def from_state(u, n, c):
                step = 2 * n + c
                dve.wait_ge(s["state_ready"], STEPS * u + step + 1)
                if not isinstance(u, int) or STEPS * u + step - NHC + 1 > 0:
                    dve.wait_ge(s["y_step"], STEPS * u + step - NHC + 1)
                nc.vector.tensor_tensor(hc[step % NHC][:, :], hs[step % 2][:, :], Cb[n % 2][:, :], ALU.mult
                                        ).then_inc(s["hc_ready"], 1)

            def post(u, d):
                dve.wait_ge(s["y_step"], STEPS * (u + 1))
                if not isinstance(u, int) or u >= 1:
                    dve.wait_ge(s["yb_ready"], u)
                for c in range(CH):
                    ins = nc.vector.scalar_tensor_tensor(out=yv[:, c, :], in0=xs[d][:, c, :],
                                                         scalar=mcol[:, d, c, 2:3], in1=PY[c][:, :],
                                                         op0=ALU.mult, op1=ALU.add)
                ins.then_inc(s["post_done"], 1)

            def tail_sum(T):
                dve.wait_ge(s["out_copied"], T + 1)
                if not isinstance(T, int) or T >= 1:
                    dve.wait_ge(s["sum_turned"], T)
                nc.vector.tensor_tensor(rT[:, :], oT[:, :], XT[:, tile_cols(T)], ALU.add).then_inc(s["sum_ready"], 1)

            def tail_stats(T, i):
                if i == 0:
                    dve.wait_ge(s["sum_turned"], T + 1)
                    src = PI[1][:, :].rearrange("p (j c) -> p j c", j=SUB)
                else:
                    dve.wait_ge(s["gain_chain"], 3 * T + 3)
                    src = R[:, tile_subs(T), :]
                bn_norm(dve, nc, src, st[i], mv[i], s["bn_done"], s["moments_ready"], s["rstd_ready"], 2 * T + i)

            def tail_apply(T, i):
                src = PI[1][:, :].rearrange("p (j c) -> p j c", j=SUB) if i == 0 else R[:, tile_subs(T), :]
                if i == 1 and (not isinstance(T, int) or T >= 1):
                    dve.wait_ge(s["x_turned"], T)
                bn_apply(dve, nc, ln[i], src, mv[i], rs[i], s["rstd_ready"], s["applied"], 2 * T + i)
                if i == 0:
                    x = ln[0][:, :, :]
                    dve.wait_ge(s["applied"], 2 * T + 1)
                    nc.vector.tensor_tensor(x, x, gb[:, 0:1, :].to_broadcast([P, SUB, P]), ALU.mult
                                            ).then_inc(s["gain_chain"], 1)
                    dve.wait_ge(s["gain_chain"], 3 * T + 1)
                    nc.vector.tensor_tensor(x, x, gb[:, 1:2, :].to_broadcast([P, SUB, P]), ALU.add
                                            ).then_inc(s["gain_chain"], 1)
                    dve.wait_ge(s["gain_chain"], 3 * T + 2)
                    r = R[:, tile_subs(T), :]
                    nc.vector.tensor_tensor(r, r, x, ALU.add).then_inc(s["gain_chain"], 1)

            def prologue():
                split(0, 0)
                blend(0)

            def unit(T, d, has_next, has_prev):
                u = 2 * T + d
                to_state(u, d, 0, 0)
                for n in range(S):
                    for c in range(CH):
                        step = 2 * n + c
                        scan(u, d, n, c)
                        if step + 1 < STEPS:
                            to_state(u, d, (step + 1) // 2, (step + 1) % 2)
                        from_state(u, n, c)
                        if step == 0 and not (isinstance(u, int) and u == 0):
                            post(u - 1, 1 - d)
                        if has_prev and d == 0:
                            if step == TAIL["sum"]:
                                tail_sum(T - 1)
                            if step == TAIL["stats1"]:
                                tail_stats(T - 1, 0)
                            if step == TAIL["apply1"]:
                                tail_apply(T - 1, 0)
                            if step == TAIL["stats2"]:
                                tail_stats(T - 1, 1)
                            if step == TAIL["apply2"]:
                                tail_apply(T - 1, 1)
                        if has_next:
                            if step == prep("split", d):
                                split(u + 1, 1 - d)
                            if step == prep("blend", d):
                                blend(u + 1)

            def epilogue():
                post(2 * TILES - 1, 1)
                T = TILES - 1
                tail_sum(T)
                tail_stats(T, 0)
                tail_apply(T, 0)
                tail_stats(T, 1)
                tail_apply(T, 1)

            drive(dve, prologue, unit, epilogue)


def expert_choice_stage(nc, a, R, XT, ident, w_dram):
    E, F, CAP = 8, 512, 1024
    FC = F // P
    BITS = 30
    with ExitStack() as ctx:
        m = Mem(nc, ctx)
        wr = m.sb("wr", [P, E])
        w1h = m.sb("e_w1h", [P, E, F], F32R)
        w1l = m.sb("e_w1l", [P, E, F], F32R)
        xb = [m.sb(f"e_xb{i}", [P, TOK]) for i in range(2)]
        xh = [m.sb(f"e_xh{i}", [P, TOK], F32R) for i in range(2)]
        xl = [m.sb(f"e_xl{i}", [P, TOK], F32R) for i in range(2)]
        b1 = m.sb("e_b1", [P, E, FC])
        w2 = m.sb("e_w2", [P, E, FC, P])
        b2 = m.sb("e_b2", [P, E])
        same = m.sb("same", [P, P])
        before = m.sb("before", [P, P])
        bit = m.sb("bit", [P, BITS], I32)
        ones = m.sb("e_ones", [P, L])
        LT = m.sb("LT", [P, 2, E, B])
        V = m.sb("V", [P, L])
        pr = m.sb("pr", [P, L])
        junk = m.sb("junk", [P, L])
        gt = m.sb("gt", [P, L])
        eq = m.sb("eq", [P, L])
        cum = m.sb("cum", [P, L])
        wt = m.sb("wt", [P, L])
        mx = m.sb("mx", [P, 1])
        mrow = m.sb("mrow", [1, E, B])
        m8 = m.sb("m8", [1, E])
        nmx = m.sb("nmx", [P, 1])
        ssum = m.sb("ssum", [P, 1])
        rtot = m.sb("rtot", [P, 1])
        cur = m.sb("cur", [P, 1], I32)
        cand = m.sb("cand", [P, 1], I32)
        keep = m.sb("keep", [P, 1], I32)
        cnt = m.sb("cnt", [P, 1])
        room = m.sb("room", [P, 1])
        off = m.sb("off", [P, 1])
        wb = [m.sb(f"wb{i}", [P, E, TOK]) for i in range(2)]
        hb = [m.sb(f"hb{i}", [P, FC, TOK]) for i in range(2)]
        u = m.sb("e_u", [P, E, TOK])
        part = [m.sb(f"part{i}", [P, TOK]) for i in range(2)]
        acc = m.sb("acc", [P, TOK])
        st = m.sb("est", [P, SUB, 6])
        mv = m.sb("emv", [P, SUB, 2])
        ve = m.sb("eve", [P, SUB])
        rs = m.sb("ers", [P, SUB])
        ln = m.sb("eln", [P, SUB, P])
        eps = m.sb("eeps", [P, SUB])
        mhalf = m.sb("emhalf", [P, SUB])
        PH = m.ps("ePH", [P, FC, TOK])
        PO = [m.ps(f"ePO{i}", [P, TOK]) for i in range(2)]
        PT = m.ps("ePT", [P, TOK])
        PB = m.ps("ePB", [P, TOK])

        names = ("routing_loaded biases_loaded w2_loaded u_ready logits_done logits_copied rows_turned rows_copied max_done max_turned "
                 "max_row_ready max_sent negmax_ready exp_done total_sent chain counted bit_sent "
                 "weight_ready weight_stored wb_loaded0 wb_loaded1 hid_done gelu_done out_done part_ready acc_step "
                 "acc_turned resid_done bn_done moments_ready var_eps_ready rstd_ready applied x_turned x_stored "
                 "consts zero_cur off_ready w1_loaded w_high w_split x_copied x_high x_split").split()
        s = {n: m.sem("e_" + n) for n in names}
        block = ctx.enter_context(nc.Block())

        def drive(eng, unit, tail):
            for T in range(2):
                unit(T, T > 0)
            with eng.Fori(2, TILES) as T:
                unit(T, True)
            tail(TILES - 1)

        @block.sync
        def _(sp):
            for dst, src in ((wr[:, :], a["wr"]), (same[:, :], a["same"]), (before[:, :], a["before"]),
                             (bit[:, :], a["bit"].partition_broadcast(P))):
                sp.dma_start(dst, src).then_inc(s["routing_loaded"], 16)
            for dst, src in ((b1[:, :, :], a["e_b1"]), (b2[:, :], a["e_b2"])):
                sp.dma_start(dst, src).then_inc(s["biases_loaded"], 16)
            sp.dma_start(wb[0][:, :, :], a["e_w1"]).then_inc(s["w1_loaded"], 16)
            sp.dma_start(w2[:, :, :, :], a["e_w2"]).then_inc(s["w2_loaded"], 16)
            sp.wait_ge(s["weight_ready"], 1)
            sp.dma_start(w_dram.rearrange("e (b t) -> (e b) t", b=B), wt[:, :]).then_inc(s["weight_stored"], 16)
            sp.wait_ge(s["weight_stored"], 16)

            def load(T, i):
                sp.dma_start(wb[i][:, :, :], w_dram[:, bass.ds(T * TOK, TOK)].partition_broadcast(P)
                             ).then_inc(s[f"wb_loaded{i}"], 16)

            sp.wait_ge(s["w_split"], E)
            load(0, 0)
            load(1, 1)
            with sp.Fori(1, TILES // 2) as q:
                for i in range(2):
                    sp.wait_ge(s["part_ready"], E * (2 * q + i - 1))
                    load(2 * q + i, i)

        @block.gpsimd
        def _(pool):
            nc.gpsimd.memset(eps[:, :], 1e-5)
            nc.gpsimd.memset(ones[:, :], 1.0).then_inc(s["consts"], 1)
            nc.gpsimd.memset(mhalf[:, :], -0.5).then_inc(s["consts"], 1)
            pool.wait_ge(s["consts"], 2)

            def root(T):
                pool_rstd(pool, nc, mv, ve, rs, eps, mhalf, s["moments_ready"], s["var_eps_ready"],
                          s["rstd_ready"], s["applied"], T)

            def split_x(T, i):
                if not isinstance(T, int) or T >= 2:
                    pool.wait_ge(s["hid_done"], FC * E * (T - 1))
                apart(pool)
                nc.gpsimd.tensor_copy(xb[i][:, :], XT[:, bass.ds(T * TOK, TOK)]).then_inc(s["x_copied"], 1)
                pool.wait_ge(s["x_copied"], T + 1)
                apart(pool)
                nc.gpsimd.tensor_copy(xh[i][:, :], xb[i][:, :]).then_inc(s["x_high"], 1)
                pool.wait_ge(s["x_high"], T + 1)
                nc.gpsimd.tensor_tensor(xl[i][:, :], xb[i][:, :], xh[i][:, :], ALU.subtract).then_inc(s["x_split"], 1)

            split_x(0, 0)
            pool.wait_ge(s["w1_loaded"], 16)
            for e in range(E):
                nc.gpsimd.tensor_copy(w1h[:, e, :], wb[0][:, e, :]).then_inc(s["w_high"], 1)
                pool.wait_ge(s["w_high"], e + 1)
                nc.gpsimd.tensor_tensor(w1l[:, e, :], wb[0][:, e, :], w1h[:, e, :], ALU.subtract
                                        ).then_inc(s["w_split"], 1)
            split_x(1, 1)
            root(0)
            split_x(2, 0)
            root(1)
            with pool.Fori(1, TILES // 2 - 1) as q:
                for i in range(2):
                    split_x(2 * q + 1 + i, 1 - i)
                    root(2 * q + i)
            split_x(TILES - 1, 1)
            root(TILES - 2)
            root(TILES - 1)

        @block.tensor
        def _(pe):
            pe.wait_ge(s["routing_loaded"], 64)
            for j in range(N // P):
                mm = nc.tensor.matmul(PT[:, j * E:(j + 1) * E], XT[:, j * P:(j + 1) * P], wr[:, :],
                                      start=True, stop=True)
            mm.then_inc(s["logits_done"], 1)
            pe.wait_ge(s["logits_copied"], 1)
            for h in range(2):
                mm = nc.tensor.transpose(PB[:, h * P:(h + 1) * P], LT[:, h, :, :].rearrange("p e b -> p (e b)"),
                                         ident[:, :])
            mm.then_inc(s["rows_turned"], 1)
            pe.wait_ge(s["max_done"], 1)
            nc.tensor.transpose(PT[0:1, 0:P], mx[:, :], ident[:, :]).then_inc(s["max_turned"], 1)
            pe.wait_ge(s["max_row_ready"], 1)
            pe.wait_ge(s["consts"], 2)
            nc.tensor.matmul(PT[:, 0:1], mrow[:, :, :].rearrange("o e b -> o (e b)"), ones[0:1, 0:1],
                             start=True, stop=True).then_inc(s["max_sent"], 1)
            pe.wait_ge(s["exp_done"], 1)
            nc.tensor.matmul(PT[:, 0:1], same[:, :], ssum[:, :], start=True, stop=True).then_inc(s["total_sent"], 1)

            def hid(T, g, e, ti, f):
                if e == 0 and f == 0:
                    pe.wait_ge(s["x_split"], T + 1)
                if isinstance(g, int) and g < E:
                    pe.wait_ge(s["w_split"], e + 1)
                if not isinstance(g, int) or g >= 1:
                    pe.wait_ge(s["gelu_done"], FC * (g - 1) + f + 1)
                apart(pe)
                cols = slice(f * P, (f + 1) * P)
                nc.tensor.matmul(PH[:, f, :], w1h[:, e, cols], xh[ti][:, :], start=True, stop=False)
                nc.tensor.matmul(PH[:, f, :], w1l[:, e, cols], xh[ti][:, :], start=False, stop=False)
                nc.tensor.matmul(PH[:, f, :], w1h[:, e, cols], xl[ti][:, :], start=False, stop=True
                                 ).then_inc(s["hid_done"], 1)

            def out(g, e, i, f):
                pe.wait_ge(s["gelu_done"], FC * g + f + 1)
                if f == 0:
                    if not isinstance(g, int) or g >= E + 2:
                        pe.wait_ge(s["part_ready"], g - 1)
                    elif g >= 2:
                        pe.wait_ge(s["u_ready"], g - 1)
                mm = nc.tensor.matmul(PO[i][:, :], w2[:, e, f, :], hb[i][:, f, :],
                                      start=(f == 0), stop=(f == FC - 1))
                if f == FC - 1:
                    mm.then_inc(s["out_done"], 1)

            def early(step):
                e, f = step // FC, step % FC
                hid(0, e, e, 0, f)
                if e == 1 and f == 0:
                    pe.wait_ge(s["w2_loaded"], 16)
                if e >= 1:
                    out(e - 1, e - 1, (e - 1) % 2, f)

            for i in range(BITS + 1):
                pe.wait_ge(s["counted"], i + 1)
                nc.tensor.matmul(PT[:, 0:1], same[:, :], cnt[:, :], start=True, stop=True).then_inc(s["bit_sent"], 1)
                if i < BITS:
                    early(i)
            pe.wait_ge(s["counted"], BITS + 2)
            nc.tensor.matmul(PB[:, 0:1], before[:, :], cum[:, L - 1:L], start=True, stop=True
                             ).then_inc(s["bit_sent"], 1)
            for step in range(BITS, E * FC):
                early(step)

            def turn(T):
                pe.wait_ge(s["acc_step"], E * (T + 1))
                for j in range(SUB):
                    mm = nc.tensor.transpose(PT[:, j * P:(j + 1) * P], acc[:, j * P:(j + 1) * P], ident[:, :])
                mm.then_inc(s["acc_turned"], 1)

            def back(T):
                pe.wait_ge(s["applied"], T + 1)
                if not isinstance(T, int) or T >= 1:
                    pe.wait_ge(s["x_stored"], T)
                for j in range(SUB):
                    mm = nc.tensor.transpose(PB[:, j * P:(j + 1) * P], ln[:, j, :], ident[:, :])
                mm.then_inc(s["x_turned"], 1)

            def unit(T, ti, has_prev):
                for e in range(E):
                    g = T * E + e
                    for f in range(FC):
                        hid(T, g, e, ti, f)
                    for f in range(FC):
                        out(g - 1, (e - 1) % E, (e + 1) % 2, f)
                    if has_prev and e == 1:
                        turn(T - 1)
                    if has_prev and e == 4:
                        back(T - 1)

            def tail(T):
                for f in range(FC):
                    out(E * TILES - 1, E - 1, 1, f)
                turn(T)
                back(T)

            unit(1, 1, True)
            with pe.Fori(1, TILES // 2) as q:
                for i in range(2):
                    unit(2 * q + i, i, True)
            tail(TILES - 1)

        @block.scalar
        def _(act):
            act.wait_ge(s["logits_done"], 1)
            nc.scalar.activation(LT[:, :, :, :], PT[:, 0:N // P * E].rearrange("p (b h e) -> p h e b", h=2, e=E),
                                 ACT.Copy).then_inc(s["logits_copied"], 1)
            act.wait_ge(s["rows_turned"], 1)
            nc.scalar.activation(V[:, :], PB[:, 0:L], ACT.Copy).then_inc(s["rows_copied"], 1)
            act.wait_ge(s["max_sent"], 1)
            nc.scalar.activation(nmx[:, :], PT[:, 0:1], ACT.Copy, scale=-1.0).then_inc(s["negmax_ready"], 1)
            act.wait_ge(s["negmax_ready"], 1)
            act.wait_ge(s["rows_copied"], 1)
            nc.scalar.activation(pr[:, :], V[:, :], ACT.Exp, bias=nmx[:, :], accum_out=ssum[:, :]
                                 ).then_inc(s["exp_done"], 1)
            act.wait_ge(s["biases_loaded"], 32)

            def offsets():
                act.wait_ge(s["bit_sent"], BITS + 2)
                nc.scalar.activation(off[:, :], PB[:, 0:1], ACT.Copy).then_inc(s["off_ready"], 1)

            def keep_out(e):
                act.wait_ge(s["out_done"], e + 1)
                nc.scalar.activation(u[:, e, :], PO[e % 2][:, :], ACT.Identity, bias=b2[:, e:e + 1]
                                     ).then_inc(s["u_ready"], 1)

            def gelu(g, e, i):
                for f in range(FC):
                    if isinstance(g, int) and g * FC + f == BITS:
                        offsets()
                    act.wait_ge(s["hid_done"], FC * g + f + 1)
                    if f == 0 and (not isinstance(g, int) or g >= 2):
                        act.wait_ge(s["out_done"], g - 1)
                    nc.scalar.activation(hb[i][:, f, :], PH[:, f, :], ACT.Gelu, bias=b1[:, e, f:f + 1]
                                         ).then_inc(s["gelu_done"], 1)

            def store(T):
                act.wait_ge(s["x_turned"], T + 1)
                apart(act)
                nc.scalar.activation(XT[:, bass.ds(T * TOK, TOK)], PB[:, :], ACT.Copy).then_inc(s["x_stored"], 1)

            def unit(T, has_prev):
                for e in range(E):
                    gelu(T * E + e, e, e % 2)
                    if isinstance(T, int) and 1 <= T * E + e <= E:
                        keep_out(T * E + e - 1)
                    if has_prev and e == 4:
                        store(T - 1)

            drive(act, unit, store)

        @block.vector
        def _(dve):
            n = [0]

            def link(ins):
                n[0] += 1
                ins.then_inc(s["chain"], 1)
                dve.wait_ge(s["chain"], n[0])

            nc.vector.memset(cur[:, :], 0).then_inc(s["zero_cur"], 1)
            dve.wait_ge(s["rows_copied"], 1)
            nc.vector.reduce_max(mx[:, :], V[:, :], AX_X).then_inc(s["max_done"], 1)
            dve.wait_ge(s["max_turned"], 1)
            link(nc.vector.reduce_max(m8[:, :], PT[0:1, 0:P].rearrange("o (e b) -> o e b", b=B), AX_X))
            nc.vector.tensor_copy(mrow[:, :, :], m8[:, :].unsqueeze(2).to_broadcast([1, E, B])
                                  ).then_inc(s["max_row_ready"], 1)
            dve.wait_ge(s["total_sent"], 1)
            link(nc.vector.reciprocal(rtot[:, :], PT[:, 0:1]))
            link(nc.vector.tensor_scalar(pr[:, :], pr[:, :], rtot[:, :], None, ALU.mult))
            dve.wait_ge(s["routing_loaded"], 64)
            dve.wait_ge(s["zero_cur"], 1)
            PER = 3
            n0 = n[0]

            def search(i):
                nc.vector.tensor_tensor(cand[:, :], cur[:, :], bit[:, bass.ds(i, 1)], ALU.bitwise_or
                                        ).then_inc(s["chain"], 1)
                dve.wait_ge(s["chain"], n0 + PER * i + 1)
                nc.vector.tensor_scalar(junk[:, :], pr[:, :], cand[:, :].bitcast(F32), None, ALU.is_ge, ALU.add,
                                        accum_out=cnt[:, :]).then_inc(s["counted"], 1)
                dve.wait_ge(s["bit_sent"], i + 1)
                nc.vector.tensor_scalar(keep[:, :], PT[:, 0:1], float(CAP), None, ALU.is_ge).then_inc(s["chain"], 1)
                dve.wait_ge(s["chain"], n0 + PER * i + 2)
                apart(dve)
                nc.vector.copy_predicated(cur[:, :], keep[:, :], cand[:, :]).then_inc(s["chain"], 1)
                dve.wait_ge(s["chain"], n0 + PER * i + 3)

            with dve.Fori(0, BITS) as i:
                search(i)
            n[0] = n0 + PER * BITS
            thr = cur[:, :].bitcast(F32)
            nc.vector.tensor_scalar(gt[:, :], pr[:, :], thr, None, ALU.is_gt, ALU.add, accum_out=cnt[:, :]
                                    ).then_inc(s["counted"], 1)
            link(nc.vector.tensor_scalar(eq[:, :], pr[:, :], thr, None, ALU.is_equal))
            nc.vector.tensor_tensor_scan(cum[:, :], ones[:, :], eq[:, :], 0.0, ALU.mult, ALU.add
                                         ).then_inc(s["counted"], 1)
            dve.wait_ge(s["bit_sent"], BITS + 1)
            link(nc.vector.tensor_scalar(room[:, :], PT[:, 0:1], -1.0, float(CAP), ALU.mult, ALU.add))
            dve.wait_ge(s["off_ready"], 1)
            link(nc.vector.tensor_scalar(cum[:, :], cum[:, :], off[:, :], room[:, :], ALU.add, ALU.is_le))
            link(nc.vector.tensor_tensor(eq[:, :], eq[:, :], cum[:, :], ALU.mult))
            link(nc.vector.tensor_tensor(gt[:, :], gt[:, :], eq[:, :], ALU.add))
            nc.vector.tensor_tensor(wt[:, :], gt[:, :], pr[:, :], ALU.mult).then_inc(s["weight_ready"], 1)
            dve.wait_ge(s["biases_loaded"], 32)

            def weigh(T, g, e, i, ti):
                early = isinstance(g, int) and g < E
                dve.wait_ge(s["u_ready" if early else "out_done"], g + 1)
                if e == 0:
                    dve.wait_ge(s[f"wb_loaded{ti}"], 16 * T_half[0])
                dst = acc if e == 0 else part[i]
                if e == 0 and (not isinstance(T, int) or T >= 1):
                    dve.wait_ge(s["acc_turned"], T)
                if early:
                    ins = nc.vector.tensor_tensor(dst[:, :], u[:, e, :], wb[ti][:, e, :], ALU.mult)
                else:
                    ins = nc.vector.scalar_tensor_tensor(out=dst[:, :], in0=PO[i][:, :], scalar=b2[:, e:e + 1],
                                                         in1=wb[ti][:, e, :], op0=ALU.add, op1=ALU.mult)
                ins.then_inc(s["part_ready"], 1)

            def add(T, g, e, i):
                dve.wait_ge(s["part_ready"], g + 1)
                if e == 0:
                    apart(dve)
                    nc.vector.engine_nop().then_inc(s["acc_step"], 1)
                else:
                    dve.wait_ge(s["acc_step"], g)
                    nc.vector.tensor_tensor(acc[:, :], acc[:, :], part[i][:, :], ALU.add).then_inc(s["acc_step"], 1)

            def resid(T):
                dve.wait_ge(s["acc_turned"], T + 1)
                r = R[:, bass.ds(T * SUB, SUB), :]
                nc.vector.tensor_tensor(r, r, PT[:, :].rearrange("p (j c) -> p j c", j=SUB), ALU.add
                                        ).then_inc(s["resid_done"], 1)

            def stats(T):
                dve.wait_ge(s["resid_done"], T + 1)
                bn_norm(dve, nc, R[:, bass.ds(T * SUB, SUB), :], st, mv, s["bn_done"], s["moments_ready"],
                        s["rstd_ready"], T)

            def apply(T):
                if not isinstance(T, int) or T >= 1:
                    dve.wait_ge(s["x_turned"], T)
                bn_apply(dve, nc, ln, R[:, bass.ds(T * SUB, SUB), :], mv, rs, s["rstd_ready"], s["applied"], T)

            T_half = [0]

            def unit(T, ti, has_prev):
                T_half[0] = T // 2 + 1 if isinstance(T, int) else T_half[0]
                for e in range(E):
                    g = T * E + e
                    weigh(T, g, e, e % 2, ti)
                    add(T, g, e, e % 2)
                    if has_prev and e == 1:
                        resid(T - 1)
                    if has_prev and e == 2:
                        stats(T - 1)
                    if has_prev and e == 3:
                        apply(T - 1)

            unit(0, 0, False)
            unit(1, 1, True)
            with dve.Fori(1, TILES // 2) as q:
                for i in range(2):
                    T_half[0] = q + 1
                    unit(2 * q + i, i, True)
            resid(TILES - 1)
            stats(TILES - 1)
            apply(TILES - 1)


def attention_stage(nc, a, R, XT, ident):
    H, DH = 8, 64
    INNER = H * DH
    IC = INNER // P
    SCALE = DH ** -0.5
    NT = L // P
    with ExitStack() as ctx:
        m = Mem(nc, ctx)
        wqkv = m.sb("wqkv", [P, 3 * INNER])
        bqk = m.sb("bqk", [P, 2, IC])
        bv = m.sb("bv", [P, INNER])
        th1 = m.sb("th1", [P, IC, H])
        th2 = m.sb("th2", [P, IC, H])
        wo = m.sb("wo", [P, IC, P])
        bo = m.sb("bo", [P, 1])
        xb = [m.sb(f"xb{i}", [P, L]) for i in range(2)]
        qT = [m.sb(f"qT{i}", [P, IC, L]) for i in range(2)]
        kT = m.sb("kT", [P, IC, L])
        kh = [m.sb(f"kh{i}", [P, IC, L], F32R) for i in range(2)]
        kl = [m.sb(f"kl{i}", [P, IC, L], F32R) for i in range(2)]
        v = m.sb("v", [P, NT, INNER])
        vh = [m.sb(f"vh{i}", [P, NT, INNER], F32R) for i in range(2)]
        vl = [m.sb(f"vl{i}", [P, NT, INNER], F32R) for i in range(2)]
        qh = [m.sb(f"qh{i}", [P, IC, L], F32R) for i in range(2)]
        ql = [m.sb(f"ql{i}", [P, IC, L], F32R) for i in range(2)]
        nm = [m.sb(f"nm{i}", [P, NT]) for i in range(2)]
        sm = [m.sb(f"sm{i}", [P, NT]) for i in range(2)]
        ri = [m.sb(f"ri{i}", [P, NT]) for i in range(2)]
        ex = [m.sb(f"ex{i}", [P, NT, L]) for i in range(2)]
        ah = [m.sb(f"ah{i}", [P, NT, L], F32R) for i in range(2)]
        al = [m.sb(f"al{i}", [P, NT, L], F32R) for i in range(2)]
        oT = [m.sb(f"a_oT{i}", [P, IC, L]) for i in range(2)]
        fo = m.sb("fo", [P, L])
        st = m.sb("ast", [P, NT, 6])
        mv = m.sb("amv", [P, NT, 2])
        ve = m.sb("ave", [P, NT])
        rs = m.sb("ars", [P, NT])
        ln = m.sb("aln", [P, NT, P])
        eps = m.sb("aeps", [P, NT])
        mhalf = m.sb("amhalf", [P, NT])
        PS = [m.ps(f"aPS{i}", [P, NT, L]) for i in range(2)]
        PA = m.ps("aPA", [P, NT, L])
        PO = [m.ps(f"aPO{i}", [P, 2, L]) for i in range(2)]
        PQ = m.ps("aPQ", [P, 2, TOK])
        PX = m.ps("aPX", [P, TOK])

        names = ("loaded consts scaled x_copied q_done q_ready k_done k_ready k_high k_split v_done v_ready v_high "
                 "v_split qh_ready qg_ready scores_done max_ready exp_done recip_ready norm_done turned ah_ready "
                 "at_ready out0_done out1_done mixed0 mixed1 proj_done proj_copied proj_turned resid_done bn_done "
                 "moments_ready var_eps_ready rstd_ready applied x_turned x_stored").split()
        s = {n: m.sem("a_" + n) for n in names}
        block = ctx.enter_context(nc.Block())
        LOADED = 16 * 7

        def after(eng, name, n):
            if not isinstance(n, int) or n > 0:
                eng.wait_ge(s[name], n)

        def drive(eng, prologue, unit, epilogue):
            prologue()
            unit(0, 0, True, False)
            unit(1, 1, True, True)
            with eng.Fori(1, B // 2 - 1) as q:
                for i in range(2):
                    unit(2 * q + i, i, True, True)
            unit(B - 2, 0, True, True)
            unit(B - 1, 1, False, True)
            epilogue()

        @block.sync
        def _(sp):
            for dst, src in ((wqkv[:, :], a["wqkv"]), (bqk[:, :, :], a["bqk"]), (bv[:, :], a["bv"].partition_broadcast(P)),
                             (th1[:, :, :], a["th1"]), (th2[:, :, :], a["th2"]),
                             (wo[:, :, :], a["wo"]), (bo[:, :], a["bo"])):
                sp.dma_start(dst, src).then_inc(s["loaded"], 16)

        @block.gpsimd
        def _(pool):
            nc.gpsimd.memset(eps[:, :], 1e-5)
            nc.gpsimd.memset(mhalf[:, :], -0.5).then_inc(s["consts"], 1)
            pool.wait_ge(s["consts"], 1)
            pool.wait_ge(s["loaded"], LOADED)

            def x_copy(b, i):
                after(pool, "v_done", b - 1)
                apart(pool)
                nc.gpsimd.tensor_copy(xb[i][:, :], XT[:, bass.ds(b * L, L)]).then_inc(s["x_copied"], 1)

            def split(b, i, src, high, low, ready, high_done, done, used):
                pool.wait_ge(s[ready], b + 1)
                after(pool, used, H * (b - 1))
                apart(pool)
                nc.gpsimd.tensor_copy(high[i][:, :, :], src[:, :, :]).then_inc(s[high_done], 1)
                pool.wait_ge(s[high_done], b + 1)
                nc.gpsimd.tensor_tensor(low[i][:, :, :], src[:, :, :], high[i][:, :, :], ALU.subtract
                                        ).then_inc(s[done], 1)

            def split_k(b, i):
                split(b, i, kT, kh, kl, "k_ready", "k_high", "k_split", "scores_done")

            def split_v(b, i):
                split(b, i, v, vh, vl, "v_ready", "v_high", "v_split", "out1_done")

            def root(b):
                pool_rstd(pool, nc, mv, ve, rs, eps, mhalf, s["moments_ready"], s["var_eps_ready"],
                          s["rstd_ready"], s["applied"], b)

            def unit(b, i, has_next, has_prev):
                if has_next:
                    x_copy(b + 1, 1 - i)
                if has_prev:
                    root(b - 1)
                if has_next:
                    split_k(b + 1, 1 - i)
                    split_v(b + 1, 1 - i)

            def prologue():
                x_copy(0, 0)
                split_k(0, 0)
                split_v(0, 0)

            drive(pool, prologue, unit, lambda: root(B - 1))

        @block.tensor
        def _(pe):
            pe.wait_ge(s["loaded"], LOADED)

            def q_or_k(b, i, which):
                after(pe, "v_ready", b) if which == 0 else pe.wait_ge(s["q_ready"], b + 1)
                for c in range(IC):
                    mm = nc.tensor.matmul(PQ[:, c // 2, c % 2 * L:(c % 2 + 1) * L],
                                          wqkv[:, which * INNER + c * P:which * INNER + (c + 1) * P],
                                          XT[:, bass.ds(b * L, L)], start=True, stop=True)
                mm.then_inc(s["q_done" if which == 0 else "k_done"], 1)

            def v_proj(b, i):
                pe.wait_ge(s["k_ready"], b + 1)
                pe.wait_ge(s["x_copied"], b + 1)
                for t in range(NT):
                    mm = nc.tensor.matmul(PQ[:, t, :], xb[i][:, t * P:(t + 1) * P], wqkv[:, 2 * INNER:3 * INNER],
                                          start=True, stop=True)
                mm.then_inc(s["v_done"], 1)

            def scores(b, i, g):
                c = H * b + g
                pe.wait_ge(s["qg_ready"], c + 1)
                if g == 0:
                    pe.wait_ge(s["k_split"], b + 1)
                after(pe, "exp_done", c - 1)
                for t in range(NT):
                    toks = slice(t * P, (t + 1) * P)
                    for j in range(IC):
                        PSt = PS[g % 2][:, t, :]
                        nc.tensor.matmul(PSt, qh[g % 2][:, j, toks], kh[i][:, j, :], start=(j == 0), stop=False)
                        nc.tensor.matmul(PSt, qh[g % 2][:, j, toks], kl[i][:, j, :], start=False, stop=False)
                        mm = nc.tensor.matmul(PSt, ql[g % 2][:, j, toks], kh[i][:, j, :], start=False,
                                              stop=(j == IC - 1))
                mm.then_inc(s["scores_done"], 1)

            def turn_probs(c, g):
                pe.wait_ge(s["norm_done"], c + 1)
                after(pe, "at_ready", c)
                for t in range(NT):
                    for k in range(NT):
                        mm = nc.tensor.transpose(PA[:, k, t * P:(t + 1) * P], ex[g % 2][:, t, k * P:(k + 1) * P],
                                                 ident[:, :])
                mm.then_inc(s["turned"], 1)

            def out(b, i, g):
                c = H * b + g
                pe.wait_ge(s["at_ready"], c + 1)
                if g == 0:
                    pe.wait_ge(s["v_split"], b + 1)
                for half in range(2):
                    after(pe, f"mixed{half}", c)
                    for j in (2 * half, 2 * half + 1):
                        chans = slice(j * P, (j + 1) * P)
                        for k in range(NT):
                            PSj = PO[half][:, j % 2, :]
                            nc.tensor.matmul(PSj, vh[i][:, k, chans], ah[g % 2][:, k, :], start=(k == 0), stop=False)
                            nc.tensor.matmul(PSj, vh[i][:, k, chans], al[g % 2][:, k, :], start=False, stop=False)
                            mm = nc.tensor.matmul(PSj, vl[i][:, k, chans], ah[g % 2][:, k, :], start=False,
                                                  stop=(k == NT - 1))
                    mm.then_inc(s[f"out{half}_done"], 1)

            def project(b, i):
                pe.wait_ge(s["mixed0"], H * (b + 1))
                pe.wait_ge(s["mixed1"], H * (b + 1))
                after(pe, "x_stored", b)
                for j in range(IC):
                    mm = nc.tensor.matmul(PX[:, 0:L], wo[:, j, :], oT[i][:, j, :], start=(j == 0), stop=(j == IC - 1))
                mm.then_inc(s["proj_done"], 1)

            def turn(b):
                pe.wait_ge(s["proj_copied"], b + 1)
                for t in range(NT):
                    mm = nc.tensor.transpose(PX[:, t * P:(t + 1) * P], fo[:, t * P:(t + 1) * P], ident[:, :])
                mm.then_inc(s["proj_turned"], 1)

            def back(b):
                pe.wait_ge(s["applied"], b + 1)
                for t in range(NT):
                    mm = nc.tensor.transpose(PX[:, t * P:(t + 1) * P], ln[:, t, :], ident[:, :])
                mm.then_inc(s["x_turned"], 1)

            def prologue():
                q_or_k(0, 0, 0)
                q_or_k(0, 0, 1)
                v_proj(0, 0)
                scores(0, 0, 0)

            def unit(b, i, has_next, has_prev):
                for g in range(H):
                    c = H * b + g
                    if g + 1 < H:
                        scores(b, i, g + 1)
                    elif has_next:
                        scores(b + 1, 1 - i, 0)
                    turn_probs(c, g)
                    if g > 0:
                        out(b, i, g - 1)
                    elif has_prev:
                        out(b - 1, 1 - i, H - 1)
                    if has_prev and g == 1:
                        project(b - 1, 1 - i)
                    if has_prev and g == 2:
                        turn(b - 1)
                    if has_prev and g == 4:
                        back(b - 1)
                    if has_next and g == 2:
                        q_or_k(b + 1, 1 - i, 0)
                    if has_next and g == 3:
                        q_or_k(b + 1, 1 - i, 1)
                    if has_next and g == 4:
                        v_proj(b + 1, 1 - i)

            def epilogue():
                out(B - 1, 1, H - 1)
                project(B - 1, 1)
                turn(B - 1)
                back(B - 1)

            drive(pe, prologue, unit, epilogue)

        @block.scalar
        def _(act):
            act.wait_ge(s["loaded"], LOADED)

            def q_or_k(b, i, which):
                if which == 0:
                    act.wait_ge(s["q_done"], b + 1)
                    after(act, "qg_ready", H * (b - 1))
                else:
                    act.wait_ge(s["k_done"], b + 1)
                    after(act, "k_split", b)
                dst = (qT[i], kT)[which]
                for c in range(IC):
                    ins = nc.scalar.activation(dst[:, c, :], PQ[:, c // 2, c % 2 * L:(c % 2 + 1) * L], ACT.Identity,
                                               bias=bqk[:, which, c:c + 1])
                ins.then_inc(s["q_ready" if which == 0 else "k_ready"], 1)

            def exps(c, g):
                act.wait_ge(s["max_ready"], c + 1)
                after(act, "turned", c - 1)
                after(act, "norm_done", c - 1)
                for t in range(NT):
                    ins = nc.scalar.activation(ex[g % 2][:, t, :], PS[g % 2][:, t, :], ACT.Exp,
                                               bias=nm[g % 2][:, t:t + 1], accum_out=sm[g % 2][:, t:t + 1])
                ins.then_inc(s["exp_done"], 1)

            def mix_q(b, i, g):
                c = H * b + g
                if g == 0:
                    act.wait_ge(s["q_ready"], b + 1)
                after(act, "scores_done", c - 1)
                for j in range(IC):
                    ins = nc.scalar.activation(qh[g % 2][:, j, :], qT[i][:, j, :], ACT.Copy, scale=th1[:, j, g:g + 1])
                ins.then_inc(s["qh_ready"], 1)

            def copy_probs(c, g):
                act.wait_ge(s["turned"], c + 1)
                after(act, "out1_done", c - 1)
                nc.scalar.activation(ah[g % 2][:, :, :], PA[:, :, :], ACT.Copy).then_inc(s["ah_ready"], 1)

            def copy_proj(b):
                act.wait_ge(s["proj_done"], b + 1)
                after(act, "proj_turned", b)
                nc.scalar.activation(fo[:, :], PX[:, 0:L], ACT.Identity, bias=bo[:, 0:1]
                                     ).then_inc(s["proj_copied"], 1)

            def store(b):
                act.wait_ge(s["x_turned"], b + 1)
                apart(act)
                nc.scalar.activation(XT[:, bass.ds(b * L, L)], PX[:, 0:L], ACT.Copy).then_inc(s["x_stored"], 1)

            def prologue():
                q_or_k(0, 0, 0)
                q_or_k(0, 0, 1)
                act.wait_ge(s["scaled"], 1)
                mix_q(0, 0, 0)
                mix_q(0, 0, 1)
                exps(0, 0)

            def unit(b, i, has_next, has_prev):
                for g in range(H):
                    c = H * b + g
                    if g + 2 < H:
                        mix_q(b, i, g + 2)
                    elif has_next:
                        mix_q(b + 1, 1 - i, g + 2 - H)
                    copy_probs(c, g)
                    if g + 1 < H or has_next:
                        exps(c + 1, (g + 1) % H)
                    if has_prev and g == 1:
                        copy_proj(b - 1)
                    if has_prev and g == 4:
                        store(b - 1)
                    if has_next and g == 2:
                        q_or_k(b + 1, 1 - i, 0)
                    if has_next and g == 3:
                        q_or_k(b + 1, 1 - i, 1)

            def epilogue():
                copy_proj(B - 1)
                store(B - 1)

            drive(act, prologue, unit, epilogue)

        @block.vector
        def _(dve):
            dve.wait_ge(s["loaded"], LOADED)

            def v_copy(b, i):
                dve.wait_ge(s["v_done"], b + 1)
                after(dve, "v_split", b)
                nc.vector.tensor_tensor(v[:, :, :], PQ[:, :, :], bv[:, :].unsqueeze(1).to_broadcast([P, NT, INNER]),
                                        ALU.add).then_inc(s["v_ready"], 1)

            def mix_q(b, i, g):
                c = H * b + g
                dve.wait_ge(s["qh_ready"], c + 1)
                for j in range(IC):
                    ins = nc.vector.scalar_tensor_tensor(out=ql[g % 2][:, j, :], in0=qT[i][:, j, :],
                                                         scalar=th1[:, j, g:g + 1], in1=qh[g % 2][:, j, :],
                                                         op0=ALU.mult, op1=ALU.subtract)
                ins.then_inc(s["qg_ready"], 1)

            def low_probs(c, g):
                dve.wait_ge(s["ah_ready"], c + 1)
                nc.vector.tensor_tensor(al[g % 2][:, :, :], PA[:, :, :], ah[g % 2][:, :, :], ALU.subtract
                                        ).then_inc(s["at_ready"], 1)

            def mix_out(b, i, g):
                c = H * b + g
                if g == 0:
                    after(dve, "proj_done", b - 1)
                for half in range(2):
                    dve.wait_ge(s[f"out{half}_done"], c + 1)
                    if g > 0:
                        dve.wait_ge(s[f"mixed{half}"], c)
                        apart(dve)
                    for j in (2 * half, 2 * half + 1):
                        o, x, w = oT[i][:, j, :], PO[half][:, j % 2, :], th2[:, j, g:g + 1]
                        if g == 0:
                            ins = nc.vector.tensor_scalar(o, x, w, None, ALU.mult)
                        else:
                            ins = nc.vector.scalar_tensor_tensor(out=o, in0=x, scalar=w, in1=o, op0=ALU.mult,
                                                                 op1=ALU.add)
                    ins.then_inc(s[f"mixed{half}"], 1)

            def maxima(c, g):
                dve.wait_ge(s["scores_done"], c + 1)
                after(dve, "exp_done", c - 1)
                nc.vector.tensor_reduce(nm[g % 2][:, :], PS[g % 2][:, :, :], AX_X, ALU.max, negate=True
                                        ).then_inc(s["max_ready"], 1)

            def norms(c, g):
                dve.wait_ge(s["exp_done"], c + 1)
                nc.vector.reciprocal(ri[g % 2][:, :], sm[g % 2][:, :]).then_inc(s["recip_ready"], 1)
                dve.wait_ge(s["recip_ready"], c + 1)
                for t in range(NT):
                    e = ex[g % 2][:, t, :]
                    ins = nc.vector.tensor_scalar(e, e, ri[g % 2][:, t:t + 1], None, ALU.mult)
                ins.then_inc(s["norm_done"], 1)

            def subs(b):
                return R[:, bass.ds(b * NT, NT), :]

            def resid(b):
                dve.wait_ge(s["proj_turned"], b + 1)
                nc.vector.tensor_tensor(subs(b), subs(b), PX[:, 0:L].rearrange("p (j c) -> p j c", j=NT), ALU.add
                                        ).then_inc(s["resid_done"], 1)

            def stats(b):
                dve.wait_ge(s["resid_done"], b + 1)
                bn_norm(dve, nc, subs(b), st, mv, s["bn_done"], s["moments_ready"], s["rstd_ready"], b)

            def apply(b):
                after(dve, "x_turned", b)
                bn_apply(dve, nc, ln, subs(b), mv, rs, s["rstd_ready"], s["applied"], b)

            def prologue():
                nc.vector.tensor_scalar(th1[:, :, :], th1[:, :, :], SCALE, None, ALU.mult).then_inc(s["scaled"], 1)
                dve.wait_ge(s["scaled"], 1)
                mix_q(0, 0, 0)
                mix_q(0, 0, 1)
                v_copy(0, 0)
                maxima(0, 0)
                norms(0, 0)

            def unit(b, i, has_next, has_prev):
                for g in range(H):
                    c = H * b + g
                    if g + 2 < H:
                        mix_q(b, i, g + 2)
                    elif has_next:
                        mix_q(b + 1, 1 - i, g + 2 - H)
                    if g + 1 < H or has_next:
                        maxima(c + 1, (g + 1) % H)
                    low_probs(c, g)
                    if g + 1 < H or has_next:
                        norms(c + 1, (g + 1) % H)
                    if g > 0:
                        mix_out(b, i, g - 1)
                    elif has_prev:
                        mix_out(b - 1, 1 - i, H - 1)
                    if has_prev and g == 2:
                        resid(b - 1)
                        stats(b - 1)
                    if has_prev and g == 3:
                        apply(b - 1)
                    if has_next and g == 4:
                        v_copy(b + 1, 1 - i)

            def epilogue():
                mix_out(B - 1, 1, H - 1)
                resid(B - 1)
                stats(B - 1)
                apply(B - 1)

            drive(dve, prologue, unit, epilogue)


def experts_stage(nc, a, R, XT, ident, out):
    E, INTER, TOP, SHARED = 64, 64, 6, 256
    PAIRS = E * INTER // P
    SC = SHARED // P
    CH = PAIRS + SC
    PIECES = 8
    PIECE = CH * P // PIECES
    FULL, GONE = 3.0e38, -3.0e38
    with ExitStack() as ctx:
        m = Mem(nc, ctx)
        wg = m.sb("x_wg", [P, E])
        w1h = m.sb("x_w1h", [P, CH * P], F32R)
        w3h = m.sb("x_w3h", [P, CH * P], F32R)
        w1l = m.sb("x_w1l", [P, CH * P], F32R)
        w3l = m.sb("x_w3l", [P, CH * P], F32R)
        w2h = m.sb("x_w2h", [P, CH * P], F32R)
        w2l = m.sb("x_w2l", [P, CH * P], F32R)
        eye2 = m.sb("eye2", [P, E])
        raw = [m.sb(f"x_raw{i}", [P, PIECE]) for i in range(3)]
        pick = m.sb("x_pick", [P, E, INTER], F32R)
        xb = [m.sb(f"x_xb{i}", [P, TOK]) for i in range(2)]
        xh = [m.sb(f"x_xh{i}", [P, TOK], F32R) for i in range(2)]
        xl = [m.sb(f"x_xl{i}", [P, TOK], F32R) for i in range(2)]
        sc = m.sb("x_sc", [P, SUB, E + 2])
        mr = m.sb("x_mr", [P, SUB, E + 2])
        top = m.sb("x_top", [P, SUB, 8])
        nmx = m.sb("x_nmx", [P, SUB])
        mask = m.sb("x_mask", [P, SUB, E])
        ex = m.sb("x_ex", [P, SUB, E])
        sm = m.sb("x_sm", [P, SUB])
        ri = m.sb("x_ri", [P, SUB])
        cf = m.sb("x_cf", [E, TOK])
        parts = [m.sb(f"x_parts{i}", [P, TOK], F32R) for i in range(2)]
        s1 = [m.sb(f"x_s1{i}", [P, TOK]) for i in range(2)]
        hx = [m.sb(f"x_hx{i}", [P, TOK]) for i in range(2)]
        hf = [m.sb(f"x_hf{i}", [P, TOK]) for i in range(2)]
        hh = [m.sb(f"x_hh{i}", [P, TOK], F32R) for i in range(2)]
        hl = [m.sb(f"x_hl{i}", [P, TOK], F32R) for i in range(2)]
        ro = m.sb("x_ro", [P, TOK])
        P1 = [m.ps(f"xP1{i}", [P, TOK]) for i in range(2)]
        P3 = [m.ps(f"xP3{i}", [P, TOK]) for i in range(2)]
        PW = [m.ps(f"xPW{i}", [P, TOK]) for i in range(2)]
        PO = m.ps("xPO", [P, TOK])
        PX = m.ps("xPX", [P, TOK])

        names = ("gate_loaded up1_loaded up3_loaded down_loaded hidden_high hidden_split consts pick_ready x_copied x_high x_split w_high w_split scores_done gate_chain top_ready "
                 "mask_ready exp_done comb_ready comb_turned comb_copied parts_ready gate_half_done up_half_done up_done silu_done product_done "
                 "hidden_ready down_done sum_copied sum_turned final_ready stored").split()
        s = {n: m.sem("x_" + n) for n in names}
        block = ctx.enter_context(nc.Block())

        def after(eng, name, n):
            if not isinstance(n, int) or n > 0:
                eng.wait_ge(s[name], n)

        def drive(eng, prologue, unit, epilogue):
            prologue()
            unit(0, 0, True, False)
            unit(1, 1, True, True)
            with eng.Fori(1, TILES // 2 - 1) as q:
                for i in range(2):
                    unit(2 * q + i, i, True, True)
            unit(TILES - 2, 0, True, True)
            unit(TILES - 1, 1, False, True)
            epilogue()

        @block.sync
        def _(sp):
            sp.dma_start(wg[:, :], a["x_wg"]).then_inc(s["gate_loaded"], 16)
            sp.dma_start(eye2[:, :], a["eye2"]).then_inc(s["gate_loaded"], 16)
            for k in range(PIECES):
                for n in range(3):
                    if k > 0:
                        sp.wait_ge(s["w_split"], 3 * (k - 1) + n + 1)
                    sp.dma_start(raw[n][:, :], a[("x_w1", "x_w3", "x_w2")[n]][:, k * PIECE:(k + 1) * PIECE]
                                 ).then_inc(s[("up1_loaded", "up3_loaded", "down_loaded")[n]], 16)

            with sp.Fori(0, TILES) as T:
                sp.wait_ge(s["final_ready"], T + 1)
                sp.dma_start(out[:, bass.ds(T * SUB, SUB), :], R[:, bass.ds(T * SUB, SUB), :]).then_inc(s["stored"], 16)
            sp.wait_ge(s["stored"], 16 * TILES)

        @block.gpsimd
        def _(pool):
            nc.gpsimd.memset(sc[:, :, E:E + 2], FULL).then_inc(s["consts"], 1)

            def x_copy(T, i):
                after(pool, "up_done", CH * (T - 1))
                apart(pool)
                nc.gpsimd.tensor_copy(xb[i][:, :], XT[:, bass.ds(T * TOK, TOK)]).then_inc(s["x_copied"], 1)

            def x_low(T, i):
                pool.wait_ge(s["x_high"], T + 1)
                nc.gpsimd.tensor_tensor(xl[i][:, :], xb[i][:, :], xh[i][:, :], ALU.subtract).then_inc(s["x_split"], 1)

            def hidden_low(T, c):
                g = CH * T + c
                pool.wait_ge(s["hidden_high"], g + 1)
                nc.gpsimd.tensor_tensor(hl[c % 2][:, :], hf[c % 2][:, :], hh[c % 2][:, :], ALU.subtract
                                        ).then_inc(s["hidden_split"], 1)

            def prologue():
                x_copy(0, 0)
                x_low(0, 0)

            def unit(T, i, has_next, has_prev):
                for c in range(CH):
                    hidden_low(T, c)
                    if has_next and c == 2:
                        x_copy(T + 1, 1 - i)
                    if has_next and c == 9:
                        x_low(T + 1, 1 - i)

            drive(pool, prologue, unit, lambda: None)

        @block.tensor
        def _(pe):
            pe.wait_ge(s["gate_loaded"], 32)

            def gate_scores(T, i):
                pe.wait_ge(s["x_copied"], T + 1)
                after(pe, "final_ready", T - 1)
                for j in range(SUB):
                    mm = nc.tensor.matmul(PX[:, j * E:(j + 1) * E], xb[i][:, j * P:(j + 1) * P], wg[:, :],
                                          start=True, stop=True)
                mm.then_inc(s["scores_done"], 1)

            def gate_turn(T):
                pe.wait_ge(s["comb_ready"], T + 1)
                apart(pe)
                for j in range(SUB):
                    mm = nc.tensor.transpose(PX[0:E, j * P:(j + 1) * P], ex[:, j, :], ident[:, :])
                mm.then_inc(s["comb_turned"], 1)

            def up(T, i, c):
                g = CH * T + c
                last = c - 2 if c >= 2 else CH - 2 + c
                cols = slice(c * P, (c + 1) * P)
                if isinstance(T, int) and T == 0:
                    pe.wait_ge(s["w_split"], 3 * (((c + 1) * P - 1) // PIECE + 1))
                if c == 0:
                    pe.wait_ge(s["x_split"], T + 1)
                    pe.wait_ge(s["parts_ready"], T + 1)
                after(pe, "silu_done", g - 1)
                apart(pe)
                nc.tensor.matmul(P1[c % 2][:, :], w1h[:, cols], xh[i][:, :], start=True, stop=False)
                nc.tensor.matmul(P1[c % 2][:, :], w1l[:, cols], xh[i][:, :], start=False, stop=False)
                nc.tensor.matmul(P1[c % 2][:, :], w1h[:, cols], xl[i][:, :], start=False, stop=True
                                 ).then_inc(s["gate_half_done"], 1)
                if last >= PAIRS:
                    after(pe, "hidden_ready", g - 1)
                else:
                    after(pe, "product_done", (T if c >= 2 else T - 1) * PAIRS + last + 1)
                apart(pe)
                nc.tensor.matmul(P3[c % 2][:, :], w3h[:, cols], xh[i][:, :], start=True, stop=False)
                nc.tensor.matmul(P3[c % 2][:, :], w3l[:, cols], xh[i][:, :], start=False, stop=False)
                mm = nc.tensor.matmul(P3[c % 2][:, :], w3h[:, cols], xl[i][:, :], start=False, stop=True)
                if c < PAIRS:
                    mm.then_inc(s["up_half_done"], 1)
                    pk = pick[:, 2 * c:2 * c + 2, :].rearrange("p e i -> p (e i)")
                    after(pe, "hidden_ready", g - 1)
                    apart(pe)
                    mm = nc.tensor.matmul(PW[c % 2][:, :], pk, parts[i][:, :], start=True, stop=True)
                mm.then_inc(s["up_done"], 1)

            def down(T, c):
                g = CH * T + c
                cols = slice(c * P, (c + 1) * P)
                pe.wait_ge(s["hidden_split"], g + 1)
                if c == 0:
                    after(pe, "sum_copied", T)
                apart(pe)
                nc.tensor.matmul(PO[:, :], w2h[:, cols], hh[c % 2][:, :], start=(c == 0), stop=False)
                nc.tensor.matmul(PO[:, :], w2l[:, cols], hh[c % 2][:, :], start=False, stop=False)
                nc.tensor.matmul(PO[:, :], w2h[:, cols], hl[c % 2][:, :], start=False, stop=(c == CH - 1)
                                 ).then_inc(s["down_done"], 1)

            def turn(T):
                pe.wait_ge(s["sum_copied"], T + 1)
                for j in range(SUB):
                    mm = nc.tensor.transpose(PX[:, j * P:(j + 1) * P], ro[:, j * P:(j + 1) * P], ident[:, :])
                mm.then_inc(s["sum_turned"], 1)

            def prologue():
                gate_scores(0, 0)
                gate_turn(0)
                pe.wait_ge(s["pick_ready"], 1)
                up(0, 0, 0)
                up(0, 0, 1)

            def unit(T, i, has_next, has_prev):
                for c in range(CH):
                    if c + 2 < CH:
                        up(T, i, c + 2)
                    elif has_next:
                        up(T + 1, 1 - i, c + 2 - CH)
                    down(T, c)
                    if has_prev and c == 1:
                        turn(T - 1)
                    if has_next and c == 8:
                        gate_scores(T + 1, 1 - i)
                    if has_next and c == 18:
                        gate_turn(T + 1)

            drive(pe, prologue, unit, lambda: turn(TILES - 1))

        @block.scalar
        def _(act):
            act.wait_ge(s["gate_loaded"], 32)
            nc.scalar.activation(pick[:, :, :], eye2[:, :].unsqueeze(2).to_broadcast([P, E, INTER]), ACT.Copy
                                 ).then_inc(s["pick_ready"], 1)

            def gate_exp(T):
                act.wait_ge(s["top_ready"], T + 1)
                after(act, "comb_turned", T)
                for j in range(SUB):
                    ins = nc.scalar.activation(ex[:, j, :], sc[:, j, 0:E], ACT.Exp, bias=nmx[:, j:j + 1])
                ins.then_inc(s["exp_done"], 1)

            def gate_copy(T, i):
                act.wait_ge(s["comb_turned"], T + 1)
                after(act, "parts_ready", T)
                nc.scalar.activation(cf[:, :], PX[0:E, :], ACT.Copy).then_inc(s["comb_copied"], 1)

            def silu(T, c):
                g = CH * T + c
                act.wait_ge(s["gate_half_done"], g + 1)
                after(act, "hidden_ready", g - 1)
                nc.scalar.activation(s1[c % 2][:, :], P1[c % 2][:, :], ACT.Silu).then_inc(s["silu_done"], 1)

            def hidden_high(T, c):
                g = CH * T + c
                act.wait_ge(s["hidden_ready"], g + 1)
                after(act, "down_done", g - 1)
                apart(act)
                nc.scalar.activation(hh[c % 2][:, :], hf[c % 2][:, :], ACT.Copy).then_inc(s["hidden_high"], 1)

            def copy_sum(T):
                act.wait_ge(s["down_done"], CH * (T + 1))
                after(act, "sum_turned", T)
                nc.scalar.activation(ro[:, :], PO[:, :], ACT.Copy).then_inc(s["sum_copied"], 1)

            def prologue():
                gate_exp(0)
                gate_copy(0, 0)
                silu(0, 0)

            def unit(T, i, has_next, has_prev):
                if has_prev:
                    copy_sum(T - 1)
                for c in range(CH):
                    if c + 1 < CH:
                        silu(T, c + 1)
                    elif has_next:
                        silu(T + 1, 0)
                    hidden_high(T, c)
                    if has_next and c == 14:
                        gate_exp(T + 1)
                    if has_next and c == 19:
                        gate_copy(T + 1, 1 - i)

            drive(act, prologue, unit, lambda: copy_sum(TILES - 1))

        @block.vector
        def _(dve):
            dve.wait_ge(s["consts"], 1)
            LINKS = 7

            def gate_top(T):
                dve.wait_ge(s["scores_done"], T + 1)
                after(dve, "exp_done", T)
                nc.vector.tensor_copy(sc[:, :, 0:E], PX[:, 0:SUB * E].rearrange("p (j e) -> p j e", j=SUB)
                                      ).then_inc(s["gate_chain"], 1)
                dve.wait_ge(s["gate_chain"], LINKS * T + 1)
                apart(dve)
                for j in range(SUB):
                    ins = nc.vector.max(top[:, j, :], sc[:, j, 0:E])
                ins.then_inc(s["gate_chain"], 1)

            def gate_mask(T):
                dve.wait_ge(s["gate_chain"], LINKS * T + 2)
                apart(dve)
                nc.vector.tensor_scalar(nmx[:, :], top[:, :, 0], -1.0, None, ALU.mult).then_inc(s["top_ready"], 1)
                nc.vector.memset(top[:, :, TOP:8], FULL).then_inc(s["gate_chain"], 1)
                dve.wait_ge(s["gate_chain"], LINKS * T + 3)
                apart(dve)
                for j in range(SUB):
                    ins = nc.vector.match_replace(mr[:, j, :], top[:, j, :], sc[:, j, :], GONE)
                ins.then_inc(s["gate_chain"], 1)
                dve.wait_ge(s["gate_chain"], LINKS * T + 4)
                nc.vector.tensor_scalar(mask[:, :, :], mr[:, :, 0:E], GONE, None, ALU.is_equal
                                        ).then_inc(s["mask_ready"], 1)

            def gate_weights(T):
                dve.wait_ge(s["mask_ready"], T + 1)
                dve.wait_ge(s["exp_done"], T + 1)
                for j in range(SUB):
                    ins = nc.vector.scalar_tensor_tensor(out=mask[:, j, :], in0=ex[:, j, :], scalar=1.0,
                                                         in1=mask[:, j, :], op0=ALU.mult, op1=ALU.mult,
                                                         accum_out=sm[:, j:j + 1])
                ins.then_inc(s["gate_chain"], 1)
                dve.wait_ge(s["gate_chain"], LINKS * T + 5)
                nc.vector.reciprocal(ri[:, :], sm[:, :]).then_inc(s["gate_chain"], 1)
                dve.wait_ge(s["gate_chain"], LINKS * T + 6)
                for j in range(SUB):
                    ins = nc.vector.tensor_scalar(ex[:, j, :], mask[:, j, :], ri[:, j:j + 1], None, ALU.mult)
                ins.then_inc(s["comb_ready"], 1)

            def gate_split(T, i):
                dve.wait_ge(s["comb_copied"], T + 1)
                after(dve, "up_done", CH * (T - 1))
                nc.vector.tensor_copy(parts[i][0:E, :], cf[:, :]).then_inc(s["gate_chain"], 1)
                dve.wait_ge(s["gate_chain"], LINKS * T + 7)
                nc.vector.tensor_tensor(parts[i][E:2 * E, :], cf[:, :], parts[i][0:E, :], ALU.subtract
                                        ).then_inc(s["parts_ready"], 1)

            def x_high(T, i):
                dve.wait_ge(s["x_copied"], T + 1)
                nc.vector.tensor_copy(xh[i][:, :], xb[i][:, :]).then_inc(s["x_high"], 1)

            def split_piece(k):
                piece = slice(k * PIECE, (k + 1) * PIECE)
                for n, (name, wh, wl) in enumerate((("up1_loaded", w1h, w1l), ("up3_loaded", w3h, w3l),
                                                    ("down_loaded", w2h, w2l))):
                    dve.wait_ge(s[name], 16 * (k + 1))
                    nc.vector.tensor_copy(wh[:, piece], raw[n][:, :]).then_inc(s["w_high"], 1)
                    dve.wait_ge(s["w_high"], 3 * k + n + 1)
                    nc.vector.tensor_tensor(wl[:, piece], raw[n][:, :], wh[:, piece], ALU.subtract
                                            ).then_inc(s["w_split"], 1)

            def product(T, c):
                g = CH * T + c
                if c < PAIRS:
                    dve.wait_ge(s["up_half_done"], PAIRS * T + c + 1)
                else:
                    dve.wait_ge(s["up_done"], g + 1)
                dve.wait_ge(s["silu_done"], g + 1)
                if c >= PAIRS:
                    after(dve, "hidden_split", g - 1)
                dst = hx if c < PAIRS else hf
                nc.vector.tensor_tensor(dst[c % 2][:, :], s1[c % 2][:, :], P3[c % 2][:, :], ALU.mult
                                        ).then_inc(s["product_done" if c < PAIRS else "hidden_ready"], 1)

            def weigh(T, c):
                g = CH * T + c
                dve.wait_ge(s["product_done"], PAIRS * T + c + 1)
                dve.wait_ge(s["up_done"], g + 1)
                after(dve, "hidden_split", g - 1)
                nc.vector.tensor_tensor(hf[c % 2][:, :], hx[c % 2][:, :], PW[c % 2][:, :], ALU.mult
                                        ).then_inc(s["hidden_ready"], 1)

            def final(T):
                dve.wait_ge(s["sum_turned"], T + 1)
                r = R[:, bass.ds(T * SUB, SUB), :]
                nc.vector.tensor_tensor(r, r, PX[:, :].rearrange("p (j c) -> p j c", j=SUB), ALU.add
                                        ).then_inc(s["final_ready"], 1)

            def prologue():
                x_high(0, 0)
                gate_top(0)
                gate_mask(0)
                gate_weights(0)
                gate_split(0, 0)
                split_piece(0)
                split_piece(1)

            def unit(T, i, has_next, has_prev):
                for c in range(CH):
                    product(T, c)
                    if c < PAIRS:
                        weigh(T, c)
                    if isinstance(T, int) and T == 0 and c % 4 == 1 and c // 4 + 2 < PIECES:
                        split_piece(c // 4 + 2)
                    if has_prev and c == 3:
                        final(T - 1)
                    if has_next and c == 5:
                        x_high(T + 1, 1 - i)
                    if has_next and c == 10:
                        gate_top(T + 1)
                    if has_next and c == 12:
                        gate_mask(T + 1)
                    if has_next and c == 16:
                        gate_weights(T + 1)
                    if has_next and c == 21:
                        gate_split(T + 1, 1 - i)

            drive(dve, prologue, unit, lambda: final(TILES - 1))


def audio_tower(nc, a, out):
    with ExitStack() as ctx:
        m = Mem(nc, ctx)
        R = m.sb("R", [P, N // P, P])
        XT = m.sb("XT", [P, N])
        ident = m.sb("ident", [P, P])
        tok_stage(nc, a, R, XT, ident)
        mixer_stage(nc, a, R, XT, ident)
        w_dram = nc.dram_tensor("token_weights", (8, N), F32, kind="Internal").ap()
        expert_choice_stage(nc, a, R, XT, ident, w_dram)
        attention_stage(nc, a, R, XT, ident)
        experts_stage(nc, a, R, XT, ident, out)


def lay_out(i):
    import numpy as np
    t = "L0_tok_"
    d = {}
    d["x"] = i["x"]
    d["ident"] = np.eye(P, dtype=np.float32)
    d["ew"] = i[t + "embed_w"].transpose(1, 2, 0)
    d["tok_cols"] = np.stack([i[t + "embed_b"], i[t + "norm0_g"], i[t + "norm0_b"]], 1)
    d["dww"] = i[t + "dw_w"][:, :, 0, :].transpose(2, 0, 1)
    d["lcol"] = np.stack([i[t + k].T for k in ("dw_b", "ln_g", "ln_b", "b2", "gamma")], 1)
    d["tok_b1"] = i[t + "b1"].reshape(8, 3, P).transpose(2, 0, 1)
    d["tok_w1"] = i[t + "w1"].transpose(0, 2, 1)
    d["tok_w2"] = i[t + "w2"].transpose(0, 2, 1).reshape(8, 3, P, P).transpose(0, 2, 1, 3)
    d["fing"] = np.stack([i[t + "final_g"], i[t + "final_b"]])
    def both(name, f):
        return np.stack([f(i["L0_attn_f_" + name]), f(i["L0_attn_b_" + name])], 1)
    halves = lambda v: v.reshape(2, P, -1).transpose(1, 0, 2)
    d["inw"] = both("in_w", lambda w: w.T)
    d["mcol"] = np.concatenate([both(k, halves) for k in ("conv_b", "dt_b", "D")], 3)
    d["m_cw"] = np.stack([i[f"L0_attn_{k}_conv_w"][:, 0, :].reshape(2, P, 4).transpose(0, 2, 1) for k in "fb"])
    d["alog"] = both("A_log", halves)
    d["xpw"] = both("xproj_w", lambda w: halves(np.concatenate([w[8:40], w[0:8]]).T))
    d["dtw"] = both("dt_w", lambda w: w.T)
    d["outw"] = both("out_w", lambda w: w)
    d["fusw"] = i["L0_attn_fusion_w"].reshape(P, 2, P).transpose(2, 1, 0)
    d["fusb"] = i["L0_attn_fusion_b"].reshape(P, 1)
    d["mix_gb"] = np.stack([i["L0_attn_ln_g"], i["L0_attn_ln_b"]])
    d["eye3"] = np.tile(np.eye(32, dtype=np.float32), (3, 1))
    d["wr"] = i["L0_ffn_Wr"]
    d["e_w1"] = i["L0_ffn_W1"].transpose(1, 0, 2)
    d["e_b1"] = i["L0_ffn_b1"].reshape(8, 4, P).transpose(2, 0, 1)
    d["e_w2"] = i["L0_ffn_W2"].reshape(8, 4, P, P).transpose(2, 0, 1, 3)
    d["e_b2"] = i["L0_ffn_b2"].T
    expert, sample = np.arange(P) // B, np.arange(P) % B
    same = expert[:, None] == expert[None, :]
    d["same"] = same.astype(np.float32)
    d["before"] = (same & (sample[:, None] < sample[None, :])).astype(np.float32)
    d["bit"] = (1 << np.arange(29, -1, -1)).astype(np.int32)
    d["wqkv"] = i["L1_attn_w_qkv"]
    bq = i["L1_attn_b_qkv"].reshape(3, 4, P)
    d["bqk"] = bq[0:2].transpose(2, 0, 1)
    d["bv"] = bq[2].reshape(512)
    d["th1"] = np.repeat(i["L1_attn_th1"], 64, 1).reshape(8, 4, P).transpose(2, 1, 0)
    d["th2"] = np.repeat(i["L1_attn_th2"].T, 64, 1).reshape(8, 4, P).transpose(2, 1, 0)
    d["wo"] = i["L1_attn_w_out"].reshape(4, P, P).transpose(1, 0, 2)
    d["bo"] = i["L1_attn_b_out"].reshape(P, 1)
    d["x_wg"] = i["L1_ffn_w_gate"].T
    up = lambda w, shared: np.concatenate([i[w].reshape(64 * 64, P), i[shared]]).T
    d["x_w1"] = up("L1_ffn_w1", "L1_ffn_w_sg")
    d["x_w3"] = up("L1_ffn_w3", "L1_ffn_w_su")
    d["x_w2"] = np.concatenate([i["L1_ffn_w2"].reshape(32, P, P), i["L1_ffn_w_sd"].T.reshape(2, P, P)]
                               ).transpose(1, 0, 2).reshape(P, -1)
    d["eye2"] = np.tile(np.eye(64, dtype=np.float32), (2, 1))
    return {k: np.ascontiguousarray(v) for k, v in d.items()}


def kernel(**inputs):
    import numpy as np
    import concourse.bacc as bacc
    from concourse.bass_utils import run_bass_kernel_spmd

    nc = bacc.Bacc("TRN2", target_bir_lowering=False, num_devices=1)
    laid = lay_out({k: np.asarray(v) for k, v in inputs.items()})
    arrays, aps = {}, {}
    for name, v in laid.items():
        arrays[f"in_{name}"] = v
        aps[name] = nc.dram_tensor(f"in_{name}", v.shape, mybir.dt.from_np(v.dtype), kind="ExternalInput").ap()
    out = nc.dram_tensor("out_0", (P, N // P, P), F32, kind="ExternalOutput").ap()
    audio_tower(nc, aps, out)
    r = run_bass_kernel_spmd(nc, [arrays], core_ids=[0])
    got = r.results[0]["out_0"]
    return np.ascontiguousarray(got.transpose(1, 0, 2)).reshape(B, L, P)
```
